# Optimizing a Trainium2 kernel written in Bass

```python
import numpy as np
import jax
import jax.numpy as jnp

def _softmax(x, axis=-1):
    return jax.nn.softmax(x, axis=axis)

def _gelu(x):
    return jax.nn.gelu(x, approximate=True)

def _silu(x):
    return jax.nn.silu(x)

def _sigmoid(x):
    return jax.nn.sigmoid(x)

def _layernorm(x, axis=-1, eps=1e-05):
    m = jnp.mean(x, axis=axis, keepdims=True)
    v = jnp.var(x, axis=axis, keepdims=True)
    return (x - m) / jnp.sqrt(v + eps)

def _scatter_add(tgt, idx, src, axis=0):
    return tgt.at[idx].add(src)

def _segment_sum(src, seg, n):
    return jax.ops.segment_sum(src, seg, n)
kernel_name = 'mk_seq_postln_d1_jaxref_r4_667b9b'

def setup_inputs(seed: int=0):
    np.random.seed(seed)
    _w = jnp.asarray

    def _L0_attn_setup():
        import jax, jax.numpy as jnp
        import numpy as np
        from jax.scipy.linalg import solve_triangular
        B, L, D, H = (1, 512, 256, 4)
        DK = DV = D // H
        CONV = 4
        FIR_S, FIR_M, FIR_L = (3, 15, 63)
        CHUNK = 32

        def _l2norm(x):
            return x * jax.lax.rsqrt(jnp.sum(x * x, -1, keepdims=True) + 1e-06)

        def _short_conv(x, w):
            K = w.shape[-1]
            l = x.shape[1]
            xp = jnp.pad(x, ((0, 0), (K - 1, 0), (0, 0)))
            y = sum((xp[:, j:j + l, :] * w[:, j] for j in range(K)))
            return jax.nn.silu(y)

        def _fir(x, filt):
            b, l, h, d = x.shape
            K = filt.shape[-1]
            xf = jnp.transpose(x.reshape(b, l, h * d), (0, 2, 1))
            y = jax.lax.conv_general_dilated(xf, filt.reshape(h * d, 1, K), (1,), [(K - 1, 0)], feature_group_count=h * d)
            return jnp.transpose(y, (0, 2, 1)).reshape(b, l, h, d)

        def _delta_rule_chunkwise(q, k, v, beta):
            b, h, Lq, dk = q.shape
            c = CHUNK
            n = Lq // c
            q = _l2norm(q)
            k = _l2norm(k)
            v = v * beta[..., None]
            kb = k * beta[..., None]
            rs = lambda t: t.reshape(b, h, n, c, t.shape[-1])
            qc, kc, vc, kbc = (rs(q), rs(k), rs(v), rs(kb))
            tri_strict = jnp.tril(jnp.ones((c, c), bool), -1)
            A = jnp.where(tri_strict, -(kbc @ jnp.swapaxes(kc, -1, -2)), 0.0)
            eye = jnp.eye(c, dtype=q.dtype)
            M = eye - A
            T = solve_triangular(M, jnp.broadcast_to(eye, M.shape), lower=True)
            u = T @ vc
            w = T @ kbc
            causal = jnp.tril(jnp.ones((c, c), bool))

            def step(S, inp):
                q_i, k_i, u_i, w_i = inp
                attn = jnp.where(causal, q_i @ jnp.swapaxes(k_i, -1, -2), 0.0)
                u_adj = u_i - w_i @ S
                o_i = q_i @ S + attn @ u_adj
                return (S + jnp.swapaxes(k_i, -1, -2) @ u_adj, o_i)
            S0 = jnp.zeros((b, h, dk, v.shape[-1]), q.dtype)
            mv = lambda t: jnp.moveaxis(t, 2, 0)
            _, o = jax.lax.scan(step, S0, (mv(qc), mv(kc), mv(u), mv(w)))
            return jnp.moveaxis(o, 0, 2).reshape(b, h, Lq, -1)

        def _rmsnorm(x, w, eps=1e-05):
            return x * jax.lax.rsqrt(jnp.mean(x * x, -1, keepdims=True) + eps) * w
        key = jax.random.key(seed)
        ks = jax.random.split(key, 16)
        wn = lambda k, shape, s: jax.random.normal(k, shape, jnp.float32) * s

        def fir_init(k, K):
            f = jnp.zeros((H, DV, K), jnp.float32).at[..., -1].set(1.0)
            return f + wn(k, (H, DV, K), 0.01)
        return {'hidden_states': jax.random.normal(ks[0], (B, L, D), jnp.float32), 'Wq': wn(ks[1], (D, D), 0.02), 'Wk': wn(ks[2], (D, D), 0.02), 'Wv': wn(ks[3], (D, D), 0.02), 'Wb': wn(ks[4], (H, D), 0.02), 'conv_q': wn(ks[5], (D, CONV), 0.1), 'conv_k': wn(ks[6], (D, CONV), 0.1), 'conv_v': wn(ks[7], (D, CONV), 0.1), 'fir_s': fir_init(ks[8], FIR_S), 'fir_m': fir_init(ks[9], FIR_M), 'fir_l': fir_init(ks[10], FIR_L), 'gate_w': wn(ks[11], (H, 5, D), 1.0 / np.sqrt(D)), 'gate_b': jnp.zeros((H, 5), jnp.float32), 'log_temp': jnp.zeros((H, 1), jnp.float32), 'eps_param': jnp.full((H, 1), 0.02, jnp.float32), 'norm_w': jnp.ones((DV,), jnp.float32), 'Wo': wn(ks[12], (D, D), 0.02)}
    _L0_attn_in = _L0_attn_setup()

    def _L0_ffn_setup():
        import jax, jax.numpy as jnp
        import numpy as np
        D_IN, D_HID = (256, 1024)

        def _ternary(key, shape):
            return jax.random.randint(key, shape, -1, 2).astype(jnp.float32)

        def _tlin(x, w, s):
            return jnp.einsum('bsi,oi->bso', x, w) * s
        key = jax.random.key(seed)
        ks = jax.random.split(key, 12)
        inv = lambda fan: 1.0 / np.sqrt(fan).astype(np.float32)
        return {'x': jax.random.normal(ks[0], (4, 512, D_IN), dtype=jnp.float32), 'w1_w': _ternary(ks[1], (D_HID, D_IN)), 'w1_s': jax.random.uniform(ks[2], (D_HID,), dtype=jnp.float32) * inv(D_IN), 'w2_w': _ternary(ks[3], (D_HID, D_IN)), 'w2_s': jax.random.uniform(ks[4], (D_HID,), dtype=jnp.float32) * inv(D_IN), 'h1_w': _ternary(ks[5], (D_HID, D_HID)), 'h1_s': jax.random.uniform(ks[6], (D_HID,), dtype=jnp.float32) * inv(D_HID), 'h2_w': _ternary(ks[7], (D_HID, D_HID)), 'h2_s': jax.random.uniform(ks[8], (D_HID,), dtype=jnp.float32) * inv(D_HID), 'w3_w': _ternary(ks[9], (D_IN, D_HID)), 'w3_s': jax.random.uniform(ks[10], (D_IN,), dtype=jnp.float32) * inv(D_HID)}
    _L0_ffn_in = _L0_ffn_setup()
    _d = {'L0_attn_hidden_states': _L0_attn_in['hidden_states'], 'L0_attn_Wq': _L0_attn_in['Wq'], 'L0_attn_Wk': _L0_attn_in['Wk'], 'L0_attn_Wv': _L0_attn_in['Wv'], 'L0_attn_Wb': _L0_attn_in['Wb'], 'L0_attn_conv_q': _L0_attn_in['conv_q'], 'L0_attn_conv_k': _L0_attn_in['conv_k'], 'L0_attn_conv_v': _L0_attn_in['conv_v'], 'L0_attn_fir_s': _L0_attn_in['fir_s'], 'L0_attn_fir_m': _L0_attn_in['fir_m'], 'L0_attn_fir_l': _L0_attn_in['fir_l'], 'L0_attn_gate_w': _L0_attn_in['gate_w'], 'L0_attn_gate_b': _L0_attn_in['gate_b'], 'L0_attn_log_temp': _L0_attn_in['log_temp'], 'L0_attn_eps_param': _L0_attn_in['eps_param'], 'L0_attn_norm_w': _L0_attn_in['norm_w'], 'L0_attn_Wo': _L0_attn_in['Wo'], 'L0_ffn_w1_w': _L0_ffn_in['w1_w'], 'L0_ffn_w1_s': _L0_ffn_in['w1_s'], 'L0_ffn_w2_w': _L0_ffn_in['w2_w'], 'L0_ffn_w2_s': _L0_ffn_in['w2_s'], 'L0_ffn_h1_w': _L0_ffn_in['h1_w'], 'L0_ffn_h1_s': _L0_ffn_in['h1_s'], 'L0_ffn_h2_w': _L0_ffn_in['h2_w'], 'L0_ffn_h2_s': _L0_ffn_in['h2_s'], 'L0_ffn_w3_w': _L0_ffn_in['w3_w'], 'L0_ffn_w3_s': _L0_ffn_in['w3_s']}
    _x0 = _d['L0_attn_hidden_states']
    _d['L0_attn_hidden_states'] = jax.random.normal(jax.random.fold_in(jax.random.key(seed), 1), (4, 2048, 256), dtype=_x0.dtype)
    del _x0
    return _d

def reference(L0_attn_hidden_states, L0_attn_Wq, L0_attn_Wk, L0_attn_Wv, L0_attn_Wb, L0_attn_conv_q, L0_attn_conv_k, L0_attn_conv_v, L0_attn_fir_s, L0_attn_fir_m, L0_attn_fir_l, L0_attn_gate_w, L0_attn_gate_b, L0_attn_log_temp, L0_attn_eps_param, L0_attn_norm_w, L0_attn_Wo, L0_ffn_w1_w, L0_ffn_w1_s, L0_ffn_w2_w, L0_ffn_w2_s, L0_ffn_h1_w, L0_ffn_h1_s, L0_ffn_h2_w, L0_ffn_h2_s, L0_ffn_w3_w, L0_ffn_w3_s):

    def _L0_attn_ref(hidden_states, Wq, Wk, Wv, Wb, conv_q, conv_k, conv_v, fir_s, fir_m, fir_l, gate_w, gate_b, log_temp, eps_param, norm_w, Wo):
        import jax, jax.numpy as jnp
        import numpy as np
        from jax.scipy.linalg import solve_triangular
        B, L, D, H = (1, 512, 256, 4)
        DK = DV = D // H
        CONV = 4
        FIR_S, FIR_M, FIR_L = (3, 15, 63)
        CHUNK = 32

        def _l2norm(x):
            return x * jax.lax.rsqrt(jnp.sum(x * x, -1, keepdims=True) + 1e-06)

        def _short_conv(x, w):
            K = w.shape[-1]
            l = x.shape[1]
            xp = jnp.pad(x, ((0, 0), (K - 1, 0), (0, 0)))
            y = sum((xp[:, j:j + l, :] * w[:, j] for j in range(K)))
            return jax.nn.silu(y)

        def _fir(x, filt):
            b, l, h, d = x.shape
            K = filt.shape[-1]
            xf = jnp.transpose(x.reshape(b, l, h * d), (0, 2, 1))
            y = jax.lax.conv_general_dilated(xf, filt.reshape(h * d, 1, K), (1,), [(K - 1, 0)], feature_group_count=h * d)
            return jnp.transpose(y, (0, 2, 1)).reshape(b, l, h, d)

        def _delta_rule_chunkwise(q, k, v, beta):
            b, h, Lq, dk = q.shape
            c = CHUNK
            n = Lq // c
            q = _l2norm(q)
            k = _l2norm(k)
            v = v * beta[..., None]
            kb = k * beta[..., None]
            rs = lambda t: t.reshape(b, h, n, c, t.shape[-1])
            qc, kc, vc, kbc = (rs(q), rs(k), rs(v), rs(kb))
            tri_strict = jnp.tril(jnp.ones((c, c), bool), -1)
            A = jnp.where(tri_strict, -(kbc @ jnp.swapaxes(kc, -1, -2)), 0.0)
            eye = jnp.eye(c, dtype=q.dtype)
            M = eye - A
            T = solve_triangular(M, jnp.broadcast_to(eye, M.shape), lower=True)
            u = T @ vc
            w = T @ kbc
            causal = jnp.tril(jnp.ones((c, c), bool))

            def step(S, inp):
                q_i, k_i, u_i, w_i = inp
                attn = jnp.where(causal, q_i @ jnp.swapaxes(k_i, -1, -2), 0.0)
                u_adj = u_i - w_i @ S
                o_i = q_i @ S + attn @ u_adj
                return (S + jnp.swapaxes(k_i, -1, -2) @ u_adj, o_i)
            S0 = jnp.zeros((b, h, dk, v.shape[-1]), q.dtype)
            mv = lambda t: jnp.moveaxis(t, 2, 0)
            _, o = jax.lax.scan(step, S0, (mv(qc), mv(kc), mv(u), mv(w)))
            return jnp.moveaxis(o, 0, 2).reshape(b, h, Lq, -1)

        def _rmsnorm(x, w, eps=1e-05):
            return x * jax.lax.rsqrt(jnp.mean(x * x, -1, keepdims=True) + eps) * w
        b, l, d = hidden_states.shape
        q = _short_conv(hidden_states @ Wq.T, conv_q).reshape(b, l, H, DK)
        k = _short_conv(hidden_states @ Wk.T, conv_k).reshape(b, l, H, DK)
        v_direct = _short_conv(hidden_states @ Wv.T, conv_v).reshape(b, l, H, DV)
        beta = jax.nn.sigmoid(hidden_states @ Wb.T)
        tp = lambda t: jnp.transpose(t, (0, 2, 1, 3))
        delta_out = tp(_delta_rule_chunkwise(tp(q), tp(k), tp(v_direct), jnp.transpose(beta, (0, 2, 1))))
        local_s = _fir(v_direct, fir_s)
        local_m = _fir(v_direct, fir_m)
        local_l = _fir(v_direct, fir_l)
        logits = jnp.einsum('bld,hpd->blhp', hidden_states, gate_w) + gate_b
        temp = jnp.exp(log_temp).reshape(1, 1, H, 1)
        probs = jax.nn.softmax(logits / temp, -1)
        eps = jnp.clip(eps_param, 0.0, 0.2).reshape(1, 1, H, 1)
        probs = probs * (1.0 - 5.0 * eps) + eps
        o = probs[..., 0:1] * local_s + probs[..., 1:2] * local_m + probs[..., 2:3] * local_l + probs[..., 3:4] * delta_out + probs[..., 4:5] * v_direct
        o = _rmsnorm(o, norm_w)
        return o.reshape(b, l, H * DV) @ Wo.T

    def _L0_ffn_ref(x, w1_w, w1_s, w2_w, w2_s, h1_w, h1_s, h2_w, h2_s, w3_w, w3_s):
        import jax, jax.numpy as jnp
        import numpy as np
        D_IN, D_HID = (256, 1024)

        def _ternary(key, shape):
            return jax.random.randint(key, shape, -1, 2).astype(jnp.float32)

        def _tlin(x, w, s):
            return jnp.einsum('bsi,oi->bso', x, w) * s
        h = jax.nn.silu(_tlin(x, w1_w, w1_s)) * _tlin(x, w2_w, w2_s)
        h = jax.nn.gelu(_tlin(h, h1_w, h1_s), approximate=False)
        h = jax.nn.gelu(_tlin(h, h2_w, h2_s), approximate=False)
        return _tlin(h, w3_w, w3_s)
    x = L0_attn_hidden_states
    x = _layernorm(x + _L0_attn_ref(x, L0_attn_Wq, L0_attn_Wk, L0_attn_Wv, L0_attn_Wb, L0_attn_conv_q, L0_attn_conv_k, L0_attn_conv_v, L0_attn_fir_s, L0_attn_fir_m, L0_attn_fir_l, L0_attn_gate_w, L0_attn_gate_b, L0_attn_log_temp, L0_attn_eps_param, L0_attn_norm_w, L0_attn_Wo), axis=-1)
    x = _layernorm(x + _L0_ffn_ref(x, L0_ffn_w1_w, L0_ffn_w1_s, L0_ffn_w2_w, L0_ffn_w2_s, L0_ffn_h1_w, L0_ffn_h1_s, L0_ffn_h2_w, L0_ffn_h2_s, L0_ffn_w3_w, L0_ffn_w3_s), axis=-1)
    return x

_drawn_inputs = setup_inputs


def setup_inputs(seed=0):
    import zlib

    import numpy as np

    out = dict(_drawn_inputs(seed))
    spreads = {'L0_attn_gate_b': (0.0, 0.721),
     'L0_attn_log_temp': (0.0, 0.8),
     'L0_attn_eps_param': (0.019999999552965164, 0.6),
     'L0_attn_norm_w': (1.0, 0.2)}
    factors = {'L0_attn_Wb': 4.478,
     'L0_ffn_w1_w': 8.0,
     'L0_ffn_w1_s': 8.0,
     'L0_ffn_w2_w': 8.0,
     'L0_ffn_w2_s': 8.0,
     'L0_ffn_h1_w': 8.0,
     'L0_ffn_h1_s': 8.0,
     'L0_ffn_h2_w': 8.0,
     'L0_ffn_h2_s': 8.0,
     'L0_ffn_w3_w': 8.0,
     'L0_ffn_w3_s': 8.0}
    for name, (base, spread) in spreads.items():
        noise = np.random.default_rng([zlib.crc32(name.encode()), seed]).standard_normal(out[name].shape)
        drawn = base * np.exp(spread * noise) if base else spread * noise
        out[name] = jnp.asarray(drawn.astype(out[name].dtype))
    for name, factor in factors.items():
        out[name] = (out[name] * factor).astype(out[name].dtype)
    return out
```

```python
import concourse.bass as bass
from concourse import mybir
from contextlib import ExitStack

f32 = mybir.dt.float32
f32r = mybir.dt.float32r
i32 = mybir.dt.int32
ALU = mybir.AluOpType
ACT = mybir.ActivationFunctionType
AX = mybir.AxisListType

P = 128
BATCH, SEQ, D, HEADS = 4, 2048, 256, 4
DK = D // HEADS
KT = D // P
STEPS = SEQ // P
TOK = BATCH * P
CONV = 4
HALO = CONV - 1
XW = P + HALO
FIRS = (3, 15, 63)
NF = len(FIRS)
WIN = 64
FIRPAD = 3 * WIN
FCH = 8
CH = 32
NQ = P // CH
BH = BATCH * KT
NS = 2 * BH
GRP = STEPS * NS
SLOTS = GRP * NQ // P
HID = 1024
HT = HID // P
NGATE = HEADS * 5
NRAW = NGATE + HEADS + 2 * HEADS
LN_EPS = 1e-5
L2_EPS = 1e-6
C_ID, C_OFF, C_ATT, C_BD, C_DIAG, C_SEL, C_END = 0, P, 2 * P, 3 * P, 4 * P, 4 * P + CH, 4 * P + CH + 2
W1, W2, H1, H2, W3 = 0, KT * HID, 2 * KT * HID, 2 * KT * HID + HT * HID, 2 * KT * HID + 2 * HT * HID
W_END = W3 + HT * D


class Stage:

    def __init__(self, nc, sems):
        self.nc, self.ctx, self.sems = nc, ExitStack(), sems

    def sb(self, name, shape, dt=f32):
        return self.ctx.enter_context(self.nc.sbuf_tensor(name, shape, dt))

    def ps(self, name, shape):
        return self.ctx.enter_context(self.nc.psum_tensor(name, shape, f32))

    def sem(self, name):
        return self.sems.enter_context(self.nc.semaphore(name))

    def pair(self, name):
        return [self.sem(f"{name}{i}") for i in range(2)]


def row(ap, t):
    names = [f"a{i}" for i in range(len(ap.shape) - 1)]
    return ap[bass.ds(t, 1)].rearrange(f"o {names[0]} {' '.join(names[1:])} -> {names[0]} (o {names[1]}) {' '.join(names[2:])}")


def bcast(ap, n):
    return bass.AP(tensor=ap.tensor, offset=ap.offset, ap=[*ap.ap, [0, n]])


def bcast_mid(ap, n):
    return bass.AP(tensor=ap.tensor, offset=ap.offset, ap=[ap.ap[0], [0, n], *ap.ap[1:]])


def project(nc, sems, io, keep):
    st = Stage(nc, sems)
    with st.ctx:
        w_qkv = st.sb("w_qkv", [P, KT, 3 * D])
        w_gate = st.sb("w_gate", [P, KT, NGATE + HEADS])
        taps = st.sb("taps", [P, 3 * KT, CONV])
        zero = st.sb("zero", [WIN, BATCH, D])
        xt = [st.sb(f"xt{i}", [P, KT, BATCH, XW]) for i in range(2)]
        acc = [st.sb(f"acc{i}", [P, BATCH, P]) for i in range(3)]
        yT = [st.sb(f"yT{i}", [P, 3 * KT, TOK]) for i in range(2)]
        sq = st.sb("sq", [P, 2 * KT, TOK])
        ktok = [st.sb(f"ktok{i}", [P, BATCH, D]) for i in range(2)]
        vtok = [st.sb(f"vtok{i}", [P, BATCH, D]) for i in range(2)]
        yrev = [st.sb(f"yrev{i}", [P, KT, BATCH, P]) for i in range(2)]
        vrev = [st.sb(f"vrev{i}", [P, BATCH, D]) for i in range(2)]
        proj = [st.ps(f"proj{i}", [P, BATCH, 2 * P]) for i in range(2)]
        side = [st.ps(f"side{i}", [P, 512]) for i in range(2)]
        tok = st.ps("tok", [P, BATCH, D])
        gates = side[0][:, 256:256 + BATCH * 24].rearrange("p (b n) -> p b n", b=BATCH)
        norms = side[1][:, 256:256 + BATCH * 8].rearrange("p (b n) -> p b n", b=BATCH)
        const, raw, gdiag = keep["const"], keep["raw"], keep["gdiag"]
        ident, headsel = const[:, C_ID:C_ID + P], const[:, C_SEL:C_SEL + 2]

        loaded = st.sem("p1_loaded")
        zeroed = st.sem("p1_zeroed")
        zero_stored = st.sem("p1_zero_stored")
        xt_ready = st.pair("p1_xt_ready")
        proj_ready, tap_done = st.sem("p1_proj_ready"), st.sem("p1_tap_done")
        conv_step, conv_done, silu_done = st.sem("p1_conv_step"), st.sem("p1_conv_done"), st.sem("p1_silu_done")
        sq_done = st.sem("p1_sq_done")
        diag_ready, ktok_ready, vtok_ready, small_ready = (st.sem(f"p1_{n}_ready") for n in ("diag", "ktok", "vtok", "small"))
        diag_out, ktok_out, vtok_out, small_out = (st.sem(f"p1_{n}_out") for n in ("diag", "ktok", "vtok", "small"))
        qk_stored, k_stored, v_stored, r_stored = (st.pair(f"p1_{n}_stored") for n in ("qk", "k", "v", "r"))
        rev_done, vrev_ready, vrev_out = st.sem("p1_rev_done"), st.sem("p1_vrev_ready"), st.sem("p1_vrev_out")
        NL = 4
        CB = 3 * KT

        with nc.Block() as block:
            @block.sync
            def _(sp):
                sp.dma_start(const[:, :], io["const"]).then_inc(loaded, 16)
                sp.dma_start(w_qkv[:, :, :], io["w_qkv"]).then_inc(loaded, 16)
                sp.dma_start(w_gate[:, :, :], io["w_gate"]).then_inc(loaded, 16)
                sp.dma_start(taps[:, :, :], io["taps"]).then_inc(loaded, 16)

                def load(t, p):
                    sp.dma_start(xt[p][:, :, :, :], row(io["xt"], t)).then_inc(xt_ready[p], 16)

                def store(t, p):
                    n = t + 1
                    sp.wait_ge(silu_done, n * CB - KT)
                    sp.dma_start(row(io["qk_s"], t), yT[p][:, 0:2 * KT, :]).then_inc(qk_stored[p], 16)
                    sp.wait_ge(ktok_out, n)
                    sp.dma_start(row(io["k_s"], t), ktok[p][:, :, :]).then_inc(k_stored[p], 16)
                    sp.wait_ge(vtok_out, n + 1)
                    sp.dma_start(io["v_s"][:, bass.ds(t * P, P), :].rearrange("b p d -> p b d"),
                                 vtok[p][:, :, :]).then_inc(v_stored[p], 16)
                    sp.wait_ge(vrev_out, n + 1)
                    sp.dma_start(io["vr_s"][:, bass.ds(t * -P + (SEQ - P), P), :].rearrange("b p d -> p b d"),
                                 vrev[p][:, :, :]).then_inc(r_stored[p], 16)

                load(0, 0)
                load(1, 1)
                sp.wait_ge(zeroed, 1)
                sp.dma_start(io["vr_s"][:, SEQ:SEQ + WIN, :].rearrange("b p d -> p b d"), zero[:, :, :]).then_inc(zero_stored, 16)
                with sp.Fori(0, STEPS // 2 - 1) as i:
                    for p in range(2):
                        store(i * 2 + p, p)
                        sp.wait_ge(small_ready, i * 2 + p + 1)
                        load(i * 2 + p + 2, p)
                for p in range(2):
                    store(STEPS - 2 + p, p)
                for p in range(2):
                    sp.wait_ge(qk_stored[p], 8 * STEPS)
                    sp.wait_ge(k_stored[p], 8 * STEPS + 16)
                    sp.wait_ge(v_stored[p], 8 * STEPS + 16)
                    sp.wait_ge(r_stored[p], 8 * STEPS + 16)
                sp.wait_ge(zero_stored, 16)

            @block.tensor
            def _(pe):
                pe.wait_ge(loaded, 16 * NL)

                def products(t, p):
                    for cb in range(CB):
                        pe.wait_ge(conv_done, t * CB + cb + 1)
                        for half in range(2):
                            for k in range(KT):
                                last = nc.tensor.matmul(
                                    proj[cb % 2][:, 2 * half:2 * half + 2, 0:XW], w_qkv[:, k, cb * P:cb * P + P],
                                    xt[p][:, k, 2 * half:2 * half + 2, :], start=(k == 0), stop=(k == KT - 1))
                        last.then_inc(proj_ready, 1)

                def after(t, p):
                    pe.wait_ge(silu_done, t * CB + 2 * KT)
                    pe.wait_ge(vrev_out, t + 1)
                    pe.wait_ge(diag_out, t + 1)
                    pe.wait_ge(small_out, t + 1)
                    for b in range(BATCH):
                        for hh in range(KT):
                            last = nc.tensor.transpose(tok[:, b, hh * P:hh * P + P],
                                                       yT[p][:, KT + hh, b * P:b * P + P], ident)
                    last.then_inc(ktok_ready, 1)
                    for b in range(BATCH):
                        for hh in range(KT):
                            for par in range(2):
                                kk = yT[p][64 * par:64 * par + DK, KT + hh, :]
                                c = (b * KT + hh) * CH
                                for q in range(NQ):
                                    part = kk[:, b * P + q * CH:b * P + q * CH + CH]
                                    last = nc.tensor.matmul(side[par][q * CH:q * CH + CH, c:c + CH], part, part,
                                                            start=True, stop=True)
                    last.then_inc(diag_ready, 1)
                    pe.wait_ge(diag_out, t + 2)
                    for b in range(BATCH):
                        for k in range(KT):
                            nc.tensor.matmul(gates[:, b, :], xt[p][:, k, b, HALO:XW], w_gate[:, k, :],
                                             start=(k == 0), stop=(k == KT - 1))
                    pe.wait_ge(sq_done, t + 1)
                    for j in range(2):
                        for hh in range(KT):
                            for b in range(BATCH):
                                c = j * HEADS + 2 * hh
                                last = nc.tensor.matmul(norms[:, b, c:c + 2], sq[:, j * KT + hh, b * P:b * P + P],
                                                        headsel, start=True, stop=True)
                    last.then_inc(small_ready, 1)
                    pe.wait_ge(silu_done, t * CB + CB)
                    pe.wait_ge(ktok_out, t + 1)
                    for b in range(BATCH):
                        for hh in range(KT):
                            last = nc.tensor.transpose(tok[:, b, hh * P:hh * P + P],
                                                       yT[p][:, 2 * KT + hh, b * P:b * P + P], ident)
                    last.then_inc(vtok_ready, 1)
                    pe.wait_ge(rev_done, t * KT + KT)
                    pe.wait_ge(vtok_out, t + 2)
                    for b in range(BATCH):
                        for hh in range(KT):
                            last = nc.tensor.transpose(tok[:, b, hh * P:hh * P + P], yrev[p][:, hh, b, :], ident)
                    last.then_inc(vrev_ready, 1)

                def arrived(p, n):
                    pe.wait_ge(xt_ready[p], n * 16 + 16)

                arrived(0, 0)
                products(0, 0)
                arrived(1, 0)
                products(1, 1)
                after(0, 0)
                with pe.Fori(1, STEPS // 2) as i:
                    arrived(0, i)
                    products(i * 2, 0)
                    after(i * 2 - 1, 1)
                    arrived(1, i)
                    products(i * 2 + 1, 1)
                    after(i * 2, 0)
                after(STEPS - 1, 1)

            @block.scalar
            def _(act):
                act.wait_ge(loaded, 16 * NL)

                def silu(t, p, cb):
                    act.wait_ge(conv_done, t * CB + cb + 3)
                    nc.scalar.activation(yT[p][:, cb, :].rearrange("p (b n) -> p b n", b=BATCH),
                                         acc[cb % 3][:, :, :], ACT.Silu).then_inc(silu_done, 1)
                    if cb >= 2 * KT:
                        nc.scalar.activation(yrev[p][:, cb - 2 * KT, :, :][:, :, ::-1], acc[cb % 3][:, :, :],
                                             ACT.Silu).then_inc(rev_done, 1)

                def tile(t, p):
                    for cb in range(CB):
                        act.wait_ge(proj_ready, t * CB + cb + 1)
                        if cb >= 3:
                            act.wait_ge(silu_done, t * CB + cb - 2)
                        nc.scalar.activation(acc[cb % 3][:, :, :], proj[cb % 2][:, :, HALO:XW], ACT.Copy,
                                             scale=taps[:, cb, HALO:CONV]).then_inc(tap_done, 1)
                        if cb >= 1:
                            silu(t, p, cb - 1)
                    silu(t, p, CB - 1)
                    act.wait_ge(silu_done, t * CB + CB)
                    act.wait_ge(rev_done, t * KT + KT)

                def copies(t, p):
                    for par in range(2):
                        act.wait_ge(diag_ready, t + 1)
                        last = nc.scalar.activation(gdiag[:, bass.ds(t * 2 + par, 1), :], side[par][:, 0:BH * CH].rearrange("p (o n) -> p o n", o=1), ACT.Copy)
                    last.then_inc(diag_out, 1)
                    act.wait_ge(ktok_ready, t + 1)
                    nc.scalar.activation(ktok[p][:, :, :], tok[:, :, :], ACT.Copy).then_inc(ktok_out, 1)
                    act.wait_ge(vrev_ready, t + 1)
                    nc.scalar.activation(vrev[p][:, :, :], tok[:, :, :], ACT.Copy).then_inc(vrev_out, 1)

                act.sem_inc(diag_out, 1)
                act.sem_inc(vrev_out, 1)
                for p in range(2):
                    act.sem_inc(k_stored[p], 16)
                    act.sem_inc(r_stored[p], 16)
                tile(0, 0)
                tile(1, 1)
                copies(0, 0)
                with act.Fori(1, STEPS // 2) as i:
                    for p in range(2):
                        t = i * 2 + p
                        act.wait_ge(qk_stored[p], i * 16)
                        act.wait_ge(vrev_ready, t - 1)
                        act.wait_ge(sq_done, t - 1)
                        tile(t, p)
                        act.wait_ge(k_stored[1 - p], (i + p) * 16)
                        act.wait_ge(r_stored[1 - p], (i + p) * 16)
                        copies(t - 1, 1 - p)
                act.wait_ge(k_stored[1], 8 * STEPS)
                act.wait_ge(r_stored[1], 8 * STEPS)
                copies(STEPS - 1, 1)

            @block.vector
            def _(dve):
                dve.wait_ge(loaded, 16 * NL)
                dve.sem_inc(conv_done, 2)
                dve.sem_inc(vtok_out, 1)
                dve.sem_inc(small_out, 1)
                for p in range(2):
                    dve.sem_inc(v_stored[p], 16)

                def tile(t):
                    for cb in range(CB):
                        dve.wait_ge(tap_done, t * CB + cb + 1)
                        for j in range(HALO):
                            if j:
                                dve.wait_ge(conv_step, (t * CB + cb) * (HALO - 1) + j)
                            nc.vector.scalar_tensor_tensor(
                                out=acc[cb % 3][:, :, :], in0=proj[cb % 2][:, :, j:j + P], scalar=taps[:, cb, j:j + 1],
                                in1=acc[cb % 3][:, :, :], op0=ALU.mult, op1=ALU.add,
                            ).then_inc(conv_step if j < HALO - 1 else conv_done, 1)

                def copies(t, p):
                    dve.wait_ge(small_ready, t + 1)
                    nc.vector.tensor_copy(raw[:, bass.ds(t * BATCH, BATCH), 0:24], gates[:, :, :])
                    nc.vector.tensor_copy(raw[:, bass.ds(t * BATCH, BATCH), 24:32], norms[:, :, :]).then_inc(small_out, 1)
                    dve.wait_ge(vtok_ready, t + 1)
                    nc.vector.tensor_copy(vtok[p][:, :, :], tok[:, :, :]).then_inc(vtok_out, 1)

                tile(0)
                tile(1)
                copies(0, 0)
                with dve.Fori(1, STEPS // 2) as i:
                    for p in range(2):
                        t = i * 2 + p
                        tile(t)
                        dve.wait_ge(v_stored[1 - p], (i + p) * 16)
                        copies(t - 1, 1 - p)
                dve.wait_ge(v_stored[1], 8 * STEPS)
                copies(STEPS - 1, 1)

            @block.gpsimd
            def _(pool):
                nc.gpsimd.memset(zero[:, :, :], 0.0).then_inc(zeroed, 1)

                def squares(t, p):
                    pool.wait_ge(silu_done, t * CB + 2 * KT)
                    if p or not isinstance(t, int):
                        pool.wait_ge(small_ready, t)
                    nc.gpsimd.tensor_tensor(sq[:, :, :], yT[p][:, 0:2 * KT, :], yT[p][:, 0:2 * KT, :],
                                            ALU.mult).then_inc(sq_done, 1)

                squares(0, 0)
                squares(1, 1)
                with pool.Fori(1, STEPS // 2) as i:
                    for p in range(2):
                        squares(i * 2 + p, p)


def weights(nc, sems, io, keep):
    st = Stage(nc, sems)
    with st.ctx:
        prm = st.sb("prm", [P, NGATE + 2 * HEADS])
        itemp = st.sb("itemp", [P, HEADS])
        eps = st.sb("eps", [P, HEADS])
        slope = st.sb("slope", [P, HEADS])
        half = st.sb("half", [P, STEPS * BATCH, HEADS])
        lg = st.sb("lg", [P, STEPS * BATCH, HEADS, 5])
        mx = st.sb("mx", [P, STEPS * BATCH * HEADS])
        beta = st.sb("beta", [P, STEPS * BATCH, HEADS])
        ssk = st.sb("ssk", [P, STEPS * BATCH, HEADS])
        rk = st.sb("rk", [P, STEPS * BATCH, HEADS])
        sk = st.sb("sk", [P, STEPS * BATCH, HEADS])
        rq = st.sb("rq", [P, STEPS * BATCH, HEADS])
        tri = st.sb("tri", [P, SLOTS, CH, CH])
        inv = st.sb("inv", [P, SLOTS, CH, CH])
        prod = st.sb("prod", [P, SLOTS * (CH - 1) * (CH - 1)])
        const, raw, gdiag, pw, scales = keep["const"], keep["raw"], keep["gdiag"], keep["pw"], keep["scales"]
        NT = STEPS * BATCH
        lgf = lg[:, :, :, :].rearrange("p t h f -> p (t h) f")
        blocks = gdiag[:, :, :].rearrange("p t (s j) -> p (t s) j", j=CH)

        def streams(ap):
            return ap.rearrange("p (t b) (k r) -> p t r (b k)", t=STEPS, r=2)

        prm_in, exps, roots = st.sem("p2_prm_in"), st.sem("p2_exps"), st.sem("p2_roots")
        chain, to_exp, to_root = st.sem("p2_chain"), st.sem("p2_to_exp"), st.sem("p2_to_root")
        diag_scaled, diag_stored, tri_in = st.sem("p2_diag_scaled"), st.sem("p2_diag_stored"), st.sem("p2_tri_in")
        inv_done, inv_stored = st.sem("p2_inv_done"), st.sem("p2_inv_stored")

        with nc.Block() as block:
            @block.sync
            def _(sp):
                src = io["prm"]
                sp.dma_start(prm[:, :], bass.AP(tensor=src.tensor, offset=0, ap=[[0, P], [1, NGATE + 2 * HEADS]])).then_inc(prm_in, 16)
                sp.wait_ge(diag_scaled, 1)
                sp.dma_start(io["a_s"], blocks).then_inc(diag_stored, 16)
                sp.wait_ge(diag_stored, 16)
                for q in range(NQ):
                    for g in range(GRP // P):
                        sp.dma_start(tri[:, q * (GRP // P) + g, :, :],
                                     io["a_s"][q * CH:q * CH + CH, g * P:g * P + P, :].rearrange("i g j -> g i j")
                                     ).then_inc(tri_in, 16)
                sp.wait_ge(inv_done, 1)
                for q in range(NQ):
                    for g in range(GRP // P):
                        sp.dma_start(io["t_s"][q * CH:q * CH + CH, g * P:g * P + P, :].rearrange("j g i -> g j i"),
                                     inv[:, q * (GRP // P) + g, :, :]).then_inc(inv_stored, 16)
                sp.wait_ge(inv_stored, 16 * SLOTS)

            @block.scalar
            def _(act):
                act.wait_ge(prm_in, 16)
                nc.scalar.activation(itemp[:, :], prm[:, NGATE:NGATE + HEADS], ACT.Exp, scale=-1.0).then_inc(exps, 1)
                nc.scalar.activation(beta[:, :, :], raw[:, :, NGATE:NGATE + HEADS], ACT.Exp, scale=-1.0).then_inc(exps, 1)
                act.wait_ge(to_exp, 1)
                nc.scalar.activation(lgf, lgf, ACT.Exp).then_inc(exps, 1)
                act.wait_ge(to_root, 1)
                nc.scalar.activation(sk[:, :, :], ssk[:, :, :], ACT.Sqrt)
                nc.scalar.activation(rq[:, :, :], rq[:, :, :], ACT.Sqrt).then_inc(roots, 1)

            @block.vector
            def _(dve):
                n = [0]

                def link(ins):
                    n[0] += 1
                    ins.then_inc(chain, 1)
                    dve.wait_ge(chain, n[0])

                nc.vector.memset(inv[:, :, :, :], 0.0)
                nc.vector.tensor_scalar(rq[:, :, :], raw[:, :, 24:24 + HEADS], L2_EPS, None, ALU.add)
                nc.vector.tensor_scalar(ssk[:, :, :], raw[:, :, 28:28 + HEADS], L2_EPS, None, ALU.add).then_inc(to_root, 1)
                dve.wait_ge(prm_in, 16)
                link(nc.vector.tensor_tensor(lg[:, :, :, :].rearrange("p t h f -> p t (h f)"), raw[:, :, 0:NGATE],
                                             bcast_mid(prm[:, 0:NGATE], NT), ALU.add))
                dve.wait_ge(exps, 1)
                link(nc.vector.tensor_tensor(lg[:, :, :, :], lg[:, :, :, :],
                                             bcast(bcast_mid(itemp[:, :], NT), 5), ALU.mult))
                link(nc.vector.tensor_reduce(mx[:, :], lgf, AX.X, ALU.max))
                nc.vector.tensor_tensor(lgf, lgf, bcast(mx[:, :], 5), ALU.subtract).then_inc(to_exp, 1)
                link(nc.vector.tensor_scalar(eps[:, :], prm[:, NGATE + HEADS:NGATE + 2 * HEADS], 0.0, 0.2, ALU.max, ALU.min))
                link(nc.vector.tensor_scalar(slope[:, :], eps[:, :], -5.0, 1.0, ALU.mult, ALU.add))
                dve.wait_ge(exps, 2)
                link(nc.vector.tensor_scalar(beta[:, :, :], beta[:, :, :], 1.0, None, ALU.add))
                link(nc.vector.reciprocal(beta[:, :, :], beta[:, :, :]))
                dve.wait_ge(exps, 3)
                link(nc.vector.tensor_reduce(mx[:, :], lgf, AX.X, ALU.add))
                link(nc.vector.reciprocal(mx[:, :], mx[:, :]))
                link(nc.vector.tensor_tensor(lgf, lgf, bcast(mx[:, :], 5), ALU.mult))
                link(nc.vector.tensor_tensor(lg[:, :, :, :], lg[:, :, :, :], bcast(bcast_mid(slope[:, :], NT), 5), ALU.mult))
                link(nc.vector.tensor_tensor(pw[:, :, :, :].rearrange("p h f t -> p t h f"), lg[:, :, :, :],
                                             bcast(bcast_mid(eps[:, :], NT), 5), ALU.add))
                link(nc.vector.reciprocal(half[:, :, :], ssk[:, :, :]))
                link(nc.vector.tensor_tensor(half[:, :, :], half[:, :, :], beta[:, :, :], ALU.mult))
                link(nc.vector.tensor_copy(scales[:, 0, :, :, :], streams(half[:, :, :])))
                gam = scales[:, 0, :, :, :].rearrange("p t r s -> p (t r s)")
                link(nc.vector.tensor_tensor(blocks, blocks, bcast(gam, CH), ALU.mult))
                nc.vector.tensor_tensor(blocks, blocks, bcast_mid(const[:, C_DIAG:C_DIAG + CH], GRP),
                                        ALU.mult).then_inc(diag_scaled, 1)
                dve.wait_ge(roots, 1)
                nc.vector.tensor_copy(scales[:, 1, :, :, :], streams(sk[:, :, :]))
                link(nc.vector.reciprocal(rq[:, :, :], rq[:, :, :]))
                link(nc.vector.tensor_tensor(rk[:, :, :], rq[:, :, :], pw[:, :, 3, :].rearrange("p h t -> p t h"), ALU.mult))
                nc.vector.tensor_copy(scales[:, 2, :, :, :], streams(rk[:, :, :]))
                flat = inv[:, :, :, :].rearrange("p s c i -> p s (c i)")
                link(nc.vector.memset(flat[:, :, 0:CH * CH:CH + 1], 1.0))
                dve.wait_ge(tri_in, 16 * SLOTS)
                for i in range(1, CH):
                    pr = prod[:, 0:SLOTS * i * i].rearrange("p (s c j) -> p s c j", s=SLOTS, c=i)
                    a = tri[:, :, i, 0:i]
                    a = bass.AP(tensor=a.tensor, offset=a.offset, ap=[a.ap[0], a.ap[1], [0, i], a.ap[2]])
                    link(nc.vector.tensor_tensor(pr, inv[:, :, 0:i, 0:i], a, ALU.mult))
                    link(nc.vector.tensor_reduce(inv[:, :, 0:i, i:i + 1].rearrange("p s c o -> p s (c o)"), pr, AX.X, ALU.add))
                nc.vector.tensor_copy(mx[:, 0:1], inv[:, 0, 0, 0:1]).then_inc(inv_done, 1)


def fir(nc, sems, io, keep):
    st = Stage(nc, sems)
    with st.ctx:
        win = [st.sb(f"win{i}", [P, BATCH, 2 * STEPS, DK]) for i in range(2)]
        toe = [st.sb(f"toe{i}", [P, FCH, NF, WIN]) for i in range(2)]
        mixed = [st.sb(f"mixed{i}", [P, STEPS * BATCH, DK]) for i in range(2)]
        part = [[st.sb(f"part{i}{f}", [P, FCH, STEPS * BATCH]) for f in range(NF)] for i in range(2)]
        two = [st.sb(f"two{i}", [P, FCH, STEPS * BATCH]) for i in range(2)]
        conv = [[st.ps(f"conv{i}{f}", [P, FCH, STEPS * BATCH]) for f in range(NF)] for i in range(2)]
        pw = keep["pw"]
        NT = STEPS * BATCH
        NG = DK // FCH

        win_in, toe_in = st.pair("p3_win_in"), st.pair("p3_toe_in")
        conv_ready, scaled = st.sem("p3_conv_ready"), st.sem("p3_scaled")
        two_done, mixed_done = st.sem("p3_two_done"), st.sem("p3_mixed_done")
        mixed_stored = st.pair("p3_mixed_stored")

        with nc.Block() as block:
            @block.sync
            def _(sp):
                def windows(h):
                    for b in range(BATCH):
                        src = io["vr_s"]
                        sp.dma_start(win[h % 2][:, b, :, :],
                                     bass.AP(tensor=src.tensor, offset=(b * (SEQ + WIN) + SEQ - WIN) * D + h * DK,
                                             ap=[[D, P], [-WIN * D, 2 * STEPS], [1, DK]])).then_inc(win_in[h % 2], 16)

                def store(h):
                    sp.wait_ge(mixed_done, (h + 1) * NG + 2)
                    for b in range(BATCH):
                        sp.dma_start(io["mix_s"][:, :, b, h * DK:h * DK + DK].rearrange("t p d -> p t d"),
                                     mixed[h % 2][:, b:NT:BATCH, :]).then_inc(mixed_stored[h % 2], 16)

                for h in range(HEADS):
                    if h >= 2:
                        sp.wait_ge(conv_ready, (h - 1) * NG)
                    windows(h)
                    for g in range(NG):
                        n = h * NG + g
                        if n >= 2:
                            sp.wait_ge(conv_ready, n - 1)
                        src = io["firp"]
                        sp.dma_start(toe[n % 2][:, :, :, :].rearrange("p c f m -> p (c f) m"),
                                     bass.AP(tensor=src.tensor, offset=(h * DK + g * FCH) * NF * FIRPAD,
                                             ap=[[1, P], [FIRPAD, FCH * NF], [1, WIN]])).then_inc(toe_in[n % 2], 16)
                    if h >= 1:
                        store(h - 1)
                store(HEADS - 1)
                for i in range(2):
                    sp.wait_ge(mixed_stored[i], 16 * BATCH * (HEADS // 2 + 1))

            @block.tensor
            def _(pe):
                with pe.Fori(0, HEADS // 2) as i:
                    for hp in range(2):
                        pe.wait_ge(win_in[hp], i * (16 * BATCH) + 16 * BATCH)
                        for g in range(NG):
                            n = (i * 2 + hp) * NG + g
                            pe.wait_ge(toe_in[g % 2], (i * 2 + hp) * (8 * NG) + (g // 2) * 16 + 16)
                            pe.wait_ge(scaled, n + 1)
                            for c in range(FCH):
                                w = win[hp][:, :, :, g * FCH + c].rearrange("p b (t e) -> p e t b", e=2)
                                for f in range(NF):
                                    for e in range(2):
                                        last = nc.tensor.matmul(conv[g % 2][f][WIN * e:WIN * e + WIN, c, :],
                                                                toe[g % 2][:, c, f, :], w[:, e, :, :],
                                                                start=True, stop=True)
                            last.then_inc(conv_ready, 1)

            @block.vector
            def _(dve):
                dve.sem_inc(scaled, 2)
                dve.sem_inc(mixed_done, 2)
                for p in range(2):
                    dve.sem_inc(mixed_stored[p], 16 * BATCH)
                with dve.Fori(0, HEADS // 2) as i:
                    for hp in range(2):
                        h = i * 2 + hp
                        for g in range(NG):
                            n = h * NG + g
                            dve.wait_ge(conv_ready, n + 1)
                            for f in range(NF):
                                last = nc.vector.tensor_tensor(
                                    part[g % 2][f][:, :, :], conv[g % 2][f][:, :, :],
                                    bcast_mid(pw[:, bass.ds(h, 1), f, :].rearrange("p o t -> p (o t)"), FCH), ALU.mult)
                            last.then_inc(scaled, 1)
                            dve.wait_ge(scaled, n + 3)
                            dve.wait_ge(two_done, n + 1)
                            if g == 0:
                                dve.wait_ge(mixed_stored[hp], i * (16 * BATCH) + 16 * BATCH)
                            nc.vector.tensor_tensor(
                                mixed[hp][:, :, g * FCH:g * FCH + FCH].rearrange("p t c -> p c t"),
                                two[g % 2][:, :, :], part[g % 2][2][:, :, :], ALU.add).then_inc(mixed_done, 1)

            @block.gpsimd
            def _(pool):
                with pool.Fori(0, HEADS // 2) as i:
                    for hp in range(2):
                        h = i * 2 + hp
                        for g in range(NG):
                            n = h * NG + g
                            pool.wait_ge(scaled, n + 3)
                            pool.wait_ge(mixed_done, n + 1)
                            nc.gpsimd.tensor_tensor(two[g % 2][:, :, :], part[g % 2][0][:, :, :], part[g % 2][1][:, :, :],
                                                    ALU.add).then_inc(two_done, 1)


def delta(nc, sems, io, keep):
    st = Stage(nc, sems)
    with st.ctx:
        wo = st.sb("wo", [P, KT, D])
        wo_raw = st.sb("wo_raw", [P, KT, D])
        norm_w = st.sb("norm_w", [P, 1])
        power = st.sb("power", [P, NS])
        head_eps = st.sb("head_eps", [P, NS])
        ln_eps = st.sb("ln_eps", [P, BATCH])
        qk = [st.sb(f"qk{i}", [P, 2 * KT, TOK]) for i in range(2)]
        ktok = [st.sb(f"kt{i}", [P, BATCH, D]) for i in range(2)]
        vtok = [st.sb(f"vt{i}", [P, BATCH, D]) for i in range(2)]
        xres = [st.sb(f"xres{i}", [P, BATCH, D]) for i in range(2)]
        mix = [st.sb(f"mix{i}", [P, BATCH, D]) for i in range(2)]
        tinv = [st.sb(f"tinv{i}", [P, NS, CH]) for i in range(2)]
        tdiag = [st.sb(f"tdiag{i}", [P, NS, P]) for i in range(2)]
        goff = [st.sb(f"goff{i}", [P, NS, P]) for i in range(2)]
        att = [st.sb(f"att{i}", [P, NS, P]) for i in range(2)]
        v2 = [st.sb(f"v2{i}", [P, 2, BH, DK]) for i in range(2)]
        x0 = st.sb("x0", [P, 2, BH, DK])
        xs = st.sb("xs", [P, 2, BH, DK])
        us = st.sb("us", [P, 2, BH, DK])
        S = st.sb("S", [P, BH, DK])
        o = st.sb("o", [P, BH, 2, DK])
        osq = st.sb("osq", [P, BH, 2, DK])
        ss = st.sb("ss", [P, NS])
        oT = st.sb("oT", [P, KT, TOK])
        y = [st.sb(f"y{i}", [P, BATCH, D]) for i in range(2)]
        stats = st.sb("stats", [P, BATCH, 6])
        mv = st.sb("mv", [P, BATCH, 2])
        rstd = st.sb("rstd", [P, BATCH])
        G = [st.ps(f"G{i}", [P, 4, P]) for i in range(2)]
        X = [st.ps(f"X{i}", [P, BH, DK]) for i in range(2)]
        Y = [st.ps(f"Y{i}", [P, BH, DK]) for i in range(2)]
        W = st.ps("W", [P, BATCH, D])
        WT = W[:, :, :].rearrange("p b d -> p (b d)").rearrange("p (k n) -> p k n", k=KT)
        const, scales = keep["const"], keep["scales"]
        ident = const[:, C_ID:C_ID + P]
        mask = [const[:, C_OFF:C_OFF + P], const[:, C_ATT:C_ATT + P]]
        ROUNDS = 8
        ITER = NQ

        tg_done, v2_done, direct_done = st.sem("p4_tg_done"), st.sem("p4_v2_done"), st.sem("p4_direct_done")
        power_set, par_in, wo_done, s_zero = st.sem("p4_power_set"), st.sem("p4_par_in"), st.sem("p4_wo_done"), st.sem("p4_zero")
        qk_in, kt_in, vt_in, x_in, mix_in, t_in = (st.pair(f"p4_{n}_in") for n in ("qk", "kt", "vt", "x", "mix", "t"))
        pre_ready, mask_done, prep_done = st.sem("p4_pre_ready"), st.sem("p4_mask_done"), st.sem("p4_prep_done")
        x_ready, x_done, y_ready, u_done = (st.sem(f"p4_{n}") for n in ("x_ready", "x_done", "y_ready", "u_done"))
        o_ready, s_ready, s_done, o_done = (st.sem(f"p4_{n}") for n in ("o_ready", "s_ready", "s_done", "o_done"))
        mixed, sq_done, ss_done, rs_done, on_done, st_done, pool_link = (
            st.sem(f"p4_{n}") for n in ("mixed", "sq_done", "ss_done", "rs_done", "on_done", "st_done", "pool_link"))
        oT_ready, oT_done, wo_ready, y_done, var_done, rstd_done, x1_done = (
            st.sem(f"p4_{n}") for n in ("oT_ready", "oT_done", "wo_ready", "y_done", "var_done", "rstd_done", "x1_done"))
        x1_stored = st.pair("p4_x1_stored")

        with nc.Block() as block:
            @block.sync
            def _(sp):
                sp.dma_start(wo_raw[:, :, :], io["w_o"]).then_inc(par_in, 16)
                sp.dma_start(norm_w[:, :], io["norm_w"]).then_inc(par_in, 16)

                def load(t, p):
                    sp.dma_start(qk[p][:, :, :], row(io["qk_s"], t)).then_inc(qk_in[p], 16)
                    sp.dma_start(tinv[p][:, :, :], io["t_s"][:, bass.ds(t * NS, NS), :]).then_inc(t_in[p], 16)
                    sp.dma_start(vtok[p][:, :, :], io["v_s"][:, bass.ds(t * P, P), :].rearrange("b p d -> p b d")).then_inc(vt_in[p], 16)
                    sp.dma_start(ktok[p][:, :, :], row(io["k_s"], t)).then_inc(kt_in[p], 16)
                    sp.dma_start(mix[p][:, :, :], row(io["mix_s"], t)).then_inc(mix_in[p], 16)
                    sp.dma_start(xres[p][:, :, :], io["x"][:, bass.ds(t * P, P), :].rearrange("b p d -> p b d")).then_inc(x_in[p], 16)

                def store(t, p):
                    sp.wait_ge(x1_done, t + 1)
                    sp.dma_start(row(io["x1_s"], t), y[p][:, :, :]).then_inc(x1_stored[p], 16)

                load(0, 0)
                load(1, 1)
                with sp.Fori(0, STEPS // 2 - 1) as i:
                    for p in range(2):
                        store(i * 2 + p, p)
                        load(i * 2 + p + 2, p)
                for p in range(2):
                    store(STEPS - 2 + p, p)
                for p in range(2):
                    sp.wait_ge(x1_stored[p], 8 * STEPS + 16)

            @block.tensor
            def _(pe):
                def pre(t, p, n):
                    pe.wait_ge(qk_in[p], n * 16 + 16)
                    for r in range(ROUNDS):
                        kind, par, half = r // 4, r // 2 % 2, r % 2
                        pe.wait_ge(mask_done, t * ROUNDS + r + 1)
                        for j in range(4):
                            s = half * 4 + j
                            b, hh = s // KT, s % KT
                            rows = slice(64 * par, 64 * par + DK)
                            last = nc.tensor.matmul(G[r % 2][:, j, :], qk[p][rows, KT + hh, b * P:b * P + P],
                                                    qk[p][rows, (0 if kind else KT) + hh, b * P:b * P + P],
                                                    start=True, stop=True)
                        last.then_inc(pre_ready, 1)

                def chain(t, p, n):
                    pe.wait_ge(s_done, t + 1)
                    pe.wait_ge(o_done, t + 1)
                    for k in range(ITER):
                        for par in range(2):
                            if k:
                                pe.wait_ge(u_done, t * 2 * ITER + 2 * (k - 1) + par + 1)
                            if k == 1:
                                pe.wait_ge(mask_done, t * ROUNDS + 4 + 2)
                            for s in range(BH):
                                b, hh = s // KT, s % KT
                                rows = slice(64 * par, 64 * par + DK)
                                if k == 0:
                                    last = nc.tensor.matmul(X[par][:, s, :], qk[p][rows, KT + hh, b * P:b * P + P],
                                                            S[rows, s, :], start=True, stop=True)
                                else:
                                    last = nc.tensor.matmul(X[par][:, s, :], goff[p][:, par * BH + s, :],
                                                            us[:, par, s, :], start=True, stop=True)
                            last.then_inc(x_ready, 1)
                        if k == 0:
                            pe.wait_ge(prep_done, t + 1)
                        for par in range(2):
                            pe.wait_ge(x_done, t * 2 * ITER + 2 * k + par + 1)
                            for s in range(BH):
                                last = nc.tensor.matmul(Y[par][:, s, :], tdiag[p][:, par * BH + s, :],
                                                        (xs if k else x0)[:, par, s, :],
                                                        start=True, stop=True)
                            last.then_inc(y_ready, 1)
                    pe.wait_ge(mask_done, t * ROUNDS + ROUNDS + 2)
                    for par in range(2):
                        pe.wait_ge(u_done, t * 2 * ITER + 2 * (ITER - 1) + par + 1)
                        for s in range(BH):
                            b, hh = s // KT, s % KT
                            rows = slice(64 * par, 64 * par + DK)
                            nc.tensor.matmul(X[par][:, s, :], qk[p][rows, hh, b * P:b * P + P], S[rows, s, :],
                                             start=True, stop=False)
                            last = nc.tensor.matmul(X[par][:, s, :], att[p][:, par * BH + s, :], us[:, par, s, :],
                                                    start=False, stop=True)
                        last.then_inc(o_ready, 1)
                    pe.wait_ge(kt_in[p], n * 16 + 16)
                    for s in range(BH):
                        b, hh = s // KT, s % KT
                        for par in range(2):
                            c = hh * P + par * DK
                            last = nc.tensor.matmul(Y[0][64 * par:64 * par + DK, s, :], ktok[p][:, b, c:c + DK],
                                                    us[:, par, s, :], start=True, stop=True)
                    last.then_inc(s_ready, 1)

                def tail(t):
                    pe.wait_ge(on_done, t + 1)
                    pe.wait_ge(y_done, t + 1)
                    for hh in range(KT):
                        for b in range(BATCH):
                            last = nc.tensor.transpose(WT[:, hh, b * P:b * P + P],
                                                       o[:, b * KT + hh, :, :].rearrange("p r d -> p (r d)"), ident)
                    last.then_inc(oT_ready, 1)
                    pe.wait_ge(oT_done, t + 1)
                    for b in range(BATCH):
                        for hh in range(KT):
                            last = nc.tensor.matmul(W[:, b, :], oT[:, hh, b * P:b * P + P], wo[:, hh, :],
                                                    start=(hh == 0), stop=(hh == KT - 1))
                    last.then_inc(wo_ready, 1)

                pe.wait_ge(s_zero, 1)
                pe.wait_ge(wo_done, 1)
                pre(0, 0, 0)
                with pe.Fori(0, STEPS // 2 - 1) as i:
                    chain(i * 2, 0, i)
                    pre(i * 2 + 1, 1, i)
                    tail(i * 2)
                    chain(i * 2 + 1, 1, i)
                    pre(i * 2 + 2, 0, i + 1)
                    tail(i * 2 + 1)
                n = STEPS // 2 - 1
                chain(STEPS - 2, 0, n)
                pre(STEPS - 1, 1, n)
                tail(STEPS - 2)
                chain(STEPS - 1, 1, n)
                tail(STEPS - 1)

            @block.scalar
            def _(act):
                def step(t):
                    for k in range(ITER):
                        for par in range(2):
                            m = t * 2 * ITER + 2 * k + par + 1
                            act.wait_ge(y_ready, m)
                            nc.scalar.activation(us[:, par, :, :], Y[par][:, :, :], ACT.Copy).then_inc(u_done, 1)
                    act.wait_ge(oT_ready, t + 1)
                    nc.scalar.activation(oT[:, :, :], WT, ACT.Copy).then_inc(oT_done, 1)

                with act.Fori(0, STEPS) as t:
                    step(t)

            @block.vector
            def _(dve):
                n = [0]
                nc.vector.memset(S[:, :, :], 0.0).then_inc(s_zero, 1)
                dve.wait_ge(par_in, 32)
                nc.vector.tensor_scalar(wo[:, :, :], wo_raw[:, :, :], norm_w[:, 0:1], None, ALU.mult).then_inc(wo_done, 1)
                dve.sem_inc(mask_done, 2)
                dve.sem_inc(s_done, 1)
                dve.sem_inc(o_done, 1)
                dve.sem_inc(y_done, 1)
                for p in range(2):
                    dve.sem_inc(x1_stored[p], 16)

                def masks(t, p):
                    for r in range(ROUNDS):
                        kind, par, half = r // 4, r // 2 % 2, r % 2
                        s = par * BH + half * 4
                        dve.wait_ge(pre_ready, t * ROUNDS + r + 1)
                        nc.vector.tensor_tensor((att if kind else goff)[p][:, s:s + 4, :], G[r % 2][:, :, :],
                                                bcast_mid(mask[kind], 4), ALU.mult).then_inc(mask_done, 1)

                def chain(t, p, n):
                    dve.wait_ge(prep_done, t + 1)
                    for k in range(ITER):
                        for par in range(2):
                            dve.wait_ge(x_ready, t * 2 * ITER + 2 * k + par + 1)
                            nc.vector.tensor_tensor((xs if k else x0)[:, par, :, :], (x0[:, par, :, :] if k else v2[p][:, par, :, :]),
                                                    X[par][:, :, :], ALU.subtract).then_inc(x_done, 1)
                    dve.wait_ge(s_ready, t + 1)
                    nc.vector.tensor_tensor(S[:, :, :], S[:, :, :], Y[0][:, :, :], ALU.add).then_inc(s_done, 1)
                    dve.wait_ge(o_ready, t * 2 + 2)
                    for par in range(2):
                        c3 = scales[:, 2, bass.ds(t, 1), par, :].rearrange("p o s -> p (o s)")
                        last = nc.vector.tensor_tensor(o[:, :, par, :], X[par][:, :, :], bcast(c3, DK), ALU.mult)
                    last.then_inc(o_done, 1)
                    dve.wait_ge(o_done, t + 2)
                    nc.vector.tensor_tensor(o[:, :, :, :].rearrange("p s r d -> p (s r d)"), o[:, :, :, :].rearrange("p s r d -> p (s r d)"),
                                            mix[p][:, :, :].rearrange("p b d -> p (b d)"), ALU.add).then_inc(mixed, 1)

                def norm(t):
                    dve.wait_ge(sq_done, t + 1)
                    nc.vector.tensor_reduce(ss[:, :], osq[:, :, :, :].rearrange("p s r d -> p (s r) d"), AX.X,
                                            ALU.add).then_inc(ss_done, 1)
                    dve.wait_ge(rs_done, t + 1)
                    of = o[:, :, :, :].rearrange("p s r d -> p (s r) d")
                    nc.vector.scalar_tensor_tensor(out=of, in0=of, scalar=float(DK) ** 0.5, in1=bcast(ss[:, :], DK),
                                                   op0=ALU.mult, op1=ALU.mult).then_inc(on_done, 1)

                def tail(t, p, n):
                    dve.wait_ge(wo_ready, t + 1)
                    dve.wait_ge(x_in[p], n * 16 + 16)
                    dve.wait_ge(x1_stored[p], n * 16 + 16)
                    nc.vector.tensor_tensor(y[p][:, :, :], W[:, :, :], xres[p][:, :, :], ALU.add).then_inc(y_done, 1)
                    dve.wait_ge(y_done, t + 2)
                    for b in range(BATCH):
                        last = nc.vector.bn_stats(stats[:, b, :], y[p][:, b, :])
                    last.then_inc(st_done, 1)
                    dve.wait_ge(par_in, 32)
                    dve.wait_ge(st_done, t + 1)
                    for b in range(BATCH):
                        last = nc.vector.bn_aggr(mv[:, b, :], stats[:, b, :])
                    last.then_inc(var_done, 1)
                    dve.wait_ge(rstd_done, t + 1)
                    for b in range(BATCH):
                        last = nc.vector.tensor_scalar(y[p][:, b, :], y[p][:, b, :], mv[:, b, 0:1], rstd[:, b:b + 1],
                                                       ALU.subtract, ALU.mult)
                    last.then_inc(x1_done, 1)

                masks(0, 0)
                with dve.Fori(0, STEPS // 2 - 1) as i:
                    for p in range(2):
                        chain(i * 2 + p, p, i)
                        norm(i * 2 + p)
                        masks(i * 2 + p + 1, 1 - p)
                        tail(i * 2 + p, p, i)
                n = STEPS // 2 - 1
                chain(STEPS - 2, 0, n)
                norm(STEPS - 2)
                masks(STEPS - 1, 1)
                tail(STEPS - 2, 0, n)
                chain(STEPS - 1, 1, n)
                norm(STEPS - 1)
                tail(STEPS - 1, 1, n)

            @block.gpsimd
            def _(pool):
                nc.gpsimd.memset(head_eps[:, :], DK * LN_EPS)
                nc.gpsimd.memset(ln_eps[:, :], LN_EPS)
                nc.gpsimd.memset(power[:, :], -0.5).then_inc(power_set, 1)
                pool.wait_ge(power_set, 1)

                def prep(t, p, n):
                    pool.wait_ge(vt_in[p], n * 16 + 16)
                    for par in range(2):
                        sk = scales[:, 1, bass.ds(t, 1), par, :].rearrange("p o s -> p (o s)")
                        last = nc.gpsimd.tensor_tensor(v2[p][:, par, :, :],
                                                vtok[p][:, :, :].rearrange("p b (k r d) -> p r (b k) d", k=KT, r=2)[:, par, :, :],
                                                bcast(sk, DK), ALU.mult)
                    last.then_inc(v2_done, 1)
                    dir_ = vtok[p][:, :, :].rearrange("p b (h d) -> p b h d", h=HEADS)
                    p4 = keep["pw"][:, :, 4, bass.ds(t * BATCH, BATCH)].rearrange("p h b -> p b h")
                    pool.wait_ge(v2_done, t + 1)
                    nc.gpsimd.tensor_tensor(dir_, dir_, bcast(p4, DK), ALU.mult).then_inc(direct_done, 1)
                    pool.wait_ge(mix_in[p], n * 16 + 16)
                    pool.wait_ge(direct_done, t + 1)
                    nc.gpsimd.tensor_tensor(mix[p][:, :, :], mix[p][:, :, :], vtok[p][:, :, :], ALU.add)
                    pool.wait_ge(t_in[p], n * 16 + 16)
                    gam = scales[:, 0, bass.ds(t, 1), :, :].rearrange("p o r s -> p (o r s)")
                    nc.gpsimd.tensor_tensor(tinv[p][:, :, :], tinv[p][:, :, :], bcast(gam, CH), ALU.mult).then_inc(tg_done, 1)
                    pool.wait_ge(tg_done, t + 1)
                    ti = tinv[p][:, :, :]
                    last = nc.gpsimd.tensor_tensor(
                        tdiag[p][:, :, :].rearrange("p s (q i) -> p s q i", q=NQ),
                        bass.AP(tensor=ti.tensor, offset=ti.offset, ap=[ti.ap[0], [CH, NS], [0, NQ], [1, CH]]),
                        bcast_mid(const[:, C_BD:C_BD + P].rearrange("p (q i) -> p q i", q=NQ), NS), ALU.mult)
                    last.then_inc(prep_done, 1)

                def norm(t):
                    pool.wait_ge(mixed, t + 1)
                    nc.gpsimd.tensor_tensor(osq[:, :, :, :], o[:, :, :, :], o[:, :, :, :], ALU.mult).then_inc(sq_done, 1)
                    pool.wait_ge(ss_done, t + 1)
                    nc.gpsimd.tensor_tensor(ss[:, :], ss[:, :], head_eps[:, :], ALU.add).then_inc(pool_link, 1)
                    pool.wait_ge(pool_link, t * 2 + 1)
                    nc.gpsimd.tensor_tensor(ss[:, :], ss[:, :], power[:, :], ALU.pow).then_inc(rs_done, 1)

                def tail(t):
                    pool.wait_ge(var_done, t + 1)
                    nc.gpsimd.tensor_tensor(rstd[:, :], mv[:, :, 1:2].rearrange("p b o -> p (b o)"), ln_eps[:, :],
                                            ALU.add).then_inc(pool_link, 1)
                    pool.wait_ge(pool_link, t * 2 + 2)
                    nc.gpsimd.tensor_tensor(rstd[:, :], rstd[:, :], power[:, 0:BATCH], ALU.pow).then_inc(rstd_done, 1)

                prep(0, 0, 0)
                with pool.Fori(0, STEPS // 2 - 1) as i:
                    prep(i * 2 + 1, 1, i)
                    norm(i * 2)
                    tail(i * 2)
                    prep(i * 2 + 2, 0, i + 1)
                    norm(i * 2 + 1)
                    tail(i * 2 + 1)
                n = STEPS // 2 - 1
                prep(STEPS - 1, 1, n)
                norm(STEPS - 2)
                tail(STEPS - 2)
                norm(STEPS - 1)
                tail(STEPS - 1)


def round_weights(nc, sems, io, wr, flag, total):
    st = Stage(nc, sems)
    with st.ctx:
        CW = 2048
        NCH = W_END // CW
        raw = [st.sb(f"wraw{i}", [P, CW]) for i in range(2)]
        diff = st.sb("wdiff", [P, CW])
        worst = st.sb("worst", [P, NCH])
        most = st.sb("most", [P, 1])
        ones = st.sb("ones", [P, 1])
        raw_in = st.pair("p5_raw_in")
        rounded, diff_done, worst_done, most_done, total_ready, flag_done, flag_stored = (
            st.sem(f"p5_{n}") for n in ("rounded", "diff_done", "worst_done", "most_done", "total_ready", "flag_done", "flag_stored"))

        with nc.Block() as block:
            @block.sync
            def _(sp):
                for c in range(NCH):
                    if c >= 2:
                        sp.wait_ge(diff_done, c - 1)
                    sp.dma_start(raw[c % 2][:, :], io["ffn_w"][:, c * CW:c * CW + CW]).then_inc(raw_in[c % 2], 16)
                sp.wait_ge(flag_done, 1)
                sp.dma_start(io["flag_s"], flag[:, :]).then_inc(flag_stored, 16)
                sp.wait_ge(flag_stored, 16)

            @block.vector
            def _(dve):
                nc.vector.memset(ones[:, :], 1.0)
                for c in range(NCH):
                    dve.wait_ge(raw_in[c % 2], 16 * (c // 2) + 16)
                    nc.vector.tensor_copy(wr[:, c * CW:c * CW + CW], raw[c % 2][:, :]).then_inc(rounded, 1)
                    dve.wait_ge(rounded, c + 1)
                    if c:
                        dve.wait_ge(worst_done, c)
                    nc.vector.tensor_tensor(diff[:, :], raw[c % 2][:, :], wr[:, c * CW:c * CW + CW].bitcast(f32),
                                            ALU.subtract).then_inc(diff_done, 1)
                    dve.wait_ge(diff_done, c + 1)
                    nc.vector.tensor_reduce(worst[:, c:c + 1], diff[:, :], AX.X, ALU.max,
                                            apply_absolute_value=True).then_inc(worst_done, 1)
                dve.wait_ge(worst_done, NCH)
                nc.vector.tensor_reduce(most[:, :], worst[:, :], AX.X, ALU.max).then_inc(most_done, 1)

            @block.tensor
            def _(pe):
                pe.wait_ge(most_done, 1)
                nc.tensor.matmul(total, most[:, :], ones[:, :], start=True, stop=True).then_inc(total_ready, 1)

            @block.scalar
            def _(act):
                act.wait_ge(total_ready, 1)
                nc.scalar.activation(flag[:, :], total, ACT.Copy).then_inc(flag_done, 1)


def ffn(nc, sems, io, keep):
    outer = Stage(nc, sems)
    with outer.ctx:
        flag = outer.sb("flag", [1, 1])
        scol = outer.sb("scol", [P, 4 * HT])
        srow = outer.sb("srow", [P, D])
        power = outer.sb("power5", [P, BATCH])
        ln_eps = outer.sb("ln_eps5", [P, BATCH])
        x1 = [outer.sb(f"x1{i}", [P, BATCH, D]) for i in range(2)]
        z = [outer.sb(f"z{i}", [P, BATCH, D]) for i in range(2)]
        gate = [outer.sb(f"gate{i}", [P, TOK]) for i in range(2)]
        stats = outer.sb("stats5", [P, BATCH, 6])
        mv = outer.sb("mv5", [P, BATCH, 2])
        rstd = outer.sb("rstd5", [P, BATCH])
        B = [outer.ps(f"B{i}", [P, TOK]) for i in range(4)]
        O = outer.ps("O", [P, BATCH, D])
        T = outer.ps("T", [P, KT, TOK])
        ident = keep["const"][:, C_ID:C_ID + P]
        fast = Stage(nc, sems)
        with fast.ctx:
            wr = fast.sb("wr", [P, W_END], f32r)
            round_weights(nc, sems, io, wr, flag, B[0][0:1, 0:1])
            xh, xl = fast.sb("xh", [P, KT, TOK], f32r), fast.sb("xl", [P, KT, TOK], f32r)
            sets = [[fast.sb(f"act{i}{n}", [P, HT, TOK], f32r) for n in "hl"] for i in range(2)]
            yb = [fast.sb(f"yb{i}", [P, TOK]) for i in range(3)]
        slow = Stage(nc, sems)
        with slow.ctx:
            wblk = [slow.sb(f"wblk{i}", [P, HT, P]) for i in range(2)]
            xf = slow.sb("xf", [P, KT, TOK])
            full = [slow.sb(f"full{i}", [P, HT, TOK]) for i in range(2)]

        par_in, power_set = outer.sem("p6_par_in"), outer.sem("p6_power_set")
        x_in, out_stored, w_in = outer.pair("p6_x_in"), outer.pair("p6_out_stored"), outer.pair("p6_w_in")
        (tr_ready, xh_done, x_split, bank_ready, gate_done, f_ready, lo_done, o_ready, o_free, z_done,
         st_done, var_done, rs_link, rstd_done, out_done, blk_used) = (outer.sem(f"p6_{n}") for n in (
             "tr_ready", "xh_done", "x_split", "bank_ready", "gate_done", "f_ready", "lo_done", "o_ready",
             "o_free", "z_done", "st_done", "var_done", "rs_link", "rstd_done", "out_done", "blk_used"))
        BLOCKS = 3 * HT
        F0 = 4
        SLOTS_T = 4 * HT
        WBLOCKS = 3 * HT + KT

        def either(eng, emit):
            inexact = eng.value_load(io["flag_s"].bitcast(i32), min_val=0, max_val=2 ** 31 - 1)
            with eng.If(inexact != 0):
                emit(True)
            with eng.Else():
                emit(False)

        with nc.Block() as block:
            @block.sync
            def _(sp):
                sp.dma_start(scol[:, :], io["scol"]).then_inc(par_in, 16)
                src = io["srow"]
                sp.dma_start(srow[:, :], bass.AP(tensor=src.tensor, offset=0, ap=[[0, P], [1, D]])).then_inc(par_in, 16)

                def load(t, p):
                    sp.dma_start(x1[p][:, :, :], row(io["x1_s"], t)).then_inc(x_in[p], 16)

                def store(t, p):
                    sp.wait_ge(out_done, t + 1)
                    sp.dma_start(io["out"][:, bass.ds(t * P, P), :].rearrange("b p d -> p b d"), z[p][:, :, :]).then_inc(out_stored[p], 16)

                def stream(t):
                    w = io["ffn_w"]
                    for n in range(WBLOCKS):
                        sp.wait_ge(blk_used, t * WBLOCKS + n + 1)
                        if n < HT:
                            for j, base in enumerate((W1, W2)):
                                sp.dma_start(wblk[n % 2][:, j * KT:j * KT + KT, :],
                                             w[:, base:base + KT * HID].rearrange("p (k m) -> p k m", k=KT)[:, :, n * P:n * P + P]
                                             ).then_inc(w_in[n % 2], 16)
                        else:
                            base, width, m = ((H1, HID, n - HT) if n < 2 * HT else (H2, HID, n - 2 * HT) if n < 3 * HT
                                              else (W3, D, n - 3 * HT))
                            sp.dma_start(wblk[n % 2][:, :, :], w[:, base:base + HT * width].rearrange("p (k m) -> p k m", k=HT)[:, :, m * P:m * P + P]
                                         ).then_inc(w_in[n % 2], 16)

                def emit(general):
                    load(0, 0)
                    load(1, 1)
                    with sp.Fori(0, STEPS // 2 - 1) as i:
                        for p in range(2):
                            if general:
                                stream(i * 2 + p)
                            store(i * 2 + p, p)
                            load(i * 2 + p + 2, p)
                    for p in range(2):
                        if general:
                            stream(STEPS - 2 + p)
                        store(STEPS - 2 + p, p)

                either(sp, emit)
                for p in range(2):
                    sp.wait_ge(out_stored[p], 8 * STEPS + 16)

            @block.tensor
            def _(pe):
                def turn(p, n):
                    pe.wait_ge(x_in[p], n * 16 + 16)
                    for k in range(KT):
                        for b in range(BATCH):
                            last = nc.tensor.transpose(T[:, k, b * P:b * P + P], x1[p][:, b, k * P:k * P + P], ident)
                    last.then_inc(tr_ready, 1)

                def layers(t, general):
                    def weights_in(n):
                        per = HT + HT + KT // 2
                        before = n // 2 * 2 if n < HT else HT + (n - HT) // 2
                        pe.wait_ge(w_in[n % 2], t * (16 * per) + 16 * (before + (2 if n < HT else 1)))

                    def block_rhs(layer, k):
                        if layer == 0:
                            return [xf[:, k, :]] if general else [xh[:, k, :], xl[:, k, :]]
                        s = (layer - 1) % 2
                        return [full[s][:, k, :]] if general else [sets[s][0][:, k, :], sets[s][1][:, k, :]]

                    pe.wait_ge(x_split, t + 1)
                    for layer in range(3):
                        kts = HT if layer else KT
                        for m in range(HT):
                            n = layer * HT + m
                            if general:
                                weights_in(n)
                            for j in range(1 if layer else 2):
                                slot = 2 * m + j if layer == 0 else (layer + 1) * HT + m
                                if layer == 0:
                                    pe.wait_ge(f_ready, F0 + t * BLOCKS + (m - 1 if m >= 2 else 2 * m - 2))
                                elif layer == 1 and m == 0:
                                    pe.wait_ge(f_ready, F0 + t * BLOCKS + HT - 1)
                                elif m >= 4 or layer == 2:
                                    pe.wait_ge(f_ready, F0 + t * BLOCKS + n - 3)
                                base, width = ((W1, W2)[j], HID) if layer == 0 else ((H1, H2)[layer - 1], HID)
                                for k in range(kts):
                                    if layer and m == 0:
                                        pe.wait_ge(f_ready if general else lo_done, (F0 if general else 0) + t * BLOCKS + (layer - 1) * HT + k + 1)
                                    c = base + k * width + m * P
                                    w = wblk[n % 2][:, j * KT + k, :] if general else wr[:, c:c + P]
                                    parts = block_rhs(layer, k)
                                    for i, part in enumerate(parts):
                                        last = nc.tensor.matmul(B[slot % 4][:, :], w, part, start=(k == 0 and i == 0),
                                                                stop=(k == kts - 1 and i == len(parts) - 1))
                                last.then_inc(bank_ready, 1)
                            if general:
                                pe.drain().then_inc(blk_used, 1)

                def last_layer(t, general):
                    pe.wait_ge(o_free, t + 1)
                    pe.wait_ge(f_ready if general else lo_done, (F0 if general else 0) + t * BLOCKS + BLOCKS)
                    if general:
                        per = HT + HT + KT // 2
                        for half in range(KT):
                            n = 3 * HT + half
                            pe.wait_ge(w_in[n % 2], t * (16 * per) + 16 * (HT + (n - HT) // 2 + 1))
                            for b in range(BATCH):
                                for k in range(HT):
                                    last = nc.tensor.matmul(O[:, b, half * P:half * P + P], full[0][:, k, b * P:b * P + P],
                                                            wblk[n % 2][:, k, :], start=(k == 0), stop=(k == HT - 1))
                            pe.drain().then_inc(blk_used, 1)
                    else:
                        for b in range(BATCH):
                            for k in range(HT):
                                for i in range(2):
                                    last = nc.tensor.matmul(O[:, b, :], sets[0][i][:, k, b * P:b * P + P],
                                                            wr[:, W3 + k * D:W3 + k * D + D], start=(k == 0 and i == 0),
                                                            stop=(k == HT - 1 and i == 1))
                    last.then_inc(o_ready, 1) if not general else pe.drain().then_inc(o_ready, 1)

                def emit(general):
                    turn(0, 0)
                    with pe.Fori(0, STEPS // 2 - 1) as i:
                        for p in range(2):
                            layers(i * 2 + p, general)
                            turn(1 - p, i + p)
                            last_layer(i * 2 + p, general)
                    layers(STEPS - 2, general)
                    turn(1, STEPS // 2 - 1)
                    last_layer(STEPS - 2, general)
                    layers(STEPS - 1, general)
                    last_layer(STEPS - 1, general)

                either(pe, emit)

            @block.scalar
            def _(act):
                act.wait_ge(par_in, 32)

                def split(t, general):
                    act.wait_ge(tr_ready, t + 1)
                    nc.scalar.activation((xf if general else xh)[:, :, :], T[:, :, :], ACT.Copy).then_inc(x_split if general else xh_done, 1)

                def layers(t, general):
                    for m in range(HT):
                        act.wait_ge(bank_ready, t * SLOTS_T + 2 * m + 1)
                        act.wait_ge(f_ready, F0 + t * BLOCKS + (m - 1 if m >= 2 else 2 * m - 2))
                        nc.scalar.activation(gate[m % 2][:, :], B[2 * m % 4][:, :], ACT.Silu, scale=scol[:, m:m + 1]).then_inc(gate_done, 1)
                    for layer in (1, 2):
                        for m in range(HT):
                            slot = (layer + 1) * HT + m
                            n = layer * HT + m
                            act.wait_ge(bank_ready, t * SLOTS_T + slot + 1)
                            if not general:
                                act.wait_ge(lo_done, t * BLOCKS + n - 2)
                            dst = full[layer % 2][:, m, :] if general else yb[n % 3][:, :]
                            last = nc.scalar.activation(dst, B[slot % 4][:, :], ACT.Gelu, scale=scol[:, slot:slot + 1])
                            if not general:
                                last = nc.scalar.activation(sets[layer % 2][0][:, m, :], B[slot % 4][:, :], ACT.Gelu,
                                                            scale=scol[:, slot:slot + 1])
                            last.then_inc(f_ready, 1)

                def emit(general):
                    split(0, general)
                    with act.Fori(0, STEPS - 1) as t:
                        layers(t, general)
                        split(t + 1, general)
                    layers(STEPS - 1, general)

                either(act, emit)

            @block.vector
            def _(dve):
                dve.wait_ge(par_in, 32)
                dve.sem_inc(f_ready, F0)
                dve.sem_inc(o_free, 1)
                dve.sem_inc(blk_used, 2)
                for p in range(2):
                    dve.sem_inc(out_stored[p], 16)

                def split(t):
                    dve.wait_ge(xh_done, t + 1)
                    nc.vector.tensor_tensor(xl[:, :, :], T[:, :, :], xh[:, :, :].bitcast(f32), ALU.subtract).then_inc(x_split, 1)

                def low(t, n, s, m):
                    dve.wait_ge(f_ready, F0 + t * BLOCKS + n + 1)
                    nc.vector.tensor_tensor(sets[s][1][:, m, :], yb[n % 3][:, :], sets[s][0][:, m, :].bitcast(f32),
                                            ALU.subtract).then_inc(lo_done, 1)

                def layers(t, general):
                    for m in range(HT):
                        dve.wait_ge(gate_done, t * HT + m + 1)
                        dve.wait_ge(bank_ready, t * SLOTS_T + 2 * m + 2)
                        if not general and m >= 3:
                            dve.wait_ge(lo_done, t * BLOCKS + m - 2)
                        for dst in [full[0][:, m, :]] if general else [yb[m % 3][:, :], sets[0][0][:, m, :]]:
                            last = nc.vector.scalar_tensor_tensor(
                                out=dst, in0=B[(2 * m + 1) % 4][:, :], scalar=scol[:, HT + m:HT + m + 1],
                                in1=gate[m % 2][:, :], op0=ALU.mult, op1=ALU.mult)
                        last.then_inc(f_ready, 1)
                        if not general and m:
                            low(t, m - 1, 0, m - 1)
                    if not general:
                        low(t, HT - 1, 0, HT - 1)
                        for layer in (1, 2):
                            for m in range(HT):
                                low(t, layer * HT + m, layer % 2, m)
                        dve.wait_ge(lo_done, t * BLOCKS + BLOCKS)

                def tail(t, p, n):
                    dve.wait_ge(o_ready, t + 1)
                    dve.wait_ge(out_stored[p], n * 16 + 16)
                    nc.vector.tensor_tensor(z[p][:, :, :], O[:, :, :], bcast_mid(srow[:, :], BATCH), ALU.mult).then_inc(o_free, 1)
                    dve.wait_ge(o_free, t + 2)
                    nc.vector.tensor_tensor(z[p][:, :, :], z[p][:, :, :], x1[p][:, :, :], ALU.add).then_inc(z_done, 1)
                    dve.wait_ge(z_done, t + 1)
                    for b in range(BATCH):
                        last = nc.vector.bn_stats(stats[:, b, :], z[p][:, b, :])
                    last.then_inc(st_done, 1)
                    dve.wait_ge(par_in, 32)
                    dve.wait_ge(st_done, t + 1)
                    for b in range(BATCH):
                        last = nc.vector.bn_aggr(mv[:, b, :], stats[:, b, :])
                    last.then_inc(var_done, 1)
                    dve.wait_ge(rstd_done, t + 1)
                    for b in range(BATCH):
                        last = nc.vector.tensor_scalar(z[p][:, b, :], z[p][:, b, :], mv[:, b, 0:1], rstd[:, b:b + 1],
                                                       ALU.subtract, ALU.mult)
                    last.then_inc(out_done, 1)

                def emit(general):
                    if not general:
                        split(0)
                    with dve.Fori(0, STEPS // 2 - 1) as i:
                        for p in range(2):
                            layers(i * 2 + p, general)
                            if not general:
                                split(i * 2 + p + 1)
                            tail(i * 2 + p, p, i)
                    n = STEPS // 2 - 1
                    layers(STEPS - 2, general)
                    if not general:
                        split(STEPS - 1)
                    tail(STEPS - 2, 0, n)
                    layers(STEPS - 1, general)
                    tail(STEPS - 1, 1, n)

                either(dve, emit)

            @block.gpsimd
            def _(pool):
                nc.gpsimd.memset(ln_eps[:, :], LN_EPS)
                nc.gpsimd.memset(power[:, :], -0.5).then_inc(power_set, 1)
                pool.wait_ge(power_set, 1)

                def tail(t):
                    pool.wait_ge(var_done, t + 1)
                    nc.gpsimd.tensor_tensor(rstd[:, :], mv[:, :, 1:2].rearrange("p b o -> p (b o)"), ln_eps[:, :],
                                            ALU.add).then_inc(rs_link, 1)
                    pool.wait_ge(rs_link, t + 1)
                    nc.gpsimd.tensor_tensor(rstd[:, :], rstd[:, :], power[:, :], ALU.pow).then_inc(rstd_done, 1)

                def emit(general):
                    with pool.Fori(0, STEPS) as t:
                        tail(t)

                either(pool, emit)


def build(nc, io):
    sems = ExitStack()
    with sems:
        whole = Stage(nc, sems)
        with whole.ctx:
            keep = {
                "const": whole.sb("const", [P, C_END]),
                "pw": whole.sb("pw", [P, HEADS, 5, STEPS * BATCH]),
                "scales": whole.sb("scales", [P, 3, STEPS, 2, BH]),
            }
            early = Stage(nc, sems)
            with early.ctx:
                keep["raw"] = early.sb("raw", [P, STEPS * BATCH, NRAW])
                keep["gdiag"] = early.sb("gdiag", [P, 2 * STEPS, BH * CH])
                project(nc, sems, io, keep)
                weights(nc, sems, io, keep)
            fir(nc, sems, io, keep)
            delta(nc, sems, io, keep)
            ffn(nc, sems, io, keep)


def host_layout(np, a):
    g = {k.replace("L0_attn_", "").replace("L0_ffn_", ""): np.asarray(v, dtype=np.float32) for k, v in a.items()}
    x = g["hidden_states"]
    cols = np.pad(x.transpose(0, 2, 1), ((0, 0), (0, 0), (HALO, 0)))
    xt = np.stack([cols[:, :, t * P:t * P + XW] for t in range(STEPS)])
    xt = xt.reshape(STEPS, BATCH, KT, P, XW).transpose(0, 3, 2, 1, 4)

    def kmajor(w):
        return w.T.reshape(w.shape[1] // P, P, w.shape[0]).transpose(1, 0, 2)

    def columns(w):
        return w.reshape(-1, P).T

    w_qkv = np.concatenate([kmajor(g[n]) for n in ("Wq", "Wk", "Wv")], axis=2)
    w_gate = np.concatenate([kmajor(g["gate_w"].reshape(NGATE, D)), kmajor(g["Wb"])], axis=2)
    taps = np.concatenate([g[n].reshape(KT, P, CONV) for n in ("conv_q", "conv_k", "conv_v")]).transpose(1, 0, 2)
    firp = np.zeros((D, NF, FIRPAD), np.float32)
    for f, (n, k) in enumerate(zip(("fir_s", "fir_m", "fir_l"), FIRS)):
        firp[:, f, WIN - 1:WIN - 1 + k] = g[n].reshape(D, k)[:, ::-1]
    prm = np.concatenate([g["gate_b"].reshape(-1), g["log_temp"].reshape(-1), g["eps_param"].reshape(-1)])[None]
    ffn_w = np.concatenate([kmajor(g[n]).reshape(P, -1) for n in ("w1_w", "w2_w", "h1_w", "h2_w", "w3_w")], axis=1)
    scol = np.concatenate([columns(g[n]) for n in ("w1_s", "w2_s", "h1_s", "h2_s")], axis=1)
    i, j = np.arange(P)[:, None], np.arange(P)[None, :]
    const = np.zeros((P, C_END), np.float32)
    const[:, C_ID:C_ID + P] = i == j
    const[:, C_OFF:C_OFF + P] = j // CH > i // CH
    const[:, C_ATT:C_ATT + P] = j >= i
    const[:, C_BD:C_BD + P] = j // CH == i // CH
    const[:, C_DIAG:C_DIAG + CH] = np.where(np.arange(CH)[None, :] < i % CH, -1.0, 0.0)
    const[:, C_SEL:C_SEL + 2] = i // DK == np.arange(2)[None, :]
    return {"x": x, "xt": xt, "w_qkv": w_qkv, "w_gate": w_gate, "taps": taps, "firp": firp, "prm": prm, "ffn_w": ffn_w,
            "scol": scol, "srow": g["w3_s"][None], "const": const, "w_o": kmajor(g["Wo"]),
            "norm_w": np.concatenate([g["norm_w"]] * 2)[:, None]}


SCRATCH = {
    "qk_s": (STEPS, P, 2 * KT, TOK),
    "k_s": (STEPS, P, BATCH, D),
    "v_s": (BATCH, SEQ, D),
    "vr_s": (BATCH, SEQ + WIN, D),
    "a_s": (P, GRP, CH),
    "t_s": (P, GRP, CH),
    "mix_s": (STEPS, P, BATCH, D),
    "x1_s": (STEPS, P, BATCH, D),
    "flag_s": (1, 1),
}


def kernel(**inputs):
    import numpy as np
    import concourse.bacc as bacc
    from concourse.bass_utils import run_bass_kernel_spmd

    nc = bacc.Bacc("TRN2", target_bir_lowering=False, num_devices=1)
    arrays = {f"in_{k}": np.ascontiguousarray(v) for k, v in host_layout(np, inputs).items()}
    io = {k[3:]: nc.dram_tensor(k, v.shape, f32, kind="ExternalInput").ap() for k, v in arrays.items()}
    for k, shape in SCRATCH.items():
        io[k] = nc.dram_tensor(k, shape, f32).ap()
    io["out"] = nc.dram_tensor("out", (BATCH, SEQ, D), f32, kind="ExternalOutput").ap()
    build(nc, io)
    r = run_bass_kernel_spmd(nc, [arrays], core_ids=[0])
    return r.results[0]["out"]
```

```python
import concourse.bass as bass
from concourse import mybir
from contextlib import ExitStack

f32 = mybir.dt.float32
f32r = mybir.dt.float32r
i32 = mybir.dt.int32
ALU = mybir.AluOpType
ACT = mybir.ActivationFunctionType
AX = mybir.AxisListType

P = 128
BATCH, SEQ, D, HEADS = 4, 2048, 256, 4
DK = D // HEADS
KT = D // P
STEPS = SEQ // P
TOK = BATCH * P
CONV = 4
HALO = CONV - 1
XW = P + HALO
FIRS = (3, 15, 63)
NF = len(FIRS)
WIN = 64
FIRPAD = 3 * WIN
FCH = 8
CH = 32
NQ = P // CH
BH = BATCH * KT
NS = 2 * BH
GRP = STEPS * NS
SLOTS = GRP * NQ // P
HID = 1024
HT = HID // P
NGATE = HEADS * 5
NRAW = NGATE + HEADS + HEADS
LN_EPS = 1e-5
L2_EPS = 1e-6
C_ID, C_OFF, C_ATT, C_DIAG, C_ONE, C_SEL, C_END = 0, P, 2 * P, 3 * P, 3 * P + CH, 3 * P + 2 * CH, 3 * P + 2 * CH + 2
W1, W2, H1, H2, W3 = 0, KT * HID, 2 * KT * HID, 2 * KT * HID + HT * HID, 2 * KT * HID + 2 * HT * HID
W_END = W3 + HT * D


class Stage:

    def __init__(self, nc, sems):
        self.nc, self.ctx, self.sems = nc, ExitStack(), sems

    def sb(self, name, shape, dt=f32):
        return self.ctx.enter_context(self.nc.sbuf_tensor(name, shape, dt))

    def ps(self, name, shape):
        return self.ctx.enter_context(self.nc.psum_tensor(name, shape, f32))

    def sem(self, name):
        return self.sems.enter_context(self.nc.semaphore(name))

    def pair(self, name):
        return [self.sem(f"{name}{i}") for i in range(2)]


def row(ap, t):
    names = [f"a{i}" for i in range(len(ap.shape) - 1)]
    return ap[bass.ds(t, 1)].rearrange(f"o {names[0]} {' '.join(names[1:])} -> {names[0]} (o {names[1]}) {' '.join(names[2:])}")


def bcast(ap, n):
    return bass.AP(tensor=ap.tensor, offset=ap.offset, ap=[*ap.ap, [0, n]])


def bcast_mid(ap, n):
    return bass.AP(tensor=ap.tensor, offset=ap.offset, ap=[ap.ap[0], [0, n], *ap.ap[1:]])


def project(nc, sems, io, keep):
    st = Stage(nc, sems)
    with st.ctx:
        w_qkv = st.sb("w_qkv", [P, KT, 3 * D])
        w_gate = st.sb("w_gate", [P, KT, NGATE + HEADS])
        taps = st.sb("taps", [P, 3 * KT, CONV])
        zero = st.sb("zero", [WIN, BATCH, D])
        xt = [st.sb(f"xt{i}", [P, KT, BATCH, XW]) for i in range(2)]
        acc = [st.sb(f"acc{i}", [P, BATCH, P]) for i in range(3)]
        yT = [st.sb(f"yT{i}", [P, 3 * KT, TOK]) for i in range(2)]
        sq = st.sb("sq", [P, KT, TOK])
        ktok = [st.sb(f"ktok{i}", [P, BATCH, D]) for i in range(2)]
        vtok = [st.sb(f"vtok{i}", [P, BATCH, D]) for i in range(2)]
        yrev = [st.sb(f"yrev{i}", [P, KT, BATCH, P]) for i in range(2)]
        vrev = [st.sb(f"vrev{i}", [P, BATCH, D]) for i in range(2)]
        proj = [st.ps(f"proj{i}", [P, BATCH, 2 * P]) for i in range(2)]
        side = [st.ps(f"side{i}", [P, 512]) for i in range(2)]
        tok = st.ps("tok", [P, BATCH, D])
        gates = side[0][:, 0:BATCH * 24].rearrange("p (b n) -> p b n", b=BATCH)
        norms = side[1][:, 0:BATCH * HEADS].rearrange("p (b n) -> p b n", b=BATCH)
        const, raw, gdiag = keep["const"], keep["raw"], keep["gdiag"]
        ident, headsel = const[:, C_ID:C_ID + P], const[:, C_SEL:C_SEL + 2]

        loaded = st.sem("p1_loaded")
        zeroed = st.sem("p1_zeroed")
        zero_stored = st.sem("p1_zero_stored")
        xt_ready = st.pair("p1_xt_ready")
        proj_ready, tap_done = st.sem("p1_proj_ready"), st.sem("p1_tap_done")
        conv_step, conv_done, silu_done = st.sem("p1_conv_step"), st.sem("p1_conv_done"), st.sem("p1_silu_done")
        sq_done = st.sem("p1_sq_done")
        diag_ready, ktok_ready, vtok_ready, small_ready = (st.sem(f"p1_{n}_ready") for n in ("diag", "ktok", "vtok", "small"))
        diag_out, ktok_out, vtok_out, small_out = (st.sem(f"p1_{n}_out") for n in ("diag", "ktok", "vtok", "small"))
        qk_stored, k_stored, v_stored, r_stored = (st.pair(f"p1_{n}_stored") for n in ("qk", "k", "v", "r"))
        rev_done, vrev_ready, vrev_out = st.sem("p1_rev_done"), st.sem("p1_vrev_ready"), st.sem("p1_vrev_out")
        NL = 4
        CB = 3 * KT

        with nc.Block() as block:
            @block.sync
            def _(sp):
                sp.dma_start(const[:, :], io["const"]).then_inc(loaded, 16)
                sp.dma_start(w_qkv[:, :, :], io["w_qkv"]).then_inc(loaded, 16)
                sp.dma_start(w_gate[:, :, :], io["w_gate"]).then_inc(loaded, 16)
                sp.dma_start(taps[:, :, :], io["taps"]).then_inc(loaded, 16)

                def load(t, p):
                    sp.dma_start(xt[p][:, :, :, :], row(io["xt"], t)).then_inc(xt_ready[p], 16)

                def store(t, p, more):
                    n = t + 1
                    sp.wait_ge(silu_done, n * CB - KT)
                    sp.dma_start(row(io["qk_s"], t), yT[p][:, 0:2 * KT, :]).then_inc(qk_stored[p], 16)
                    if more:
                        sp.wait_ge(small_ready, n)
                        load(t + 2, p)
                    sp.wait_ge(ktok_out, n)
                    sp.dma_start(row(io["k_s"], t), ktok[p][:, :, :]).then_inc(k_stored[p], 16)
                    sp.wait_ge(vtok_out, n)
                    sp.dma_start(io["v_s"][:, bass.ds(t * P, P), :].rearrange("b p d -> p b d"),
                                 vtok[p][:, :, :]).then_inc(v_stored[p], 16)
                    sp.wait_ge(vrev_out, n + 1)
                    sp.dma_start(io["vr_s"][:, bass.ds(t * -P + (SEQ - P), P), :].rearrange("b p d -> p b d"),
                                 vrev[p][:, :, :]).then_inc(r_stored[p], 16)

                load(0, 0)
                load(1, 1)
                sp.wait_ge(zeroed, 1)
                sp.dma_start(io["vr_s"][:, SEQ:SEQ + WIN, :].rearrange("b p d -> p b d"), zero[:, :, :]).then_inc(zero_stored, 16)
                with sp.Fori(0, STEPS // 2 - 1) as i:
                    for p in range(2):
                        store(i * 2 + p, p, True)
                for p in range(2):
                    store(STEPS - 2 + p, p, False)
                for p in range(2):
                    sp.wait_ge(qk_stored[p], 8 * STEPS)
                    sp.wait_ge(k_stored[p], 8 * STEPS + 16)
                    sp.wait_ge(v_stored[p], 8 * STEPS + 16)
                    sp.wait_ge(r_stored[p], 8 * STEPS + 16)
                sp.wait_ge(zero_stored, 16)

            @block.tensor
            def _(pe):
                pe.wait_ge(loaded, 16 * NL)

                def products(t, p, cb):
                    pe.wait_ge(conv_done, t * CB + cb + 1)
                    for half in range(2):
                        for k in range(KT):
                            last = nc.tensor.matmul(
                                proj[cb % 2][:, 2 * half:2 * half + 2, 0:XW], w_qkv[:, k, cb * P:cb * P + P],
                                xt[p][:, k, 2 * half:2 * half + 2, :], start=(k == 0), stop=(k == KT - 1))
                    last.then_inc(proj_ready, 1)

                def turn(src):
                    for b in range(BATCH):
                        for hh in range(KT):
                            last = nc.tensor.transpose(tok[:, b, hh * P:hh * P + P], src(hh, b), ident)
                    return last

                def keys(t, p):
                    pe.wait_ge(silu_done, t * CB + 2 * KT)
                    pe.wait_ge(vrev_out, t + 1)
                    pe.wait_ge(small_out, t + 1)
                    turn(lambda hh, b: yT[p][:, KT + hh, b * P:b * P + P]).then_inc(ktok_ready, 1)
                    for b in range(BATCH):
                        for hh in range(KT):
                            for par in range(2):
                                kk = yT[p][64 * par:64 * par + DK, KT + hh, :]
                                c = (b * KT + hh) * 2 * CH
                                for q in range(0, NQ, 2):
                                    part = kk[:, b * P + q * CH:b * P + (q + 2) * CH]
                                    last = nc.tensor.matmul(side[par][q * CH:(q + 2) * CH, c:c + 2 * CH], part, part,
                                                            start=True, stop=True)
                    last.then_inc(diag_ready, 1)

                def small(t, p):
                    pe.wait_ge(diag_out, t + 1)
                    for b in range(BATCH):
                        for k in range(KT):
                            nc.tensor.matmul(gates[:, b, :], xt[p][:, k, b, HALO:XW], w_gate[:, k, :],
                                             start=(k == 0), stop=(k == KT - 1))
                    pe.wait_ge(sq_done, t + 1)
                    for hh in range(KT):
                        for b in range(BATCH):
                            last = nc.tensor.matmul(norms[:, b, 2 * hh:2 * hh + 2], sq[:, hh, b * P:b * P + P],
                                                    headsel, start=True, stop=True)
                    last.then_inc(small_ready, 1)

                def values(t, p):
                    pe.wait_ge(silu_done, t * CB + CB)
                    pe.wait_ge(ktok_out, t + 1)
                    turn(lambda hh, b: yT[p][:, 2 * KT + hh, b * P:b * P + P]).then_inc(vtok_ready, 1)

                def back_to_front(t, p):
                    pe.wait_ge(rev_done, t * KT + KT)
                    pe.wait_ge(vtok_out, t + 1)
                    turn(lambda hh, b: yrev[p][:, hh, b, :]).then_inc(vrev_ready, 1)

                after = {0: keys, 1: small, 2: values, 4: back_to_front}

                def step(t, p, n, follow):
                    pe.wait_ge(xt_ready[p], n * 16 + 16)
                    for cb in range(CB):
                        products(t, p, cb)
                        if follow and cb in after:
                            after[cb](t - 1, 1 - p)

                step(0, 0, 0, False)
                with pe.Fori(0, STEPS // 2 - 1) as i:
                    step(i * 2 + 1, 1, i, True)
                    step(i * 2 + 2, 0, i + 1, True)
                step(STEPS - 1, 1, STEPS // 2 - 1, True)
                for piece in after.values():
                    piece(STEPS - 1, 1)

            @block.scalar
            def _(act):
                act.wait_ge(loaded, 16 * NL)

                def silu(t, p, cb):
                    act.wait_ge(conv_done, t * CB + cb + 3)
                    nc.scalar.activation(yT[p][:, cb, :].rearrange("p (b n) -> p b n", b=BATCH),
                                         acc[cb % 3][:, :, :], ACT.Silu).then_inc(silu_done, 1)
                    if cb >= 2 * KT:
                        nc.scalar.activation(yrev[p][:, cb - 2 * KT, :, :][:, :, ::-1], acc[cb % 3][:, :, :],
                                             ACT.Silu).then_inc(rev_done, 1)

                def keys_out(t, p, n):
                    act.wait_ge(ktok_ready, t + 1)
                    act.wait_ge(k_stored[p], n * 16 + 16)
                    nc.scalar.activation(ktok[p][:, :, :], tok[:, :, :], ACT.Copy).then_inc(ktok_out, 1)
                    act.wait_ge(diag_ready, t + 1)
                    for par in range(2):
                        for q in range(NQ):
                            rows = slice(q * CH, q * CH + CH)
                            src = side[par][rows, :].rearrange("p (s e c) -> p e s c", e=2, c=CH)[:, q % 2, :, :]
                            last = nc.scalar.activation(
                                gdiag[rows, bass.ds(t * 2 + par, 1), :].rearrange("p o (s c) -> p (o s) c", c=CH), src, ACT.Copy)
                    last.then_inc(diag_out, 1)

                def reversed_out(t, p, n):
                    act.wait_ge(vrev_ready, t + 1)
                    act.wait_ge(r_stored[p], n * 16 + 16)
                    nc.scalar.activation(vrev[p][:, :, :], tok[:, :, :], ACT.Copy).then_inc(vrev_out, 1)

                def step(t, p, n, follow, fresh):
                    for cb in range(CB):
                        act.wait_ge(proj_ready, t * CB + cb + 1)
                        if cb >= 3:
                            act.wait_ge(silu_done, t * CB + cb - 2)
                        nc.scalar.activation(acc[cb % 3][:, :, :], proj[cb % 2][:, :, HALO:XW], ACT.Copy,
                                             scale=taps[:, cb, HALO:CONV]).then_inc(tap_done, 1)
                        if follow and cb == 0:
                            keys_out(t - 1, 1 - p, n)
                        if cb >= 1:
                            if cb == 1 and not fresh:
                                act.wait_ge(qk_stored[p], (n + 1 - p) * 16)
                                act.wait_ge(sq_done, t - 1)
                            silu(t, p, cb - 1)
                        if follow and cb == 4:
                            reversed_out(t - 1, 1 - p, n)
                    silu(t, p, CB - 1)
                    act.wait_ge(silu_done, t * CB + CB)
                    act.wait_ge(rev_done, t * KT + KT)

                act.sem_inc(vrev_out, 1)
                for p in range(2):
                    act.sem_inc(k_stored[p], 16)
                    act.sem_inc(r_stored[p], 16)
                step(0, 0, 0, False, True)
                step(1, 1, 0, True, True)
                with act.Fori(1, STEPS // 2) as i:
                    step(i * 2, 0, i - 1, True, False)
                    step(i * 2 + 1, 1, i, True, False)
                keys_out(STEPS - 1, 1, STEPS // 2 - 1)
                reversed_out(STEPS - 1, 1, STEPS // 2 - 1)

            @block.vector
            def _(dve):
                dve.wait_ge(loaded, 16 * NL)
                dve.sem_inc(conv_done, 2)
                dve.sem_inc(small_out, 1)
                for p in range(2):
                    dve.sem_inc(v_stored[p], 16)

                def convolution(t, cb):
                    dve.wait_ge(tap_done, t * CB + cb + 1)
                    for j in range(HALO):
                        if j:
                            dve.wait_ge(conv_step, (t * CB + cb) * (HALO - 1) + j)
                        nc.vector.scalar_tensor_tensor(
                            out=acc[cb % 3][:, :, :], in0=proj[cb % 2][:, :, j:j + P], scalar=taps[:, cb, j:j + 1],
                            in1=acc[cb % 3][:, :, :], op0=ALU.mult, op1=ALU.add,
                        ).then_inc(conv_step if j < HALO - 1 else conv_done, 1)

                def small_copies(t):
                    dve.wait_ge(small_ready, t + 1)
                    nc.vector.tensor_copy(raw[:, bass.ds(t * BATCH, BATCH), 0:24], gates[:, :, :])
                    nc.vector.tensor_copy(raw[:, bass.ds(t * BATCH, BATCH), 24:24 + HEADS], norms[:, :, :]).then_inc(small_out, 1)

                def values_out(t, p, n):
                    dve.wait_ge(vtok_ready, t + 1)
                    dve.wait_ge(v_stored[p], n * 16 + 16)
                    nc.vector.tensor_copy(vtok[p][:, :, :], tok[:, :, :]).then_inc(vtok_out, 1)

                def step(t, p, n, follow):
                    for cb in range(CB):
                        convolution(t, cb)
                        if follow and cb == 1:
                            small_copies(t - 1)
                        if follow and cb == 2:
                            values_out(t - 1, 1 - p, n)

                step(0, 0, 0, False)
                with dve.Fori(0, STEPS // 2 - 1) as i:
                    step(i * 2 + 1, 1, i, True)
                    step(i * 2 + 2, 0, i, True)
                step(STEPS - 1, 1, STEPS // 2 - 1, True)
                small_copies(STEPS - 1)
                values_out(STEPS - 1, 1, STEPS // 2 - 1)

            @block.gpsimd
            def _(pool):
                nc.gpsimd.memset(zero[:, :, :], 0.0).then_inc(zeroed, 1)

                def squares(t, p, first):
                    pool.wait_ge(silu_done, t * CB + KT)
                    if not first:
                        pool.wait_ge(small_ready, t)
                    nc.gpsimd.tensor_tensor(sq[:, :, :], yT[p][:, 0:KT, :], yT[p][:, 0:KT, :],
                                            ALU.mult).then_inc(sq_done, 1)

                squares(0, 0, True)
                squares(1, 1, False)
                with pool.Fori(1, STEPS // 2) as i:
                    for p in range(2):
                        squares(i * 2 + p, p, False)


def weights(nc, sems, io, keep):
    st = Stage(nc, sems)
    with st.ctx:
        prm = st.sb("prm", [P, NGATE + 2 * HEADS])
        itemp = st.sb("itemp", [P, HEADS])
        eps = st.sb("eps", [P, HEADS])
        slope = st.sb("slope", [P, HEADS])
        half = st.sb("half", [P, STEPS * BATCH, HEADS])
        lg = st.sb("lg", [P, STEPS * BATCH, HEADS, 5])
        mx = st.sb("mx", [P, STEPS * BATCH * HEADS])
        beta = st.sb("beta", [P, STEPS * BATCH, HEADS])
        ssk = st.sb("ssk", [P, STEPS * BATCH, HEADS])
        gam = st.sb("gam", [P, STEPS, 2, BH])
        rq = st.sb("rq", [P, STEPS * BATCH, HEADS])
        tri = st.sb("tri", [P, SLOTS, CH, CH])
        inv = st.sb("inv", [P, SLOTS, CH, CH])
        prod = st.sb("prod", [P, GRP * CH])
        kk = st.sb("kk", [P, STEPS, 2, BH])
        gamT = st.ps("gamT", [P, GRP // P, P])
        const, raw, gdiag, pw, scales = keep["const"], keep["raw"], keep["gdiag"], keep["pw"], keep["scales"]
        NT = STEPS * BATCH
        lgf = lg[:, :, :, :].rearrange("p t h f -> p (t h) f")
        blocks = gdiag[:, :, :].rearrange("p t (s j) -> p (t s) j", j=CH)

        def streams(ap):
            return ap.rearrange("p (t b) (k r) -> p t r (b k)", t=STEPS, r=2)

        prm_in, exps, roots = st.sem("p2_prm_in"), st.sem("p2_exps"), st.sem("p2_roots")
        chain, to_exp, to_root = st.sem("p2_chain"), st.sem("p2_to_exp"), st.sem("p2_to_root")
        diag_scaled, diag_stored, tri_in = st.sem("p2_diag_scaled"), st.sem("p2_diag_stored"), st.sem("p2_tri_in")
        inv_done, inv_stored = st.sem("p2_inv_done"), st.sem("p2_inv_stored")
        gam_turned, turned, diag_picked = st.sem("p2_gam_turned"), st.sem("p2_turned"), st.sem("p2_diag_picked")

        with nc.Block() as block:
            @block.sync
            def _(sp):
                src = io["prm"]
                sp.dma_start(prm[:, :], bass.AP(tensor=src.tensor, offset=0, ap=[[0, P], [1, NGATE + 2 * HEADS]])).then_inc(prm_in, 16)
                sp.wait_ge(diag_scaled, 1)
                sp.dma_start(io["a_s"], blocks).then_inc(diag_stored, 16)
                sp.wait_ge(diag_stored, 16)
                for q in range(NQ):
                    for g in range(GRP // P):
                        sp.dma_start(tri[:, q * (GRP // P) + g, :, :],
                                     io["a_s"][q * CH:q * CH + CH, g * P:g * P + P, :].rearrange("i g j -> g i j")
                                     ).then_inc(tri_in, 16)
                sp.wait_ge(inv_done, GRP // P)
                for name, buf in (("t_s", inv), ("d_s", tri)):
                    if buf is tri:
                        sp.wait_ge(turned, 1)
                    for q in range(NQ):
                        for g in range(GRP // P):
                            sp.dma_start(io[name][q * CH:q * CH + CH, g * P:g * P + P, :].rearrange("j g i -> g j i"),
                                         buf[:, q * (GRP // P) + g, :, :]).then_inc(inv_stored, 16)
                sp.wait_ge(inv_stored, 16 * 2 * SLOTS)

            @block.scalar
            def _(act):
                act.wait_ge(prm_in, 16)
                nc.scalar.activation(itemp[:, :], prm[:, NGATE:NGATE + HEADS], ACT.Exp, scale=-1.0).then_inc(exps, 1)
                nc.scalar.activation(beta[:, :, :], raw[:, :, NGATE:NGATE + HEADS], ACT.Exp, scale=-1.0).then_inc(exps, 1)
                act.wait_ge(to_exp, 1)
                nc.scalar.activation(lgf, lgf, ACT.Exp).then_inc(exps, 1)
                act.wait_ge(to_root, 1)
                nc.scalar.activation(scales[:, 0, :, :].rearrange("p t (b h) -> p (t b) h", b=BATCH), ssk[:, :, :], ACT.Sqrt)
                nc.scalar.activation(rq[:, :, :], rq[:, :, :], ACT.Sqrt).then_inc(roots, 1)
                act.wait_ge(inv_done, GRP // P)
                nc.scalar.activation(tri[:, :, :, :], inv[:, :, :, :].rearrange("p s c i -> p s i c"), ACT.Copy).then_inc(turned, 1)

            @block.vector
            def _(dve):
                n = [0]

                def link(ins):
                    n[0] += 1
                    ins.then_inc(chain, 1)
                    dve.wait_ge(chain, n[0])

                nc.vector.memset(inv[:, :, :, :], 0.0)
                nc.vector.tensor_scalar(rq[:, :, :], raw[:, :, 24:24 + HEADS], L2_EPS, None, ALU.add)
                dve.wait_ge(diag_picked, 1)
                link(nc.vector.tensor_reduce(kk[:, :, :, :].rearrange("p t r s -> p (t r s)"),
                                             prod[:, :].rearrange("p (g j) -> p g j", j=CH), AX.X, ALU.add))
                for par in range(2):
                    last = nc.vector.tensor_scalar(streams(ssk[:, :, :])[:, :, par, :], kk[:, :, par, :], L2_EPS, None, ALU.add)
                last.then_inc(to_root, 1)
                dve.wait_ge(prm_in, 16)
                link(nc.vector.tensor_tensor(lg[:, :, :, :].rearrange("p t h f -> p t (h f)"), raw[:, :, 0:NGATE],
                                             bcast_mid(prm[:, 0:NGATE], NT), ALU.add))
                dve.wait_ge(exps, 1)
                link(nc.vector.tensor_tensor(lg[:, :, :, :], lg[:, :, :, :],
                                             bcast(bcast_mid(itemp[:, :], NT), 5), ALU.mult))
                link(nc.vector.tensor_reduce(mx[:, :], lgf, AX.X, ALU.max))
                nc.vector.tensor_tensor(lgf, lgf, bcast(mx[:, :], 5), ALU.subtract).then_inc(to_exp, 1)
                link(nc.vector.tensor_scalar(eps[:, :], prm[:, NGATE + HEADS:NGATE + 2 * HEADS], 0.0, 0.2, ALU.max, ALU.min))
                link(nc.vector.tensor_scalar(slope[:, :], eps[:, :], -5.0, 1.0, ALU.mult, ALU.add))
                dve.wait_ge(exps, 2)
                link(nc.vector.tensor_scalar(beta[:, :, :], beta[:, :, :], 1.0, None, ALU.add))
                link(nc.vector.reciprocal(beta[:, :, :], beta[:, :, :]))
                dve.wait_ge(exps, 3)
                link(nc.vector.tensor_reduce(mx[:, :], lgf, AX.X, ALU.add))
                link(nc.vector.reciprocal(mx[:, :], mx[:, :]))
                link(nc.vector.tensor_tensor(lgf, lgf, bcast(mx[:, :], 5), ALU.mult))
                link(nc.vector.tensor_tensor(lg[:, :, :, :], lg[:, :, :, :], bcast(bcast_mid(slope[:, :], NT), 5), ALU.mult))
                link(nc.vector.tensor_tensor(pw[:, :, :, :].rearrange("p h f t -> p t h f"), lg[:, :, :, :],
                                             bcast(bcast_mid(eps[:, :], NT), 5), ALU.add))
                link(nc.vector.reciprocal(half[:, :, :], ssk[:, :, :]))
                link(nc.vector.tensor_tensor(half[:, :, :], half[:, :, :], beta[:, :, :], ALU.mult))
                link(nc.vector.tensor_copy(gam[:, :, :, :], streams(half[:, :, :])))
                flat_gam = gam[:, :, :, :].rearrange("p t r s -> p (t r s)")
                link(nc.vector.tensor_tensor(blocks, blocks, bcast(flat_gam, CH), ALU.mult))
                nc.vector.tensor_tensor(blocks, blocks, bcast_mid(const[:, C_DIAG:C_DIAG + CH], GRP),
                                        ALU.mult).then_inc(diag_scaled, 1)
                dve.wait_ge(roots, 1)
                link(nc.vector.reciprocal(rq[:, :, :], rq[:, :, :]))
                nc.vector.tensor_tensor(scales[:, 1, :, :].rearrange("p t (b h) -> p (t b) h", b=BATCH), rq[:, :, :],
                                        pw[:, :, 3, :].rearrange("p h t -> p t h"), ALU.mult)
                flat = inv[:, :, :, :].rearrange("p s c i -> p s (c i)")
                link(nc.vector.memset(flat[:, :, 0:CH * CH:CH + 1], 1.0))
                dve.wait_ge(tri_in, 16 * SLOTS)
                for i in range(1, CH):
                    pr = prod[:, 0:SLOTS * i * i].rearrange("p (s c j) -> p s c j", s=SLOTS, c=i)
                    a = tri[:, :, i, 0:i]
                    a = bass.AP(tensor=a.tensor, offset=a.offset, ap=[a.ap[0], a.ap[1], [0, i], a.ap[2]])
                    link(nc.vector.tensor_tensor(pr, inv[:, :, 0:i, 0:i], a, ALU.mult))
                    link(nc.vector.tensor_reduce(inv[:, :, 0:i, i:i + 1].rearrange("p s c o -> p s (c o)"), pr, AX.X, ALU.add))
                dve.wait_ge(gam_turned, 1)
                for g in range(GRP // P):
                    part = inv[:, g:SLOTS:GRP // P, :, :]
                    nc.vector.tensor_tensor(part, part, bcast(gamT[:, g, :].rearrange("p (q c) -> p q c", q=NQ), CH),
                                            ALU.mult).then_inc(inv_done, 1)

            @block.gpsimd
            def _(pool):
                nc.gpsimd.tensor_tensor(prod[:, :].rearrange("p (g j) -> p g j", j=CH), blocks,
                                        bcast_mid(const[:, C_ONE:C_ONE + CH], GRP), ALU.mult).then_inc(diag_picked, 1)

            @block.tensor
            def _(pe):
                pe.wait_ge(diag_scaled, 1)
                for g in range(GRP // P):
                    last = nc.tensor.transpose(gamT[:, g, :], gam[:, :, :, :].rearrange("p t r s -> p (t r s)")[:, g * P:g * P + P],
                                               const[:, C_ID:C_ID + P])
                last.then_inc(gam_turned, 1)


def fir(nc, sems, io, keep):
    st = Stage(nc, sems)
    with st.ctx:
        win = [st.sb(f"win{i}", [P, BATCH, 2 * STEPS, DK]) for i in range(2)]
        toe = [st.sb(f"toe{i}", [P, FCH, NF, WIN]) for i in range(2)]
        mixed = [st.sb(f"mixed{i}", [P, STEPS * BATCH, DK]) for i in range(2)]
        part = [[st.sb(f"part{i}{f}", [P, FCH, STEPS * BATCH]) for f in range(NF)] for i in range(2)]
        two = [st.sb(f"two{i}", [P, FCH, STEPS * BATCH]) for i in range(2)]
        conv = [[st.ps(f"conv{i}{f}", [P, FCH, STEPS * BATCH]) for f in range(NF)] for i in range(2)]
        pw = keep["pw"]
        NT = STEPS * BATCH
        NG = DK // FCH

        win_in, toe_in = st.pair("p3_win_in"), st.pair("p3_toe_in")
        conv_ready, scaled = st.sem("p3_conv_ready"), st.sem("p3_scaled")
        two_done, mixed_done = st.sem("p3_two_done"), st.sem("p3_mixed_done")
        mixed_stored = st.pair("p3_mixed_stored")

        with nc.Block() as block:
            @block.sync
            def _(sp):
                def windows(h):
                    for b in range(BATCH):
                        src = io["vr_s"]
                        sp.dma_start(win[h % 2][:, b, :, :],
                                     bass.AP(tensor=src.tensor, offset=(b * (SEQ + WIN) + SEQ - WIN) * D + h * DK,
                                             ap=[[D, P], [-WIN * D, 2 * STEPS], [1, DK]])).then_inc(win_in[h % 2], 16)

                def store(h):
                    sp.wait_ge(mixed_done, (h + 1) * NG + 2)
                    for b in range(BATCH):
                        sp.dma_start(io["mix_s"][:, :, b, h * DK:h * DK + DK].rearrange("t p d -> p t d"),
                                     mixed[h % 2][:, b:NT:BATCH, :]).then_inc(mixed_stored[h % 2], 16)

                for h in range(HEADS):
                    if h >= 2:
                        sp.wait_ge(conv_ready, (h - 1) * NG)
                    windows(h)
                    for g in range(NG):
                        n = h * NG + g
                        if n >= 2:
                            sp.wait_ge(conv_ready, n - 1)
                        src = io["firp"]
                        sp.dma_start(toe[n % 2][:, :, :, :].rearrange("p c f m -> p (c f) m"),
                                     bass.AP(tensor=src.tensor, offset=(h * DK + g * FCH) * NF * FIRPAD,
                                             ap=[[1, P], [FIRPAD, FCH * NF], [1, WIN]])).then_inc(toe_in[n % 2], 16)
                    if h >= 1:
                        store(h - 1)
                store(HEADS - 1)
                for i in range(2):
                    sp.wait_ge(mixed_stored[i], 16 * BATCH * (HEADS // 2 + 1))

            @block.tensor
            def _(pe):
                with pe.Fori(0, HEADS // 2) as i:
                    for hp in range(2):
                        pe.wait_ge(win_in[hp], i * (16 * BATCH) + 16 * BATCH)
                        for g in range(NG):
                            n = (i * 2 + hp) * NG + g
                            pe.wait_ge(toe_in[g % 2], (i * 2 + hp) * (8 * NG) + (g // 2) * 16 + 16)
                            pe.wait_ge(scaled, n + 1)
                            for c in range(FCH):
                                w = win[hp][:, :, :, g * FCH + c].rearrange("p b (t e) -> p e t b", e=2)
                                for f in range(NF):
                                    for e in range(2):
                                        last = nc.tensor.matmul(conv[g % 2][f][WIN * e:WIN * e + WIN, c, :],
                                                                toe[g % 2][:, c, f, :], w[:, e, :, :],
                                                                start=True, stop=True)
                            last.then_inc(conv_ready, 1)

            @block.vector
            def _(dve):
                dve.sem_inc(scaled, 2)
                dve.sem_inc(mixed_done, 2)
                for p in range(2):
                    dve.sem_inc(mixed_stored[p], 16 * BATCH)
                with dve.Fori(0, HEADS // 2) as i:
                    for hp in range(2):
                        h = i * 2 + hp
                        for g in range(NG):
                            n = h * NG + g
                            dve.wait_ge(conv_ready, n + 1)
                            for f in range(NF):
                                last = nc.vector.tensor_tensor(
                                    part[g % 2][f][:, :, :], conv[g % 2][f][:, :, :],
                                    bcast_mid(pw[:, bass.ds(h, 1), f, :].rearrange("p o t -> p (o t)"), FCH), ALU.mult)
                            last.then_inc(scaled, 1)
                            dve.wait_ge(scaled, n + 3)
                            dve.wait_ge(two_done, n + 1)
                            if g == 0:
                                dve.wait_ge(mixed_stored[hp], i * (16 * BATCH) + 16 * BATCH)
                            nc.vector.tensor_tensor(
                                mixed[hp][:, :, g * FCH:g * FCH + FCH].rearrange("p t c -> p c t"),
                                two[g % 2][:, :, :], part[g % 2][2][:, :, :], ALU.add).then_inc(mixed_done, 1)

            @block.gpsimd
            def _(pool):
                with pool.Fori(0, HEADS // 2) as i:
                    for hp in range(2):
                        h = i * 2 + hp
                        for g in range(NG):
                            n = h * NG + g
                            pool.wait_ge(scaled, n + 3)
                            pool.wait_ge(mixed_done, n + 1)
                            nc.gpsimd.tensor_tensor(two[g % 2][:, :, :], part[g % 2][0][:, :, :], part[g % 2][1][:, :, :],
                                                    ALU.add).then_inc(two_done, 1)


def delta(nc, sems, io, keep):
    st = Stage(nc, sems)
    with st.ctx:
        wo = st.sb("wo", [P, KT, D])
        wo_raw = st.sb("wo_raw", [P, KT, D])
        norm_w = st.sb("norm_w", [P, 1])
        power = st.sb("power", [P, NS])
        head_eps = st.sb("head_eps", [P, NS])
        ln_eps = st.sb("ln_eps", [P, BATCH])
        qk = [st.sb(f"qk{i}", [P, 2 * KT, TOK]) for i in range(2)]
        ktok = [st.sb(f"kt{i}", [P, BATCH, D]) for i in range(2)]
        vtok = [st.sb(f"vt{i}", [P, BATCH, D]) for i in range(2)]
        xres = [st.sb(f"xres{i}", [P, BATCH, D]) for i in range(2)]
        mix = [st.sb(f"mix{i}", [P, BATCH, D]) for i in range(2)]
        ddiag = [st.sb(f"ddiag{i}", [P, NS, P]) for i in range(2)]
        tdiag = [st.sb(f"tdiag{i}", [P, NS, P]) for i in range(2)]
        lt = st.sb("lt", [P, NS, P])
        nmat = st.sb("nmat", [P, NS, P])
        r1 = st.sb("r1", [P, NS, P])
        r2 = st.sb("r2", [P, NS, P])
        tt = [st.sb(f"tt{i}", [P, NS, P]) for i in range(2)]
        att = [st.sb(f"att{i}", [P, NS, P]) for i in range(2)]
        v2 = [st.sb(f"v2{i}", [P, NS, DK]) for i in range(2)]
        x0 = st.sb("x0", [P, BH, 2, DK])
        us = st.sb("us", [P, BH, 2, DK])
        S = st.sb("S", [P, BH, 2, DK])
        o = st.sb("o", [P, BH, 2, DK])
        osq = st.sb("osq", [P, BH, 2, DK])
        ss = st.sb("ss", [P, NS])
        oT = st.sb("oT", [P, KT, TOK])
        y = [st.sb(f"y{i}", [P, BATCH, D]) for i in range(2)]
        stats = st.sb("stats", [P, BATCH, 6])
        mv = st.sb("mv", [P, BATCH, 2])
        rstd = st.sb("rstd", [P, BATCH])
        R = [st.ps(f"R{i}", [P, 4, P]) for i in range(4)]
        X = [st.ps(f"X{i}", [P, BH // 2, 2, DK]) for i in range(2)]
        Y = [st.ps(f"Y{i}", [P, BH // 2, 2, DK]) for i in range(2)]
        SI = Y[0][:, :, :, :].rearrange("p s r d -> p (s r) d")
        const, scales = keep["const"], keep["scales"]
        ident = const[:, C_ID:C_ID + P]
        off_mask, att_mask = const[:, C_OFF:C_OFF + P], const[:, C_ATT:C_ATT + P]

        def rounds(pre, tail):
            k, n, q, a, b, c = ([(kind, g, "act" if kind == "N" else "dve") for g in range(4)] for kind in "KNQABC")
            t, w = ([(kind, g, "act" if kind == "T" else "dve") for g in range(2)] for kind in "TW")
            return (k if pre else []) + (t if tail else []) + (n if pre else []) + (w if tail else []) + (q + a + b + c if pre else [])

        PRE, FULL, LAST = rounds(True, False), rounds(True, True), rounds(False, True)

        def used(seq, engine, n=None):
            return sum(e == engine for _, _, e in seq[:n])

        power_set, par_in, wo_done, s_zero, d_zero = (st.sem(f"p4_{n}") for n in ("power_set", "par_in", "wo_done", "s_zero", "d_zero"))
        qk_in, kt_in, vt_in, x_in, mix_in, d_in = (st.pair(f"p4_{n}_in") for n in ("qk", "kt", "vt", "x", "mix", "d"))
        round_ready, dve_out, act_out = st.sem("p4_round_ready"), st.sem("p4_dve_out"), st.sem("p4_act_out")
        x_ready, x_done, y_ready, u_done = (st.sem(f"p4_{n}") for n in ("x_ready", "x_done", "y_ready", "u_done"))
        o_ready, s_ready, s_done, o_done = (st.sem(f"p4_{n}") for n in ("o_ready", "s_ready", "s_done", "o_done"))
        v2_done, direct_done, prep_done = st.sem("p4_v2_done"), st.sem("p4_direct_done"), st.sem("p4_prep_done")
        mixed, sq_done, ss_done, rs_done, on_done, st_done, pool_link = (
            st.sem(f"p4_{n}") for n in ("mixed", "sq_done", "ss_done", "rs_done", "on_done", "st_done", "pool_link"))
        y_done, var_done, rstd_done, x1_done = (st.sem(f"p4_{n}") for n in ("y_done", "var_done", "rstd_done", "x1_done"))
        x1_stored = st.pair("p4_x1_stored")
        NPRE, NFULL = len(PRE), len(FULL)
        MID = STEPS - 2

        def base(t, seq_count):
            pre, full = seq_count(PRE), seq_count(FULL)
            return (t - 1) * full + 2 * pre if isinstance(t, int) else t * full + (2 * pre - full)

        def dve_base(t):
            return base(t, lambda s: used(s, "dve"))

        def act_base(t):
            return base(t, lambda s: used(s, "act"))

        with nc.Block() as block:
            @block.sync
            def _(sp):
                sp.dma_start(wo_raw[:, :, :], io["w_o"]).then_inc(par_in, 16)
                sp.dma_start(norm_w[:, :], io["norm_w"]).then_inc(par_in, 16)

                def load(t, p):
                    sp.dma_start(qk[p][:, :, :], row(io["qk_s"], t)).then_inc(qk_in[p], 16)
                    for q in range(NQ):
                        part = slice(q * CH, q * CH + CH)
                        sp.dma_start(ddiag[p][part, :, part], io["d_s"][part, bass.ds(t * NS, NS), :]).then_inc(d_in[p], 16)
                        sp.dma_start(tdiag[p][part, :, part], io["t_s"][part, bass.ds(t * NS, NS), :]).then_inc(d_in[p], 16)
                    sp.dma_start(vtok[p][:, :, :], io["v_s"][:, bass.ds(t * P, P), :].rearrange("b p d -> p b d")).then_inc(vt_in[p], 16)
                    sp.dma_start(ktok[p][:, :, :], row(io["k_s"], t)).then_inc(kt_in[p], 16)

                def load_mix(t, p):
                    sp.dma_start(mix[p][:, :, :], row(io["mix_s"], t)).then_inc(mix_in[p], 16)

                def load_x(t, p):
                    sp.dma_start(xres[p][:, :, :], io["x"][:, bass.ds(t * P, P), :].rearrange("b p d -> p b d")).then_inc(x_in[p], 16)

                def next_loads(t, p):
                    sp.wait_ge(s_ready, t + 1)
                    load(t + 2, p)
                    sp.wait_ge(mixed, t + 1)
                    load_mix(t + 2, p)

                def store(t, p):
                    sp.wait_ge(x1_done, t + 1)
                    sp.dma_start(row(io["x1_s"], t), y[p][:, :, :]).then_inc(x1_stored[p], 16)

                sp.wait_ge(d_zero, 4)
                for t in range(2):
                    load(t, t)
                    load_mix(t, t)
                    load_x(t, t)
                next_loads(0, 0)
                with sp.Fori(0, MID // 2 - 1) as i:
                    for j in range(2):
                        t = i * 2 + 1 + j
                        next_loads(t, 1 - j)
                        store(t - 1, j)
                        load_x(t + 1, j)
                t = MID - 1
                next_loads(t, 1)
                for t in range(MID - 1, MID + 1):
                    store(t - 1, (t - 1) % 2)
                    load_x(t + 1, (t + 1) % 2)
                for t in range(STEPS - 2, STEPS):
                    store(t, t % 2)
                for p in range(2):
                    sp.wait_ge(x1_stored[p], 8 * STEPS + 16)

            @block.tensor
            def _(pe):
                def bank_free(seq, r, dve0, act0):
                    if r >= 4:
                        before, engine = seq[:r - 3], seq[r - 4][2]
                        pe.wait_ge(dve_out if engine == "dve" else act_out, (dve0 if engine == "dve" else act0) + used(before, engine))
                    elif not isinstance(dve0, int) or dve0:
                        pe.wait_ge(dve_out, dve0 - 3 + r)

                def empties(seq, kind, g):
                    r = next(i for i, x in enumerate(seq) if x[:2] == (kind, g))
                    return used(seq, seq[r][2], r + 1)

                def run(kinds, seq, t, p, n, tp, dve0, act0):
                    for r, (kind, g, _) in enumerate(seq):
                        if kind not in kinds:
                            continue
                        bank = R[r % 4]
                        if g == 0:
                            if kind == "K":
                                pe.wait_ge(qk_in[p], n * 16 + 16)
                            if kind == "N":
                                pe.wait_ge(d_in[p], n * (32 * NQ) + 32 * NQ)
                            if kind == "T":
                                pe.wait_ge(on_done, tp + 1)
                        before = {"N": "K", "A": "N", "B": "A", "C": "B", "W": "T"}.get(kind)
                        if before:
                            for h in [g] if kind != "W" else ([1] if g == 0 else []):
                                engine = seq[next(i for i, x in enumerate(seq) if x[:2] == (before, h))][2]
                                pe.wait_ge(dve_out if engine == "dve" else act_out,
                                           (dve0 if engine == "dve" else act0) + empties(seq, before, h))
                        bank_free(seq, r, dve0, act0)
                        par, half = g // 2, g % 2
                        if kind in "KNQABC":
                            for j in range(4):
                                s = half * 4 + j
                                b, hh = s // KT, s % KT
                                c = par * BH + s
                                if kind in "KQ":
                                    rows = slice(64 * par, 64 * par + DK)
                                    left = qk[p][rows, KT + hh, b * P:b * P + P]
                                    right = qk[p][rows, (KT if kind == "K" else 0) + hh, b * P:b * P + P]
                                else:
                                    left = (lt if kind == "N" else nmat)[:, c, :]
                                    right = {"N": ddiag[p], "A": tdiag[p], "B": r1, "C": r2}[kind][:, c, :]
                                last = nc.tensor.matmul(bank[:, j, :], left, right, start=True, stop=True)
                        elif kind == "T":
                            for b in range(BATCH):
                                last = nc.tensor.transpose(bank[:, b, :], o[:, b * KT + g, :, :].rearrange("p r d -> p (r d)"), ident)
                        else:
                            for j in range(2):
                                b = 2 * g + j
                                for hh in range(KT):
                                    last = nc.tensor.matmul(bank[:, 2 * j:2 * j + 2, :], oT[:, hh, b * P:b * P + P], wo[:, hh, :],
                                                            start=(hh == 0), stop=(hh == KT - 1))
                        last.then_inc(round_ready, 1)

                def from_state(t, p):
                    pe.wait_ge(s_done, t * 2 + 2)
                    pe.wait_ge(o_done, t * 2 + 2)
                    for s in range(BH):
                        b, hh = s // KT, s % KT
                        last = nc.tensor.matmul(X[s // 4][:, s % 4, :, :], qk[p][:, KT + hh, b * P:b * P + P],
                                                S[:, s, :, :], start=True, stop=True)
                        if s % 4 == 3:
                            last.then_inc(x_ready, 1)

                def solve(t, p):
                    for i in range(2):
                        pe.wait_ge(x_done, t * 2 + i + 1)
                        for s in range(4 * i, 4 * i + 4):
                            for par in range(2):
                                last = nc.tensor.matmul(Y[i][:, s % 4, par, :], tt[p][:, par * BH + s, :], x0[:, s, par, :],
                                                        start=True, stop=True)
                        last.then_inc(y_ready, 1)

                def outputs(t, p, n):
                    pe.wait_ge(u_done, t * 2 + 2)
                    for s in range(BH):
                        b, hh = s // KT, s % KT
                        nc.tensor.matmul(X[s // 4][:, s % 4, :, :], qk[p][:, hh, b * P:b * P + P], S[:, s, :, :],
                                         start=True, stop=False)
                        for par in range(2):
                            last = nc.tensor.matmul(X[s // 4][:, s % 4, par, :], att[p][:, par * BH + s, :], us[:, s, par, :],
                                                    start=False, stop=(par == 1))
                        if s % 4 == 3:
                            last.then_inc(o_ready, 1)
                    pe.wait_ge(kt_in[p], n * 16 + 16)
                    for s in range(BH):
                        b, hh = s // KT, s % KT
                        for par in range(2):
                            c = hh * P + par * DK
                            last = nc.tensor.matmul(SI[64 * par:64 * par + DK, s, :], ktok[p][:, b, c:c + DK],
                                                    us[:, s, par, :], start=True, stop=True)
                    last.then_inc(s_ready, 1)

                pe.wait_ge(s_zero, 1)
                pe.wait_ge(wo_done, 1)

                def step(t, p, n, nn, seq, dve0, act0, last_c):
                    rest = (seq, t + 1, 1 - p, nn, t - 1, dve0, act0)
                    from_state(t, p)
                    run("K", *rest)
                    run("T", *rest)
                    pe.wait_ge(dve_out, last_c)
                    solve(t, p)
                    run("N", *rest)
                    run("W", *rest)
                    outputs(t, p, n)
                    run("QABC", *rest)

                run("KNQABC", PRE, 0, 0, 0, 0, 0, 0)
                d, a = used(PRE, "dve"), used(PRE, "act")
                step(0, 0, 0, 0, PRE, d, a, d)
                with pe.Fori(0, MID // 2) as i:
                    for j in range(2):
                        t = i * 2 + 1 + j
                        step(t, 1 - j, i + j, i + 1, FULL, dve_base(t), act_base(t), dve_base(t))
                t = STEPS - 1
                step(t, 1, t // 2, 0, LAST, dve_base(t), act_base(t), dve_base(t))
                d, a = dve_base(t) + used(LAST, "dve"), act_base(t) + used(LAST, "act")
                pe.wait_ge(dve_out, d)
                pe.wait_ge(act_out, a)
                pe.wait_ge(on_done, STEPS)
                for g in range(2):
                    for b in range(BATCH):
                        last = nc.tensor.transpose(R[g][:, b, :], o[:, b * KT + g, :, :].rearrange("p r d -> p (r d)"), ident)
                    last.then_inc(round_ready, 1)
                pe.wait_ge(act_out, a + 2)
                for g in range(2):
                    for j in range(2):
                        b = 2 * g + j
                        for hh in range(KT):
                            last = nc.tensor.matmul(R[2 + g][:, 2 * j:2 * j + 2, :], oT[:, hh, b * P:b * P + P], wo[:, hh, :],
                                                    start=(hh == 0), stop=(hh == KT - 1))
                    last.then_inc(round_ready, 1)

            def arrived(eng, seq, kind, g, round0):
                r = next(i for i, x in enumerate(seq) if x[:2] == (kind, g))
                eng.wait_ge(round_ready, round0 + r + 1)
                return R[r % 4]

            def round_base(t):
                return base(t, len)

            @block.scalar
            def _(act):
                def copy_rounds(kind, seq, round0):
                    for g in range(4 if kind == "N" else 2):
                        bank = arrived(act, seq, kind, g, round0)
                        c = g * 4
                        dst = nmat[:, c:c + 4, :] if kind == "N" else oT[:, g, :].rearrange("p (b n) -> p b n", b=BATCH)
                        nc.scalar.activation(dst, bank[:, :, :], ACT.Copy).then_inc(act_out, 1)

                def step(t, seq, round0, pre, tail):
                    if tail:
                        copy_rounds("T", seq, round0)
                    for i in range(2):
                        act.wait_ge(y_ready, t * 2 + i + 1)
                        nc.scalar.activation(us[:, 4 * i:4 * i + 4, :, :], Y[i][:, :, :, :], ACT.Copy).then_inc(u_done, 1)
                    if pre:
                        copy_rounds("N", seq, round0)
                    act.wait_ge(mixed, t + 1)
                    nc.scalar.activation(osq[:, :, :, :], o[:, :, :, :], ACT.Square).then_inc(sq_done, 1)

                copy_rounds("N", PRE, 0)
                step(0, PRE, NPRE, True, False)
                with act.Fori(0, MID) as i:
                    step(i + 1, FULL, round_base(i + 1), True, True)
                t = STEPS - 1
                step(t, LAST, round_base(t), False, True)
                copy_rounds("T", LAST, round_base(t) + len(LAST))

            @block.vector
            def _(dve):
                nc.vector.memset(S[:, :, :, :], 0.0).then_inc(s_zero, 1)
                dve.wait_ge(par_in, 32)
                nc.vector.tensor_scalar(wo[:, :, :], wo_raw[:, :, :], norm_w[:, 0:1], None, ALU.mult).then_inc(wo_done, 1)
                dve.sem_inc(s_done, 2)
                dve.sem_inc(o_done, 2)
                for p in range(2):
                    dve.sem_inc(x1_stored[p], 16)

                def evacuate(kind, seq, round0, p):
                    for g in range(4):
                        bank = arrived(dve, seq, kind, g, round0)
                        c = slice(g * 4, g * 4 + 4)
                        if kind in "KQ":
                            last = nc.vector.tensor_tensor((lt if kind == "K" else att[p])[:, c, :], bank[:, :, :],
                                                           bcast_mid(off_mask if kind == "K" else att_mask, 4), ALU.mult)
                        else:
                            dst = {"A": r1, "B": r2, "C": tt[p]}[kind]
                            last = nc.vector.tensor_tensor(dst[:, c, :], tdiag[p][:, c, :], bank[:, :, :], ALU.subtract)
                        last.then_inc(dve_out, 1)

                def right_side(t, p):
                    dve.wait_ge(prep_done, t + 1)
                    for i in range(2):
                        dve.wait_ge(x_ready, t * 2 + i + 1)
                        nc.vector.tensor_tensor(x0[:, 4 * i:4 * i + 4, :, :].rearrange("p s r d -> p (s r) d"), v2[p][:, 8 * i:8 * i + 8, :],
                                                X[i][:, :, :, :].rearrange("p s r d -> p (s r) d"), ALU.subtract).then_inc(x_done, 1)

                def outputs(t, p):
                    for i in range(2):
                        dve.wait_ge(o_ready, t * 2 + i + 1)
                        c3 = scales[:, 1, bass.ds(t, 1), 8 * i:8 * i + 8].rearrange("p o s -> p (o s)")
                        nc.vector.tensor_tensor(o[:, 4 * i:4 * i + 4, :, :].rearrange("p s r d -> p (s r) d"),
                                                X[i][:, :, :, :].rearrange("p s r d -> p (s r) d"), bcast(c3, DK), ALU.mult).then_inc(o_done, 1)
                    dve.wait_ge(s_ready, t + 1)
                    for par in range(2):
                        rows = slice(64 * par, 64 * par + DK)
                        nc.vector.tensor_tensor(S[rows, :, par, :], S[rows, :, par, :], SI[rows, :, :], ALU.add).then_inc(s_done, 1)
                    dve.wait_ge(o_done, t * 2 + 4)
                    of = o[:, :, :, :].rearrange("p s r d -> p (s r d)")
                    nc.vector.tensor_tensor(of, of, mix[p][:, :, :].rearrange("p b d -> p (b d)"), ALU.add).then_inc(mixed, 1)

                def head_sums(t):
                    dve.wait_ge(sq_done, t + 1)
                    nc.vector.tensor_reduce(ss[:, :], osq[:, :, :, :].rearrange("p s r d -> p (s r) d"), AX.X,
                                            ALU.add).then_inc(ss_done, 1)

                def head_norm(t):
                    dve.wait_ge(rs_done, t + 1)
                    of = o[:, :, :, :].rearrange("p s r d -> p (s r) d")
                    nc.vector.scalar_tensor_tensor(out=of, in0=of, scalar=float(DK) ** 0.5, in1=bcast(ss[:, :], DK),
                                                   op0=ALU.mult, op1=ALU.mult).then_inc(on_done, 1)

                def residual(t, p, n, seq, round0):
                    dve.wait_ge(x_in[p], n * 16 + 16)
                    dve.wait_ge(x1_stored[p], n * 16 + 16)
                    for g in range(2):
                        bank = arrived(dve, seq, "W", g, round0)
                        nc.vector.tensor_tensor(y[p][:, 2 * g:2 * g + 2, :], bank[:, :, :].rearrange("p (b k) d -> p b (k d)", b=2),
                                                xres[p][:, 2 * g:2 * g + 2, :], ALU.add).then_inc(dve_out, 1)

                def spread(t, p, out0):
                    dve.wait_ge(dve_out, out0)
                    for b in range(BATCH):
                        last = nc.vector.bn_stats(stats[:, b, :], y[p][:, b, :])
                    last.then_inc(st_done, 1)

                def spread_sum(t):
                    dve.wait_ge(par_in, 32)
                    dve.wait_ge(st_done, t + 1)
                    for b in range(BATCH):
                        last = nc.vector.bn_aggr(mv[:, b, :], stats[:, b, :])
                    last.then_inc(var_done, 1)

                def layer_norm(t, p):
                    dve.wait_ge(rstd_done, t + 1)
                    for b in range(BATCH):
                        last = nc.vector.tensor_scalar(y[p][:, b, :], y[p][:, b, :], mv[:, b, 0:1], rstd[:, b:b + 1],
                                                       ALU.subtract, ALU.mult)
                    last.then_inc(x1_done, 1)

                def step(t, p, ntail, seq, round0, dve0, pre, tail):
                    right_side(t, p)
                    if pre:
                        evacuate("K", seq, round0, 1 - p)
                    if tail:
                        residual(t - 1, 1 - p, ntail, seq, round0)
                    outputs(t, p)
                    if pre:
                        evacuate("Q", seq, round0, 1 - p)
                    head_sums(t)
                    if tail:
                        spread(t - 1, 1 - p, dve0 + used(seq, "dve", 1 + next(i for i, x in enumerate(seq) if x[:2] == ("W", 1))))
                    if pre:
                        evacuate("A", seq, round0, 1 - p)
                    if tail:
                        spread_sum(t - 1)
                    if pre:
                        evacuate("B", seq, round0, 1 - p)
                    head_norm(t)
                    if tail:
                        layer_norm(t - 1, 1 - p)
                    if pre:
                        evacuate("C", seq, round0, 1 - p)

                for kind in "KQABC":
                    evacuate(kind, PRE, 0, 0)
                step(0, 0, 0, PRE, NPRE, used(PRE, "dve"), True, False)
                with dve.Fori(0, MID // 2) as i:
                    for j in range(2):
                        t = i * 2 + 1 + j
                        step(t, 1 - j, i, FULL, round_base(t), dve_base(t), True, True)
                t = STEPS - 1
                step(t, 1, (t - 1) // 2, LAST, round_base(t), dve_base(t), False, True)
                residual(t, 1, t // 2, LAST, round_base(t) + len(LAST))
                spread(t, 1, dve_base(t) + 2 * used(LAST, "dve"))
                spread_sum(t)
                layer_norm(t, 1)

            @block.gpsimd
            def _(pool):
                for p in range(2):
                    for buf in (ddiag[p], tdiag[p]):
                        nc.gpsimd.memset(buf[:, :, :], 0.0).then_inc(d_zero, 1)
                nc.gpsimd.memset(head_eps[:, :], DK * LN_EPS)
                nc.gpsimd.memset(ln_eps[:, :], LN_EPS)
                nc.gpsimd.memset(power[:, :], -0.5).then_inc(power_set, 1)
                pool.wait_ge(power_set, 1)

                def prep(t, p, n):
                    pool.wait_ge(vt_in[p], n * 16 + 16)
                    sk = scales[:, 0, bass.ds(t, 1), :].rearrange("p o s -> p (o s)")
                    by_head = vtok[p][:, :, :].rearrange("p b (h d) -> p (b h) d", h=HEADS)
                    nc.gpsimd.tensor_tensor(v2[p][:, :, :], by_head, bcast(sk, DK), ALU.mult).then_inc(v2_done, 1)
                    dir_ = vtok[p][:, :, :].rearrange("p b (h d) -> p b h d", h=HEADS)
                    p4 = keep["pw"][:, :, 4, bass.ds(t * BATCH, BATCH)].rearrange("p h b -> p b h")
                    pool.wait_ge(v2_done, t + 1)
                    nc.gpsimd.tensor_tensor(dir_, dir_, bcast(p4, DK), ALU.mult).then_inc(direct_done, 1)
                    pool.wait_ge(mix_in[p], n * 16 + 16)
                    pool.wait_ge(direct_done, t + 1)
                    nc.gpsimd.tensor_tensor(mix[p][:, :, :], mix[p][:, :, :], vtok[p][:, :, :], ALU.add).then_inc(prep_done, 1)

                def norm(t, links):
                    pool.wait_ge(ss_done, t + 1)
                    nc.gpsimd.tensor_tensor(ss[:, :], ss[:, :], head_eps[:, :], ALU.add).then_inc(pool_link, 1)
                    pool.wait_ge(pool_link, links)
                    nc.gpsimd.tensor_tensor(ss[:, :], ss[:, :], power[:, :], ALU.pow).then_inc(rs_done, 1)

                def tail(t, links):
                    pool.wait_ge(var_done, t + 1)
                    nc.gpsimd.tensor_tensor(rstd[:, :], mv[:, :, 1:2].rearrange("p b o -> p (b o)"), ln_eps[:, :],
                                            ALU.add).then_inc(pool_link, 1)
                    pool.wait_ge(pool_link, links)
                    nc.gpsimd.tensor_tensor(rstd[:, :], rstd[:, :], power[:, 0:BATCH], ALU.pow).then_inc(rstd_done, 1)

                prep(0, 0, 0)
                prep(1, 1, 0)
                norm(0, 1)
                with pool.Fori(0, MID // 2) as i:
                    for j in range(2):
                        t = i * 2 + 1 + j
                        pool.wait_ge(x_done, t * 2)
                        prep(t + 1, j, i + 1)
                        norm(t, t * 2)
                        tail(t - 1, t * 2 + 1)
                t = STEPS - 1
                norm(t, t * 2)
                tail(t - 1, t * 2 + 1)
                tail(t, t * 2 + 2)


def round_weights(nc, sems, io, wr, flag, total):
    st = Stage(nc, sems)
    with st.ctx:
        CW = 2048
        NCH = W_END // CW
        raw = [st.sb(f"wraw{i}", [P, CW]) for i in range(2)]
        diff = st.sb("wdiff", [P, CW])
        worst = st.sb("worst", [P, NCH])
        most = st.sb("most", [P, 1])
        ones = st.sb("ones", [P, 1])
        raw_in = st.pair("p5_raw_in")
        rounded, diff_done, worst_done, most_done, total_ready, flag_done, flag_stored = (
            st.sem(f"p5_{n}") for n in ("rounded", "diff_done", "worst_done", "most_done", "total_ready", "flag_done", "flag_stored"))

        with nc.Block() as block:
            @block.sync
            def _(sp):
                for c in range(NCH):
                    if c >= 2:
                        sp.wait_ge(diff_done, c - 1)
                    sp.dma_start(raw[c % 2][:, :], io["ffn_w"][:, c * CW:c * CW + CW]).then_inc(raw_in[c % 2], 16)
                sp.wait_ge(flag_done, 1)
                sp.dma_start(io["flag_s"], flag[:, :]).then_inc(flag_stored, 16)
                sp.wait_ge(flag_stored, 16)

            @block.vector
            def _(dve):
                nc.vector.memset(ones[:, :], 1.0)
                for c in range(NCH):
                    dve.wait_ge(raw_in[c % 2], 16 * (c // 2) + 16)
                    nc.vector.tensor_copy(wr[:, c * CW:c * CW + CW], raw[c % 2][:, :]).then_inc(rounded, 1)
                    dve.wait_ge(rounded, c + 1)
                    if c:
                        dve.wait_ge(worst_done, c)
                    nc.vector.tensor_tensor(diff[:, :], raw[c % 2][:, :], wr[:, c * CW:c * CW + CW].bitcast(f32),
                                            ALU.subtract).then_inc(diff_done, 1)
                    dve.wait_ge(diff_done, c + 1)
                    nc.vector.tensor_reduce(worst[:, c:c + 1], diff[:, :], AX.X, ALU.max,
                                            apply_absolute_value=True).then_inc(worst_done, 1)
                dve.wait_ge(worst_done, NCH)
                nc.vector.tensor_reduce(most[:, :], worst[:, :], AX.X, ALU.max).then_inc(most_done, 1)

            @block.tensor
            def _(pe):
                pe.wait_ge(most_done, 1)
                nc.tensor.matmul(total, most[:, :], ones[:, :], start=True, stop=True).then_inc(total_ready, 1)

            @block.scalar
            def _(act):
                act.wait_ge(total_ready, 1)
                nc.scalar.activation(flag[:, :], total, ACT.Copy).then_inc(flag_done, 1)


def ffn(nc, sems, io, keep):
    outer = Stage(nc, sems)
    with outer.ctx:
        flag = outer.sb("flag", [1, 1])
        scol = outer.sb("scol", [P, 4 * HT])
        srow = outer.sb("srow", [P, D])
        power = outer.sb("power5", [P, BATCH])
        ln_eps = outer.sb("ln_eps5", [P, BATCH])
        x1 = [outer.sb(f"x1{i}", [P, BATCH, D]) for i in range(2)]
        z = [outer.sb(f"z{i}", [P, BATCH, D]) for i in range(2)]
        gate = [outer.sb(f"gate{i}", [P, TOK]) for i in range(2)]
        stats = outer.sb("stats5", [P, BATCH, 6])
        mv = outer.sb("mv5", [P, BATCH, 2])
        rstd = outer.sb("rstd5", [P, BATCH])
        B = [outer.ps(f"B{i}", [P, TOK]) for i in range(4)]
        O = outer.ps("O", [P, BATCH, D])
        T = outer.ps("T", [P, KT, TOK])
        ident = keep["const"][:, C_ID:C_ID + P]
        fast = Stage(nc, sems)
        with fast.ctx:
            wr = fast.sb("wr", [P, W_END], f32r)
            round_weights(nc, sems, io, wr, flag, B[0][0:1, 0:1])
            xh, xl = fast.sb("xh", [P, KT, TOK], f32r), fast.sb("xl", [P, KT, TOK], f32r)
            sets = [[fast.sb(f"act{i}{n}", [P, HT, TOK], f32r) for n in "hl"] for i in range(2)]
            yb = [fast.sb(f"yb{i}", [P, TOK]) for i in range(3)]
        slow = Stage(nc, sems)
        with slow.ctx:
            wblk = [slow.sb(f"wblk{i}", [P, HT, P]) for i in range(2)]
            xf = slow.sb("xf", [P, KT, TOK])
            full = [slow.sb(f"full{i}", [P, HT, TOK]) for i in range(2)]

        par_in, power_set = outer.sem("p6_par_in"), outer.sem("p6_power_set")
        x_in, out_stored, w_in = outer.pair("p6_x_in"), outer.pair("p6_out_stored"), outer.pair("p6_w_in")
        (tr_ready, xh_done, x_split, bank_ready, gate_done, f_ready, hi_done, lo_done, o_ready, o_free, z_done,
         st_done, var_done, rs_link, rstd_done, out_done, blk_used) = (outer.sem(f"p6_{n}") for n in (
             "tr_ready", "xh_done", "x_split", "bank_ready", "gate_done", "f_ready", "hi_done", "lo_done", "o_ready",
             "o_free", "z_done", "st_done", "var_done", "rs_link", "rstd_done", "out_done", "blk_used"))
        BLOCKS = 3 * HT
        F0 = 4
        SLOTS_T = 4 * HT
        WBLOCKS = 3 * HT + KT

        def either(eng, emit):
            inexact = eng.value_load(io["flag_s"].bitcast(i32), min_val=0, max_val=2 ** 31 - 1)
            with eng.If(inexact != 0):
                emit(True)
            with eng.Else():
                emit(False)

        with nc.Block() as block:
            @block.sync
            def _(sp):
                sp.dma_start(scol[:, :], io["scol"]).then_inc(par_in, 16)
                src = io["srow"]
                sp.dma_start(srow[:, :], bass.AP(tensor=src.tensor, offset=0, ap=[[0, P], [1, D]])).then_inc(par_in, 16)

                def load(t, p):
                    sp.dma_start(x1[p][:, :, :], row(io["x1_s"], t)).then_inc(x_in[p], 16)

                def store(t, p):
                    sp.wait_ge(out_done, t + 1)
                    sp.dma_start(io["out"][:, bass.ds(t * P, P), :].rearrange("b p d -> p b d"), z[p][:, :, :]).then_inc(out_stored[p], 16)

                def stream(t):
                    w = io["ffn_w"]
                    for n in range(WBLOCKS):
                        sp.wait_ge(blk_used, t * WBLOCKS + n + 1)
                        if n < HT:
                            for j, base in enumerate((W1, W2)):
                                sp.dma_start(wblk[n % 2][:, j * KT:j * KT + KT, :],
                                             w[:, base:base + KT * HID].rearrange("p (k m) -> p k m", k=KT)[:, :, n * P:n * P + P]
                                             ).then_inc(w_in[n % 2], 16)
                        else:
                            base, width, m = ((H1, HID, n - HT) if n < 2 * HT else (H2, HID, n - 2 * HT) if n < 3 * HT
                                              else (W3, D, n - 3 * HT))
                            sp.dma_start(wblk[n % 2][:, :, :], w[:, base:base + HT * width].rearrange("p (k m) -> p k m", k=HT)[:, :, m * P:m * P + P]
                                         ).then_inc(w_in[n % 2], 16)

                def emit(general):
                    load(0, 0)
                    load(1, 1)
                    if general:
                        stream(0)
                    with sp.Fori(0, STEPS // 2 - 1) as i:
                        for p in range(2):
                            if general:
                                stream(i * 2 + p + 1)
                            store(i * 2 + p, p)
                            load(i * 2 + p + 2, p)
                    if general:
                        stream(STEPS - 1)
                    for p in range(2):
                        store(STEPS - 2 + p, p)

                either(sp, emit)
                for p in range(2):
                    sp.wait_ge(out_stored[p], 8 * STEPS + 16)

            @block.tensor
            def _(pe):
                def turn(p, n):
                    pe.wait_ge(x_in[p], n * 16 + 16)
                    for k in range(KT):
                        for b in range(BATCH):
                            last = nc.tensor.transpose(T[:, k, b * P:b * P + P], x1[p][:, b, k * P:k * P + P], ident)
                    last.then_inc(tr_ready, 1)

                def layers(t, general):
                    def weights_in(n):
                        per = HT + HT + KT // 2
                        before = n // 2 * 2 if n < HT else HT + (n - HT) // 2
                        pe.wait_ge(w_in[n % 2], t * (16 * per) + 16 * (before + (2 if n < HT else 1)))

                    def block_rhs(layer, k):
                        if layer == 0:
                            return [xf[:, k, :]] if general else [xh[:, k, :], xl[:, k, :]]
                        s = (layer - 1) % 2
                        return [full[s][:, k, :]] if general else [sets[s][0][:, k, :], sets[s][1][:, k, :]]

                    pe.wait_ge(x_split, t + 1)
                    for layer in range(3):
                        kts = HT if layer else KT
                        for m in range(HT):
                            n = layer * HT + m
                            if general:
                                weights_in(n)
                            for j in range(1 if layer else 2):
                                slot = 2 * m + j if layer == 0 else (layer + 1) * HT + m
                                if layer == 0:
                                    pe.wait_ge(f_ready, F0 + t * BLOCKS + (m - 1 if m >= 2 else 2 * m - 2))
                                elif layer == 1 and m == 0:
                                    pe.wait_ge(f_ready, F0 + t * BLOCKS + HT - 1)
                                elif m >= 4 or layer == 2:
                                    pe.wait_ge(f_ready, F0 + t * BLOCKS + n - 3)
                                base, width = ((W1, W2)[j], HID) if layer == 0 else ((H1, H2)[layer - 1], HID)
                                for k in range(kts):
                                    if layer and m == 0:
                                        pe.wait_ge(f_ready if general else lo_done, (F0 if general else 0) + t * BLOCKS + (layer - 1) * HT + k + 1)
                                    c = base + k * width + m * P
                                    w = wblk[n % 2][:, j * KT + k, :] if general else wr[:, c:c + P]
                                    parts = block_rhs(layer, k)
                                    for i, part in enumerate(parts):
                                        last = nc.tensor.matmul(B[slot % 4][:, :], w, part, start=(k == 0 and i == 0),
                                                                stop=(k == kts - 1 and i == len(parts) - 1))
                                last.then_inc(bank_ready, 1)
                            if general:
                                pe.drain().then_inc(blk_used, 1)

                def last_layer(t, general):
                    pe.wait_ge(o_free, t + 1)
                    if general:
                        pe.wait_ge(f_ready, F0 + t * BLOCKS + BLOCKS)
                        per = HT + HT + KT // 2
                        for half in range(KT):
                            n = 3 * HT + half
                            pe.wait_ge(w_in[n % 2], t * (16 * per) + 16 * (HT + (n - HT) // 2 + 1))
                            for b in range(BATCH):
                                for k in range(HT):
                                    last = nc.tensor.matmul(O[:, b, half * P:half * P + P], full[0][:, k, b * P:b * P + P],
                                                            wblk[n % 2][:, k, :], start=(k == 0), stop=(k == HT - 1))
                            pe.drain().then_inc(blk_used, 1)
                    else:
                        for first in range(2):
                            for k in range(HT):
                                if first == 0:
                                    pe.wait_ge(lo_done, t * BLOCKS + 2 * HT + k + 1)
                                for i in range(2):
                                    for b in (first, first + 2):
                                        last = nc.tensor.matmul(O[:, b, :], sets[0][i][:, k, b * P:b * P + P],
                                                                wr[:, W3 + k * D:W3 + k * D + D], start=(k == 0 and i == 0),
                                                                stop=(k == HT - 1 and i == 1))
                    last.then_inc(o_ready, 1) if not general else pe.drain().then_inc(o_ready, 1)

                def emit(general):
                    turn(0, 0)
                    with pe.Fori(0, STEPS // 2 - 1) as i:
                        for p in range(2):
                            layers(i * 2 + p, general)
                            turn(1 - p, i + p)
                            last_layer(i * 2 + p, general)
                    layers(STEPS - 2, general)
                    turn(1, STEPS // 2 - 1)
                    last_layer(STEPS - 2, general)
                    layers(STEPS - 1, general)
                    last_layer(STEPS - 1, general)

                either(pe, emit)

            @block.scalar
            def _(act):
                act.wait_ge(par_in, 32)

                def split(t, general):
                    act.wait_ge(tr_ready, t + 1)
                    nc.scalar.activation((xf if general else xh)[:, :, :], T[:, :, :], ACT.Copy).then_inc(x_split if general else xh_done, 1)

                def high(t, m):
                    act.wait_ge(f_ready, F0 + t * BLOCKS + m + 1)
                    nc.scalar.activation(sets[0][0][:, m, :], yb[m % 3][:, :], ACT.Copy).then_inc(hi_done, 1)

                def layers(t, general):
                    for m in range(HT):
                        act.wait_ge(bank_ready, t * SLOTS_T + 2 * m + 1)
                        act.wait_ge(f_ready, F0 + t * BLOCKS + (m - 1 if m >= 2 else 2 * m - 2))
                        nc.scalar.activation(gate[m % 2][:, :], B[2 * m % 4][:, :], ACT.Silu, scale=scol[:, m:m + 1]).then_inc(gate_done, 1)
                        if not general and m:
                            high(t, m - 1)
                    if not general:
                        high(t, HT - 1)
                    for layer in (1, 2):
                        for m in range(HT):
                            slot = (layer + 1) * HT + m
                            n = layer * HT + m
                            act.wait_ge(bank_ready, t * SLOTS_T + slot + 1)
                            if not general:
                                act.wait_ge(lo_done, t * BLOCKS + n - 2)
                            dst = full[layer % 2][:, m, :] if general else yb[n % 3][:, :]
                            last = nc.scalar.activation(dst, B[slot % 4][:, :], ACT.Gelu, scale=scol[:, slot:slot + 1])
                            if not general:
                                last = nc.scalar.activation(sets[layer % 2][0][:, m, :], B[slot % 4][:, :], ACT.Gelu,
                                                            scale=scol[:, slot:slot + 1])
                            last.then_inc(f_ready, 1)

                def emit(general):
                    split(0, general)
                    with act.Fori(0, STEPS - 1) as t:
                        layers(t, general)
                        split(t + 1, general)
                    layers(STEPS - 1, general)

                either(act, emit)

            @block.vector
            def _(dve):
                dve.wait_ge(par_in, 32)
                dve.sem_inc(f_ready, F0)
                dve.sem_inc(o_free, 1)
                dve.sem_inc(blk_used, 2)
                for p in range(2):
                    dve.sem_inc(out_stored[p], 16)

                def split(t):
                    dve.wait_ge(xh_done, t + 1)
                    nc.vector.tensor_tensor(xl[:, :, :], T[:, :, :], xh[:, :, :].bitcast(f32), ALU.subtract).then_inc(x_split, 1)

                def low(t, n, s, m):
                    if n < HT:
                        dve.wait_ge(hi_done, t * HT + n + 1)
                    else:
                        dve.wait_ge(f_ready, F0 + t * BLOCKS + n + 1)
                    nc.vector.tensor_tensor(sets[s][1][:, m, :], yb[n % 3][:, :], sets[s][0][:, m, :].bitcast(f32),
                                            ALU.subtract).then_inc(lo_done, 1)

                def layers(t, general, after_first):
                    for m in range(HT):
                        dve.wait_ge(gate_done, t * HT + m + 1)
                        dve.wait_ge(bank_ready, t * SLOTS_T + 2 * m + 2)
                        if not general and m >= 3:
                            dve.wait_ge(lo_done, t * BLOCKS + m - 2)
                        dst = full[0][:, m, :] if general else yb[m % 3][:, :]
                        nc.vector.scalar_tensor_tensor(out=dst, in0=B[(2 * m + 1) % 4][:, :], scalar=scol[:, HT + m:HT + m + 1],
                                                       in1=gate[m % 2][:, :], op0=ALU.mult, op1=ALU.mult).then_inc(f_ready, 1)
                        if not general and m:
                            low(t, m - 1, 0, m - 1)
                    if not general:
                        low(t, HT - 1, 0, HT - 1)
                    for layer in (1, 2):
                        for m in range(HT):
                            if not general:
                                low(t, layer * HT + m, layer % 2, m)
                            if layer == 1 and m < len(after_first):
                                after_first[m]()
                    if not general:
                        dve.wait_ge(lo_done, t * BLOCKS + BLOCKS)

                def tail(t, p, n):
                    def scale():
                        dve.wait_ge(o_ready, t + 1)
                        dve.wait_ge(out_stored[p], n * 16 + 16)
                        nc.vector.tensor_tensor(z[p][:, :, :], O[:, :, :], bcast_mid(srow[:, :], BATCH), ALU.mult).then_inc(o_free, 1)

                    def residual():
                        dve.wait_ge(o_free, t + 2)
                        nc.vector.tensor_tensor(z[p][:, :, :], z[p][:, :, :], x1[p][:, :, :], ALU.add).then_inc(z_done, 1)

                    def spread():
                        dve.wait_ge(z_done, t + 1)
                        for b in range(BATCH):
                            last = nc.vector.bn_stats(stats[:, b, :], z[p][:, b, :])
                        last.then_inc(st_done, 1)

                    def spread_sum():
                        dve.wait_ge(par_in, 32)
                        dve.wait_ge(st_done, t + 1)
                        for b in range(BATCH):
                            last = nc.vector.bn_aggr(mv[:, b, :], stats[:, b, :])
                        last.then_inc(var_done, 1)

                    def layer_norm():
                        dve.wait_ge(rstd_done, t + 1)
                        for b in range(BATCH):
                            last = nc.vector.tensor_scalar(z[p][:, b, :], z[p][:, b, :], mv[:, b, 0:1], rstd[:, b:b + 1],
                                                           ALU.subtract, ALU.mult)
                        last.then_inc(out_done, 1)

                    return [scale, residual, spread, spread_sum, layer_norm]

                def emit(general):
                    if not general:
                        split(0)
                    layers(0, general, [])
                    if not general:
                        split(1)
                    with dve.Fori(0, STEPS // 2 - 1) as i:
                        for p in range(2):
                            t = i * 2 + p + 1
                            layers(t, general, tail(t - 1, p, i))
                            if not general:
                                split(t + 1)
                    layers(STEPS - 1, general, tail(STEPS - 2, 0, STEPS // 2 - 1))
                    for piece in tail(STEPS - 1, 1, STEPS // 2 - 1):
                        piece()

                either(dve, emit)

            @block.gpsimd
            def _(pool):
                nc.gpsimd.memset(ln_eps[:, :], LN_EPS)
                nc.gpsimd.memset(power[:, :], -0.5).then_inc(power_set, 1)
                pool.wait_ge(power_set, 1)

                def tail(t):
                    pool.wait_ge(var_done, t + 1)
                    nc.gpsimd.tensor_tensor(rstd[:, :], mv[:, :, 1:2].rearrange("p b o -> p (b o)"), ln_eps[:, :],
                                            ALU.add).then_inc(rs_link, 1)
                    pool.wait_ge(rs_link, t + 1)
                    nc.gpsimd.tensor_tensor(rstd[:, :], rstd[:, :], power[:, :], ALU.pow).then_inc(rstd_done, 1)

                def emit(general):
                    with pool.Fori(0, STEPS) as t:
                        tail(t)

                either(pool, emit)


def build(nc, io):
    sems = ExitStack()
    with sems:
        whole = Stage(nc, sems)
        with whole.ctx:
            keep = {
                "const": whole.sb("const", [P, C_END]),
                "pw": whole.sb("pw", [P, HEADS, 5, STEPS * BATCH]),
                "scales": whole.sb("scales", [P, 2, STEPS, NS]),
            }
            early = Stage(nc, sems)
            with early.ctx:
                keep["raw"] = early.sb("raw", [P, STEPS * BATCH, NRAW])
                keep["gdiag"] = early.sb("gdiag", [P, 2 * STEPS, BH * CH])
                project(nc, sems, io, keep)
                weights(nc, sems, io, keep)
            fir(nc, sems, io, keep)
            delta(nc, sems, io, keep)
            ffn(nc, sems, io, keep)


def host_layout(np, a):
    g = {k.replace("L0_attn_", "").replace("L0_ffn_", ""): np.asarray(v, dtype=np.float32) for k, v in a.items()}
    x = g["hidden_states"]
    cols = np.pad(x.transpose(0, 2, 1), ((0, 0), (0, 0), (HALO, 0)))
    xt = np.stack([cols[:, :, t * P:t * P + XW] for t in range(STEPS)])
    xt = xt.reshape(STEPS, BATCH, KT, P, XW).transpose(0, 3, 2, 1, 4)

    def kmajor(w):
        return w.T.reshape(w.shape[1] // P, P, w.shape[0]).transpose(1, 0, 2)

    def columns(w):
        return w.reshape(-1, P).T

    w_qkv = np.concatenate([kmajor(g[n]) for n in ("Wq", "Wk", "Wv")], axis=2)
    w_gate = np.concatenate([kmajor(g["gate_w"].reshape(NGATE, D)), kmajor(g["Wb"])], axis=2)
    taps = np.concatenate([g[n].reshape(KT, P, CONV) for n in ("conv_q", "conv_k", "conv_v")]).transpose(1, 0, 2)
    firp = np.zeros((D, NF, FIRPAD), np.float32)
    for f, (n, k) in enumerate(zip(("fir_s", "fir_m", "fir_l"), FIRS)):
        firp[:, f, WIN - 1:WIN - 1 + k] = g[n].reshape(D, k)[:, ::-1]
    prm = np.concatenate([g["gate_b"].reshape(-1), g["log_temp"].reshape(-1), g["eps_param"].reshape(-1)])[None]
    ffn_w = np.concatenate([kmajor(g[n]).reshape(P, -1) for n in ("w1_w", "w2_w", "h1_w", "h2_w", "w3_w")], axis=1)
    scol = np.concatenate([columns(g[n]) for n in ("w1_s", "w2_s", "h1_s", "h2_s")], axis=1)
    i, j = np.arange(P)[:, None], np.arange(P)[None, :]
    const = np.zeros((P, C_END), np.float32)
    const[:, C_ID:C_ID + P] = i == j
    const[:, C_OFF:C_OFF + P] = j // CH > i // CH
    const[:, C_ATT:C_ATT + P] = j >= i
    const[:, C_DIAG:C_DIAG + CH] = np.where(np.arange(CH)[None, :] < i % CH, -1.0, 0.0)
    const[:, C_ONE:C_ONE + CH] = np.arange(CH)[None, :] == i % CH
    const[:, C_SEL:C_SEL + 2] = i // DK == np.arange(2)[None, :]
    return {"x": x, "xt": xt, "w_qkv": w_qkv, "w_gate": w_gate, "taps": taps, "firp": firp, "prm": prm, "ffn_w": ffn_w,
            "scol": scol, "srow": g["w3_s"][None], "const": const, "w_o": kmajor(g["Wo"]),
            "norm_w": np.concatenate([g["norm_w"]] * 2)[:, None]}


SCRATCH = {
    "qk_s": (STEPS, P, 2 * KT, TOK),
    "k_s": (STEPS, P, BATCH, D),
    "v_s": (BATCH, SEQ, D),
    "vr_s": (BATCH, SEQ + WIN, D),
    "a_s": (P, GRP, CH),
    "d_s": (P, GRP, CH),
    "t_s": (P, GRP, CH),
    "mix_s": (STEPS, P, BATCH, D),
    "x1_s": (STEPS, P, BATCH, D),
    "flag_s": (1, 1),
}


def kernel(**inputs):
    import numpy as np
    import concourse.bacc as bacc
    from concourse.bass_utils import run_bass_kernel_spmd

    nc = bacc.Bacc("TRN2", target_bir_lowering=False, num_devices=1)
    arrays = {f"in_{k}": np.ascontiguousarray(v) for k, v in host_layout(np, inputs).items()}
    io = {k[3:]: nc.dram_tensor(k, v.shape, f32, kind="ExternalInput").ap() for k, v in arrays.items()}
    for k, shape in SCRATCH.items():
        io[k] = nc.dram_tensor(k, shape, f32).ap()
    io["out"] = nc.dram_tensor("out", (BATCH, SEQ, D), f32, kind="ExternalOutput").ap()
    build(nc, io)
    r = run_bass_kernel_spmd(nc, [arrays], core_ids=[0])
    return r.results[0]["out"]
```

```python
import concourse.bass as bass
from concourse import mybir
from contextlib import ExitStack

f32 = mybir.dt.float32
f32r = mybir.dt.float32r
i32 = mybir.dt.int32
ALU = mybir.AluOpType
ACT = mybir.ActivationFunctionType
AX = mybir.AxisListType

P = 128
BATCH, SEQ, D, HEADS = 4, 2048, 256, 4
DK = D // HEADS
KT = D // P
STEPS = SEQ // P
TOK = BATCH * P
CONV = 4
HALO = CONV - 1
XW = P + HALO
FIRS = (3, 15, 63)
NF = len(FIRS)
WIN = 64
FIRPAD = 3 * WIN
FCH = 8
CH = 32
NQ = P // CH
BH = BATCH * KT
NS = 2 * BH
GRP = STEPS * NS
SLOTS = GRP * NQ // P
BLOCK_PARTS = ((0, STEPS // 2), (STEPS // 2, 3 * STEPS // 4), (3 * STEPS // 4, STEPS))
HID = 1024
HT = HID // P
NGATE = HEADS * 5
NRAW = NGATE + HEADS + HEADS
LN_EPS = 1e-5
L2_EPS = 1e-6
C_ID, C_OFF, C_ATT, C_ONE, C_SEL, C_END = 0, P, 2 * P, 3 * P, 3 * P + CH, 3 * P + CH + 2
W1, W2, H1, H2, W3 = 0, KT * HID, 2 * KT * HID, 2 * KT * HID + HT * HID, 2 * KT * HID + 2 * HT * HID
W_END = W3 + HT * D


class Stage:

    def __init__(self, nc, sems):
        self.nc, self.ctx, self.sems = nc, ExitStack(), sems

    def sb(self, name, shape, dt=f32):
        return self.ctx.enter_context(self.nc.sbuf_tensor(name, shape, dt))

    def ps(self, name, shape):
        return self.ctx.enter_context(self.nc.psum_tensor(name, shape, f32))

    def sem(self, name):
        return self.sems.enter_context(self.nc.semaphore(name))

    def pair(self, name):
        return [self.sem(f"{name}{i}") for i in range(2)]


def row(ap, t):
    names = [f"a{i}" for i in range(len(ap.shape) - 1)]
    return ap[bass.ds(t, 1)].rearrange(f"o {names[0]} {' '.join(names[1:])} -> {names[0]} (o {names[1]}) {' '.join(names[2:])}")


def bcast(ap, n):
    return bass.AP(tensor=ap.tensor, offset=ap.offset, ap=[*ap.ap, [0, n]])


def bcast_mid(ap, n):
    return bass.AP(tensor=ap.tensor, offset=ap.offset, ap=[ap.ap[0], [0, n], *ap.ap[1:]])


def blocks_in(queue, io, keep, part):
    first, end = BLOCK_PARTS[part]
    g, rows = first // (STEPS // 2), slice(first * NS % P, (end * NS - 1) % P + 1)
    for q in range(NQ):
        queue.dma_start(keep["tri"][rows, q * (GRP // P) + g, :, :],
                        io["a_s"][q * CH:q * CH + CH, first * NS:end * NS, :].rearrange("i n j -> n i j")
                        ).then_inc(keep["tri_in"], 16)


def project(nc, sems, io, keep):
    st = Stage(nc, sems)
    with st.ctx:
        w_qkv = st.sb("w_qkv", [P, KT, 3 * D])
        w_gate = st.sb("w_gate", [P, KT, NGATE + HEADS])
        taps = st.sb("taps", [P, 3 * KT, CONV])
        zero = st.sb("zero", [WIN, HEADS, BATCH * DK])
        xt = [st.sb(f"xt{i}", [P, KT, BATCH, XW]) for i in range(2)]
        acc = [st.sb(f"acc{i}", [P, BATCH, P]) for i in range(3)]
        yT = [st.sb(f"yT{i}", [P, 3 * KT, TOK]) for i in range(2)]
        sq = st.sb("sq", [P, KT, TOK])
        ktok = [st.sb(f"ktok{i}", [P, BATCH, D]) for i in range(2)]
        vtok = [st.sb(f"vtok{i}", [P, HEADS, BATCH, DK]) for i in range(2)]
        picked = [st.sb(f"picked{i}", [P, NS, CH]) for i in range(2)]
        proj = [st.ps(f"proj{i}", [P, BATCH, 2 * P]) for i in range(2)]
        side = [st.ps(f"side{i}", [P, 512]) for i in range(2)]
        tok = st.ps("tok", [P, BATCH, D])
        gates = side[0][:, 0:BATCH * 24].rearrange("p (b n) -> p b n", b=BATCH)
        norms = side[1][:, 0:BATCH * HEADS].rearrange("p (b n) -> p b n", b=BATCH)
        kfull = [st.sb(f"kfull{i}", [P, NS, P]) for i in range(2)]
        const, raw, kk = keep["const"], keep["raw"], keep["kk"]
        ident, headsel = const[:, C_ID:C_ID + P], const[:, C_SEL:C_SEL + 2]

        loaded, prm_in = st.sem("p1_loaded"), st.sem("p1_prm_in")
        zeroed = st.sem("p1_zeroed")
        zero_stored = st.sem("p1_zero_stored")
        xt_ready = st.pair("p1_xt_ready")
        proj_ready, tap_done = st.sem("p1_proj_ready"), st.sem("p1_tap_done")
        conv_step, conv_done, silu_done = st.sem("p1_conv_step"), st.sem("p1_conv_done"), st.sem("p1_silu_done")
        sq_done, diag_picked, kk_summed = st.sem("p1_sq_done"), st.sem("p1_diag_picked"), st.sem("p1_kk_summed")
        kk_stored, diag_stored, kk_masked = st.pair("p1_kk_stored"), st.pair("p1_diag_stored"), st.sem("p1_kk_masked")
        kk_ready, ktok_ready, vtok_ready, small_ready = (st.sem(f"p1_{n}_ready") for n in ("kk", "ktok", "vtok", "small"))
        kk_out, ktok_out, vtok_out, small_out = (st.sem(f"p1_{n}_out") for n in ("kk", "ktok", "vtok", "small"))
        qk_stored, k_stored, v_stored = (st.pair(f"p1_{n}_stored") for n in ("qk", "k", "v"))
        NL = 4
        CB = 3 * KT

        with nc.Block() as block:
            @block.sync
            def _(sp):
                sp.dma_start(const[:, :], io["const"]).then_inc(loaded, 16)
                sp.dma_start(w_qkv[:, :, :], io["w_qkv"]).then_inc(loaded, 16)
                sp.dma_start(w_gate[:, :, :], io["w_gate"]).then_inc(loaded, 16)
                sp.dma_start(taps[:, :, :], io["taps"]).then_inc(loaded, 16)
                src = io["prm"]
                sp.dma_start(keep["prm"][:, :], bass.AP(tensor=src.tensor, offset=0, ap=[[0, P], [1, NGATE + 2 * HEADS]])
                             ).then_inc(prm_in, 16)

                def load(t, p):
                    sp.dma_start(xt[p][:, :, :, :], row(io["xt"], t)).then_inc(xt_ready[p], 16)

                def store(t, p, more):
                    n = t + 1
                    sp.wait_ge(silu_done, n * CB - KT)
                    sp.dma_start(row(io["qk_s"], t), yT[p][:, 0:2 * KT, :]).then_inc(qk_stored[p], 16)
                    if more:
                        sp.wait_ge(small_ready, n)
                        load(t + 2, p)
                    sp.wait_ge(kk_out, 4 * n)
                    for q in range(NQ):
                        rows = slice(q * CH, q * CH + CH)
                        sp.dma_start(io["a_s"][rows, bass.ds(t * NS, NS), :], kfull[p][rows, :, rows]).then_inc(diag_stored[p], 16)
                    sp.wait_ge(ktok_out, n)
                    sp.dma_start(row(io["k_s"], t), ktok[p][:, :, :]).then_inc(k_stored[p], 16)
                    sp.wait_ge(vtok_out, n + 1)
                    sp.dma_start(io["v_s"][:, :, bass.ds(t + 1, 1), :, :].rearrange("h p o b d -> p h (o b d)"),
                                 vtok[p][:, :, :, :].rearrange("p h b d -> p h (b d)")).then_inc(v_stored[p], 16)
                    sp.wait_ge(kk_masked, n)
                    sp.dma_start(io["kk_s"][:, bass.ds(t * NS, NS), :], kfull[p][:, :, :]).then_inc(kk_stored[p], 16)

                load(0, 0)
                load(1, 1)
                sp.wait_ge(zeroed, 1)
                sp.dma_start(io["v_s"][:, WIN:P, 0, :, :].rearrange("h p b d -> p h (b d)"), zero[:, :, :]).then_inc(zero_stored, 16)
                done = 0
                for part, (_, end) in enumerate(BLOCK_PARTS):
                    with sp.Fori(done // 2, min(end, STEPS - 2) // 2) as i:
                        for p in range(2):
                            store(i * 2 + p, p, True)
                    done = end
                    if end < STEPS:
                        for p in range(2):
                            sp.wait_ge(diag_stored[p], end // 2 * (16 * NQ))
                        blocks_in(sp, io, keep, part)
                for p in range(2):
                    store(STEPS - 2 + p, p, False)
                for p in range(2):
                    sp.wait_ge(qk_stored[p], 8 * STEPS)
                    sp.wait_ge(k_stored[p], 8 * STEPS + 16)
                    sp.wait_ge(v_stored[p], 8 * STEPS + 16)
                sp.wait_ge(zero_stored, 16)
                sp.wait_ge(prm_in, 16)
                for p in range(2):
                    sp.wait_ge(kk_stored[p], 8 * STEPS + 16)
                    sp.wait_ge(diag_stored[p], STEPS // 2 * (16 * NQ))

            @block.tensor
            def _(pe):
                pe.wait_ge(loaded, 16 * NL)

                def products(t, p, cb):
                    pe.wait_ge(conv_done, t * CB + cb + 1)
                    for half in range(2):
                        for k in range(KT):
                            last = nc.tensor.matmul(
                                proj[cb % 2][:, 2 * half:2 * half + 2, 0:XW], w_qkv[:, k, cb * P:cb * P + P],
                                xt[p][:, k, 2 * half:2 * half + 2, :], start=(k == 0), stop=(k == KT - 1))
                    last.then_inc(proj_ready, 1)

                def turn(src):
                    for b in range(BATCH):
                        for hh in range(KT):
                            last = nc.tensor.transpose(tok[:, b, hh * P:hh * P + P], src(hh, b), ident)
                    return last

                def keys(t, p):
                    pe.wait_ge(silu_done, t * CB + 2 * KT)
                    pe.wait_ge(vtok_out, t + 1)
                    pe.wait_ge(small_out, t + 1)
                    turn(lambda hh, b: yT[p][:, KT + hh, b * P:b * P + P]).then_inc(ktok_ready, 1)
                    squared(t, p, 0)

                def squared(t, p, first):
                    for g in range(first, first + 2):
                        if g >= 2:
                            pe.wait_ge(kk_out, t * 4 + g - 1)
                        par, half = g // 2, g % 2
                        for j in range(4):
                            s = half * 4 + j
                            b, hh = s // KT, s % KT
                            kt = yT[p][64 * par:64 * par + DK, KT + hh, b * P:b * P + P]
                            last = nc.tensor.matmul(side[g % 2][:, j * P:j * P + P], kt, kt, start=True, stop=True)
                        last.then_inc(kk_ready, 1)

                def small(t, p):
                    pe.wait_ge(kk_out, t * 4 + 4)
                    for b in range(BATCH):
                        for k in range(KT):
                            nc.tensor.matmul(gates[:, b, :], xt[p][:, k, b, HALO:XW], w_gate[:, k, :],
                                             start=(k == 0), stop=(k == KT - 1))
                    pe.wait_ge(sq_done, t + 1)
                    for hh in range(KT):
                        for b in range(BATCH):
                            last = nc.tensor.matmul(norms[:, b, 2 * hh:2 * hh + 2], sq[:, hh, b * P:b * P + P],
                                                    headsel, start=True, stop=True)
                    last.then_inc(small_ready, 1)

                def values(t, p):
                    pe.wait_ge(silu_done, t * CB + CB)
                    pe.wait_ge(ktok_out, t + 1)
                    turn(lambda hh, b: yT[p][:, 2 * KT + hh, b * P:b * P + P]).then_inc(vtok_ready, 1)

                after = {0: keys, 1: lambda t, p: squared(t, p, 2), 2: small, 4: values}

                def step(t, p, n, follow):
                    pe.wait_ge(xt_ready[p], n * 16 + 16)
                    for cb in range(CB):
                        products(t, p, cb)
                        if follow and cb in after:
                            after[cb](t - 1, 1 - p)

                step(0, 0, 0, False)
                with pe.Fori(0, STEPS // 2 - 1) as i:
                    step(i * 2 + 1, 1, i, True)
                    step(i * 2 + 2, 0, i + 1, True)
                step(STEPS - 1, 1, STEPS // 2 - 1, True)
                for piece in after.values():
                    piece(STEPS - 1, 1)

            @block.scalar
            def _(act):
                act.wait_ge(loaded, 16 * NL)

                def silu(t, p, cb):
                    act.wait_ge(conv_done, t * CB + cb + 3)
                    nc.scalar.activation(yT[p][:, cb, :].rearrange("p (b n) -> p b n", b=BATCH),
                                         acc[cb % 3][:, :, :], ACT.Silu).then_inc(silu_done, 1)

                def keys_out(t, p, n):
                    act.wait_ge(ktok_ready, t + 1)
                    act.wait_ge(k_stored[p], n * 16 + 16)
                    nc.scalar.activation(ktok[p][:, :, :], tok[:, :, :], ACT.Copy).then_inc(ktok_out, 1)
                    act.wait_ge(kk_stored[p], n * 16 + 16)
                    act.wait_ge(kk_summed, t + 1)
                    squared_out(t, p, 0)

                def squared_out(t, p, first):
                    for g in range(first, first + 2):
                        act.wait_ge(kk_ready, t * 4 + g + 1)
                        nc.scalar.activation(kfull[p][:, g * 4:g * 4 + 4, :], side[g % 2][:, :].rearrange("p (s n) -> p s n", n=P),
                                             ACT.Copy).then_inc(kk_out, 1)

                def step(t, p, n, follow, fresh):
                    for cb in range(CB):
                        act.wait_ge(proj_ready, t * CB + cb + 1)
                        if cb >= 3:
                            act.wait_ge(silu_done, t * CB + cb - 2)
                        nc.scalar.activation(acc[cb % 3][:, :, :], proj[cb % 2][:, :, HALO:XW], ACT.Copy,
                                             scale=taps[:, cb, HALO:CONV]).then_inc(tap_done, 1)
                        if follow and cb == 0:
                            keys_out(t - 1, 1 - p, n)
                        if follow and cb == 1:
                            squared_out(t - 1, 1 - p, 2)
                        if cb >= 1:
                            if cb == 1 and not fresh:
                                act.wait_ge(qk_stored[p], (n + 1 - p) * 16)
                                act.wait_ge(sq_done, t - 1)
                                act.wait_ge(vtok_ready, t - 1)
                            silu(t, p, cb - 1)
                    silu(t, p, CB - 1)
                    act.wait_ge(silu_done, t * CB + CB)

                for p in range(2):
                    act.sem_inc(k_stored[p], 16)
                    act.sem_inc(kk_stored[p], 16)
                step(0, 0, 0, False, True)
                step(1, 1, 0, True, True)
                with act.Fori(1, STEPS // 2) as i:
                    step(i * 2, 0, i - 1, True, False)
                    step(i * 2 + 1, 1, i, True, False)
                keys_out(STEPS - 1, 1, STEPS // 2 - 1)
                squared_out(STEPS - 1, 1, 2)

            @block.vector
            def _(dve):
                dve.wait_ge(loaded, 16 * NL)
                dve.sem_inc(conv_done, 2)
                dve.sem_inc(small_out, 1)
                dve.sem_inc(vtok_out, 1)
                dve.sem_inc(kk_summed, 2)
                for p in range(2):
                    dve.sem_inc(v_stored[p], 16)

                def convolution(t, cb):
                    dve.wait_ge(tap_done, t * CB + cb + 1)
                    for j in range(HALO):
                        if j:
                            dve.wait_ge(conv_step, (t * CB + cb) * (HALO - 1) + j)
                        nc.vector.scalar_tensor_tensor(
                            out=acc[cb % 3][:, :, :], in0=proj[cb % 2][:, :, j:j + P], scalar=taps[:, cb, j:j + 1],
                            in1=acc[cb % 3][:, :, :], op0=ALU.mult, op1=ALU.add,
                        ).then_inc(conv_step if j < HALO - 1 else conv_done, 1)

                def small_copies(t):
                    dve.wait_ge(small_ready, t + 1)
                    nc.vector.tensor_copy(raw[:, bass.ds(t * BATCH, BATCH), 0:24], gates[:, :, :])
                    nc.vector.tensor_copy(raw[:, bass.ds(t * BATCH, BATCH), 24:24 + HEADS], norms[:, :, :]).then_inc(small_out, 1)

                def values_out(t, p, n):
                    dve.wait_ge(vtok_ready, t + 1)
                    dve.wait_ge(v_stored[p], n * 16 + 16)
                    dve.wait_ge(diag_picked, t * NQ + NQ)
                    nc.vector.tensor_copy(vtok[p][:, :, :, :].rearrange("p h b d -> p b h d"),
                                          tok[:, :, :].rearrange("p b (h d) -> p b h d", d=DK)).then_inc(vtok_out, 1)
                    nc.vector.tensor_reduce(kk[:, bass.ds(t, 1), :, :].rearrange("p o r s -> p (o r s)"), picked[p][:, :, :],
                                            AX.X, ALU.add).then_inc(kk_summed, 1)

                def step(t, p, n, follow):
                    for cb in range(CB):
                        convolution(t, cb)
                        if follow and cb == 2:
                            small_copies(t - 1)
                        if follow and cb == 4:
                            values_out(t - 1, 1 - p, n)

                step(0, 0, 0, False)
                with dve.Fori(0, STEPS // 2 - 1) as i:
                    step(i * 2 + 1, 1, i, True)
                    step(i * 2 + 2, 0, i, True)
                step(STEPS - 1, 1, STEPS // 2 - 1, True)
                small_copies(STEPS - 1)
                values_out(STEPS - 1, 1, STEPS // 2 - 1)

            @block.gpsimd
            def _(pool):
                nc.gpsimd.memset(zero[:, :, :], 0.0).then_inc(zeroed, 1)

                def squares(t, p):
                    pool.wait_ge(silu_done, t * CB + KT)
                    nc.gpsimd.tensor_tensor(sq[:, :, :], yT[p][:, 0:KT, :], yT[p][:, 0:KT, :],
                                            ALU.mult).then_inc(sq_done, 1)

                def diagonals(t, p, n):
                    for q in range(NQ):
                        rows = slice(q * CH, q * CH + CH)
                        if q:
                            pool.wait_ge(diag_picked, t * NQ + q)
                        nc.gpsimd.tensor_tensor(picked[p][rows, :, :], kfull[p][rows, :, rows],
                                                bcast_mid(const[rows, C_ONE:C_ONE + CH], NS), ALU.mult).then_inc(diag_picked, 1)
                    pool.wait_ge(diag_stored[p], n * (16 * NQ) + 16 * NQ)
                    pool.wait_ge(diag_picked, t * NQ + NQ)
                    nc.gpsimd.tensor_tensor(kfull[p][:, :, :], kfull[p][:, :, :], bcast_mid(const[:, C_OFF:C_OFF + P], NS),
                                            ALU.mult).then_inc(kk_masked, 1)

                def step(t, p, n):
                    pool.wait_ge(small_ready, t)
                    if not isinstance(t, int) or t > 1:
                        pool.wait_ge(kk_masked, t - 1)
                    squares(t, p)
                    pool.wait_ge(kk_out, t * 4)
                    pool.wait_ge(kk_summed, t)
                    pool.wait_ge(sq_done, t + 1)
                    diagonals(t - 1, 1 - p, n)

                pool.wait_ge(loaded, 16 * NL)
                squares(0, 0)
                step(1, 1, 0)
                with pool.Fori(1, STEPS // 2) as i:
                    for p in range(2):
                        step(i * 2 + p, p, i - 1 + p)
                pool.wait_ge(kk_out, 4 * STEPS)
                pool.wait_ge(kk_summed, STEPS)
                pool.wait_ge(sq_done, STEPS)
                diagonals(STEPS - 1, 1, STEPS // 2 - 1)


def weights_fir(nc, sems, io, keep):
    st = Stage(nc, sems)
    with st.ctx:
        itemp = st.sb("itemp", [P, HEADS])
        eps = st.sb("eps", [P, HEADS])
        slope = st.sb("slope", [P, HEADS])
        half = st.sb("half", [P, STEPS * BATCH, HEADS])
        lg = st.sb("lg", [P, STEPS * BATCH, HEADS, 5])
        mx = st.sb("mx", [P, STEPS * BATCH * HEADS])
        beta = st.sb("beta", [P, STEPS * BATCH, HEADS])
        ssk = st.sb("ssk", [P, STEPS * BATCH, HEADS])
        rq = st.sb("rq", [P, STEPS * BATCH, HEADS])
        gam = st.sb("gam", [P, STEPS, 2, BH])
        gamT, neg_gamT = st.sb("gamT", [P, SLOTS, CH]), st.sb("neg_gamT", [P, SLOTS, CH])
        prod = st.sb("prod", [P, SLOTS * CH * CH])
        win = [st.sb(f"win{i}", [P, 2 * STEPS * BATCH, DK]) for i in range(2)]
        toe = [st.sb(f"toe{i}", [P, FCH, NF, WIN]) for i in range(2)]
        outs = [st.sb(f"outs{i}", [P, FCH, NF * WIN]) for i in range(2)]
        two = [st.sb(f"two{i}", [P, FCH, WIN]) for i in range(2)]
        mixed = [st.sb(f"mixed{i}", [P, WIN, DK // 2]) for i in range(2)]
        pwT = st.sb("pwT", [P, HEADS, NF * WIN])
        conv = [st.ps(f"conv{i}", [P, FCH // 2, 512]) for i in range(2)]
        const, prm, raw, kk, tri, pw, scales = (keep[n] for n in ("const", "prm", "raw", "kk", "tri", "pw", "scales"))
        ident = const[:, C_ID:C_ID + P]
        NT = STEPS * BATCH
        NG = DK // FCH
        lgf = lg[:, :, :, :].rearrange("p t h f -> p (t h) f")
        turned_inv = prod[:, :].rearrange("p (s c i) -> p s c i", c=CH, i=CH)
        FIRST = [(WIN + 1 - k) // 16 * 16 for k in FIRS]
        NSUB = GRP // P
        HALF = NG // 2
        NWIN = 3 * BATCH
        EARLY = 3 * CH // 4
        gam_ps = conv[0][:, 0, 0:GRP].rearrange("p (g n) -> p g n", g=NSUB)
        pw_ps = conv[1][:, 0:2, :].rearrange("p b n -> p (b n)")[:, 0:HEADS * NF * WIN]

        def streams(ap):
            return ap.rearrange("p (t b) (k r) -> p t r (b k)", t=STEPS, r=2)

        exps, roots = st.sem("p2_exps"), st.sem("p2_roots")
        chain, to_exp, to_root, pw_done = st.sem("p2_chain"), st.sem("p2_to_exp"), st.sem("p2_to_root"), st.sem("p2_pw_done")
        gam_done, gam_turned, upper_zero = st.sem("p2_gam_done"), st.sem("p2_gam_turned"), st.sem("p2_upper_zero")
        inv_done, inv_stored, turned = st.sem("p2_inv_done"), st.sem("p2_inv_stored"), st.sem("p2_turned")
        tables_turned, tables_out = st.sem("p2_tables_turned"), st.sem("p2_tables_out")
        win_in, toe_in, toe_zero = st.pair("p2_win_in"), st.pair("p2_toe_in"), st.sem("p2_toe_zero")
        conv_ready, conv_out, scaled = st.sem("p2_conv_ready"), st.sem("p2_conv_out"), st.sem("p2_scaled")
        two_done, mixed_done, mixed_stored = st.sem("p2_two_done"), st.sem("p2_mixed_done"), st.pair("p2_mixed_stored")
        tri_in = keep["tri_in"]

        with nc.Block() as block:
            @block.sync
            def _(sp):
                def windows(h, i):
                    e, t = i // BATCH, i % BATCH * (STEPS // BATCH)
                    steps = slice(t, t + STEPS // BATCH)
                    after = slice(t + 1, t + 1 + STEPS // BATCH)
                    parts = [(slice(0, P), slice(0, P), after)] if e else [
                        (slice(0, WIN), slice(WIN, P), steps), (slice(WIN, P), slice(0, WIN), after)]
                    for rows, tokens, ts in parts:
                        sp.dma_start(win[h % 2][rows, e * NT + t * BATCH:e * NT + steps.stop * BATCH, :],
                                     io["v_s"][h, tokens, ts, :, :].rearrange("p t b d -> p (t b) d")).then_inc(win_in[h % 2], 16)

                def toeplitz(n):
                    for f, k in enumerate(FIRS):
                        src = io["firp"]
                        sp.dma_start(toe[n % 2][FIRST[f]:, :, f, :],
                                     bass.AP(tensor=src.tensor, offset=(n * FCH * NF + f) * FIRPAD + FIRST[f],
                                             ap=[[1, P - FIRST[f]], [NF * FIRPAD, FCH], [1, WIN]])).then_inc(toe_in[n % 2], 16)

                def store(u):
                    sp.wait_ge(mixed_done, (u + 1) * HALF + 2)
                    sp.dma_start(io["mix_s"][:, :, :, u, :, :].rearrange("e t b m d -> (e t b) m d"),
                                 mixed[u % 2][:, :, :]).then_inc(mixed_stored[u % 2], 16)

                def blocks_out(name, buf, g, rows):
                    sp.dma_start(io[name][g * P:g * P + P, :, rows, :].rearrange("n q i j -> n q (i j)"),
                                 buf[:, g:SLOTS:NSUB, rows, :].rearrange("p q i j -> p q (i j)")).then_inc(inv_stored, 16)

                for i in range(2 * BATCH):
                    windows(0, i)
                sp.wait_ge(toe_zero, 2)
                toeplitz(0)
                toeplitz(1)
                for n in range(HEADS * NG):
                    h, g = n // NG, n % NG
                    sp.wait_ge(conv_ready, n + 1)
                    if n + 2 < HEADS * NG:
                        toeplitz(n + 2)
                    if h + 1 < HEADS:
                        windows(h + 1, g)
                    if n > HALF and n % HALF == 2:
                        store(n // HALF - 1)
                    if h == HEADS - 1 and g % 3 == 0 and g // 3 < NSUB:
                        sp.wait_ge(inv_done, 1)
                        blocks_out("d_s", tri, g // 3, slice(0, EARLY))
                sp.wait_ge(inv_done, 2)
                for g in range(NSUB):
                    blocks_out("d_s", tri, g, slice(EARLY, CH))
                for g in range(NSUB):
                    sp.wait_ge(turned, g + 1)
                    blocks_out("t_s", turned_inv, g, slice(0, CH))
                store(2 * HEADS - 1)
                sp.wait_ge(inv_stored, 16 * 3 * NSUB)
                for u in range(2):
                    sp.wait_ge(mixed_stored[u], 16 * HEADS + 16)

            @block.tensor
            def _(pe):
                pe.wait_ge(gam_done, 1)
                for g in range(NSUB):
                    last = nc.tensor.transpose(gam_ps[:, g, :], gam[:, :, :, :].rearrange("p t r s -> p (t r s)")[:, g * P:g * P + P],
                                               ident)
                last.then_inc(gam_turned, 1)
                pe.wait_ge(pw_done, 1)
                for h in range(HEADS):
                    for f in range(NF):
                        for e in range(2):
                            part = slice(e * WIN, e * WIN + WIN)
                            c = (h * NF + f) * WIN
                            last = nc.tensor.matmul(pw_ps[part, c:c + WIN], pw[part, h, f, :], ident[part, part],
                                                    start=True, stop=True)
                last.then_inc(tables_turned, 1)
                pe.wait_ge(tables_out, 3)
                with pe.Fori(0, HEADS // 2) as i:
                    for hp in range(2):
                        pe.wait_ge(win_in[hp], i * (16 * NWIN) + 16 * NWIN)
                        for g in range(NG):
                            n = (i * 2 + hp) * NG + g
                            pe.wait_ge(toe_in[g % 2], (n + (2 - g % 2)) * (8 * NF))
                            pe.wait_ge(conv_out, n + 1)
                            for c in range(FCH):
                                last = nc.tensor.matmul(conv[g % 2][:, c // 2, c % 2 * NF * WIN:(c % 2 + 1) * NF * WIN],
                                                        win[hp][:, :, g * FCH + c], toe[g % 2][:, c, :, :],
                                                        start=True, stop=True)
                            last.then_inc(conv_ready, 1)

            @block.scalar
            def _(act):
                nc.scalar.activation(itemp[:, :], prm[:, NGATE:NGATE + HEADS], ACT.Exp, scale=-1.0).then_inc(exps, 1)
                nc.scalar.activation(beta[:, :, :], raw[:, :, NGATE:NGATE + HEADS], ACT.Exp, scale=-1.0).then_inc(exps, 1)
                blocks_in(act, io, keep, len(BLOCK_PARTS) - 1)
                act.wait_ge(to_exp, 1)
                nc.scalar.activation(lgf, lgf, ACT.Exp).then_inc(exps, 1)
                act.wait_ge(to_root, 1)
                nc.scalar.activation(scales[:, 0, :, :].rearrange("p t (b h) -> p (t b) h", b=BATCH), ssk[:, :, :], ACT.Sqrt)
                nc.scalar.activation(rq[:, :, :], rq[:, :, :], ACT.Sqrt).then_inc(roots, 1)
                for scale, dst in ((-1.0, neg_gamT), (1.0, gamT)):
                    act.wait_ge(gam_turned, 1)
                    nc.scalar.activation(dst[:, :, :].rearrange("p (q g) i -> p g q i", g=NSUB),
                                         gam_ps.rearrange("p g (q i) -> p g q i", i=CH), ACT.Copy, scale=scale).then_inc(tables_out, 1)
                act.wait_ge(tables_turned, 1)
                nc.scalar.activation(pwT[:, :, :].rearrange("p h (f m) -> p (h f) m", m=WIN)[:, :, ::-1],
                                     pw_ps.rearrange("p (n m) -> p n m", m=WIN), ACT.Copy).then_inc(tables_out, 1)
                act.sem_inc(conv_out, 2)
                act.sem_inc(mixed_done, 2)
                with act.Fori(0, HEADS * NG // 2) as i:
                    for j in range(2):
                        n = i * 2 + j
                        act.wait_ge(conv_ready, n + 1)
                        act.wait_ge(mixed_done, n + 1)
                        nc.scalar.activation(outs[j][:, :, :].rearrange("p (k e) n -> p k e n", e=2),
                                             conv[j][:, :, 0:2 * NF * WIN].rearrange("p k (e n) -> p k e n", e=2),
                                             ACT.Copy).then_inc(conv_out, 1)
                act.wait_ge(conv_out, HEADS * NG + 2)
                act.sem_inc(conv_out, 1)

            @block.vector
            def _(dve):
                n = [0]

                def link(ins):
                    n[0] += 1
                    ins.then_inc(chain, 1)
                    dve.wait_ge(chain, n[0])

                nc.vector.tensor_scalar(rq[:, :, :], raw[:, :, NGATE + HEADS:NRAW], L2_EPS, None, ALU.add)
                for par in range(2):
                    last = nc.vector.tensor_scalar(streams(ssk[:, :, :])[:, :, par, :], kk[:, :, par, :], L2_EPS, None, ALU.add)
                last.then_inc(to_root, 1)
                link(nc.vector.tensor_tensor(lg[:, :, :, :].rearrange("p t h f -> p t (h f)"), raw[:, :, 0:NGATE],
                                             bcast_mid(prm[:, 0:NGATE], NT), ALU.add))
                dve.wait_ge(exps, 1)
                link(nc.vector.tensor_tensor(lg[:, :, :, :], lg[:, :, :, :],
                                             bcast(bcast_mid(itemp[:, :], NT), 5), ALU.mult))
                link(nc.vector.tensor_reduce(mx[:, :], lgf, AX.X, ALU.max))
                nc.vector.tensor_tensor(lgf, lgf, bcast(mx[:, :], 5), ALU.subtract).then_inc(to_exp, 1)
                dve.wait_ge(exps, 2)
                link(nc.vector.tensor_scalar(beta[:, :, :], beta[:, :, :], 1.0, None, ALU.add))
                dve.wait_ge(to_root, 1)
                link(nc.vector.tensor_tensor(half[:, :, :], ssk[:, :, :], beta[:, :, :], ALU.mult))
                link(nc.vector.reciprocal(half[:, :, :], half[:, :, :]))
                for par in range(2):
                    last = nc.vector.tensor_copy(gam[:, :, par, :], streams(half[:, :, :])[:, :, par, :])
                last.then_inc(gam_done, 1)
                link(nc.vector.tensor_scalar(eps[:, :], prm[:, NGATE + HEADS:NGATE + 2 * HEADS], 0.0, 0.2, ALU.max, ALU.min))
                link(nc.vector.tensor_scalar(slope[:, :], eps[:, :], -5.0, 1.0, ALU.mult, ALU.add))
                dve.wait_ge(exps, 3)
                link(nc.vector.tensor_reduce(mx[:, :], lgf, AX.X, ALU.add))
                link(nc.vector.reciprocal(mx[:, :], mx[:, :]))
                by_head = mx[:, :].rearrange("p (t h) -> p t h", h=HEADS)
                link(nc.vector.tensor_tensor(by_head, by_head, bcast_mid(slope[:, :], NT), ALU.mult))
                link(nc.vector.tensor_tensor(lgf, lgf, bcast(mx[:, :], 5), ALU.mult))
                nc.vector.tensor_tensor(pw[:, :, :, :].rearrange("p h f t -> p t h f"), lg[:, :, :, :],
                                        bcast(bcast_mid(eps[:, :], NT), 5), ALU.add).then_inc(pw_done, 1)
                dve.wait_ge(pw_done, 1)
                dve.wait_ge(roots, 1)
                link(nc.vector.reciprocal(rq[:, :, :], rq[:, :, :]))
                nc.vector.tensor_tensor(scales[:, 1, :, :].rearrange("p t (b h) -> p (t b) h", b=BATCH), rq[:, :, :],
                                        pw[:, :, 3, :].rearrange("p h t -> p t h"), ALU.mult)

                dve.wait_ge(tri_in, 16 * NQ * len(BLOCK_PARTS))
                dve.wait_ge(tables_out, 1)
                for i in range(1, CH):
                    last = nc.vector.tensor_tensor(tri[:, :, i, 0:i], tri[:, :, i, 0:i], bcast(neg_gamT[:, :, i], i), ALU.mult)
                link(last)

                def inverse_row(i):
                    pr = prod[:, 0:SLOTS * i * i].rearrange("p (s c j) -> p s c j", s=SLOTS, c=i)
                    a = tri[:, :, i, 0:i]
                    a = bass.AP(tensor=a.tensor, offset=a.offset, ap=[a.ap[0], a.ap[1], [0, i], a.ap[2]])
                    link(nc.vector.tensor_tensor(pr, tri[:, :, 0:i, 0:i].rearrange("p s j c -> p s c j"), a, ALU.mult))
                    link(nc.vector.tensor_reduce(tri[:, :, i:i + 1, 0:i].rearrange("p s o c -> p s (o c)"), pr, AX.X, ALU.add))

                dve.wait_ge(tables_out, 2)
                link(nc.vector.tensor_copy(tri[:, :, :, :].rearrange("p s i j -> p s (i j)")[:, :, 0:CH * CH:CH + 1], gamT[:, :, :]))
                dve.wait_ge(upper_zero, 1)
                for i in range(1, CH):
                    inverse_row(i)
                    if i == EARLY - 1:
                        dve.sem_inc(inv_done, 1)
                dve.sem_inc(inv_done, 1)
                for g in range(NSUB):
                    nc.vector.tensor_copy(turned_inv[:, g:SLOTS:NSUB, :, :],
                                          tri[:, g:SLOTS:NSUB, :, :].rearrange("p q i c -> p q c i")).then_inc(turned, 1)

            @block.gpsimd
            def _(pool):
                for i in range(2):
                    nc.gpsimd.memset(toe[i][:, :, :, :], 0.0).then_inc(toe_zero, 1)
                pool.wait_ge(tri_in, 16 * NQ * len(BLOCK_PARTS))
                for i in range(CH - 1):
                    last = nc.gpsimd.memset(tri[:, :, i, i + 1:CH], 0.0)
                last.then_inc(upper_zero, 1)
                for u in range(2):
                    pool.sem_inc(mixed_stored[u], 16)
                pool.wait_ge(conv_out, 3)
                with pool.Fori(0, HEADS) as h:
                    for g in range(NG):
                        n = h * NG + g
                        part = outs[g % 2][:, :, :].rearrange("p c (f m) -> p f c m", f=NF)
                        nc.gpsimd.tensor_tensor(outs[g % 2][:, :, :], outs[g % 2][:, :, :],
                                                bcast_mid(pwT[:, bass.ds(h, 1), :].rearrange("p o n -> p (o n)"), FCH),
                                                ALU.mult).then_inc(scaled, 1)
                        pool.wait_ge(scaled, n + 1)
                        nc.gpsimd.tensor_tensor(two[g % 2][:, :, :], part[:, 0, :, :], part[:, 1, :, :], ALU.add).then_inc(two_done, 1)
                        pool.wait_ge(two_done, n + 1)
                        pool.wait_ge(conv_out, n + 4)
                        u, c = g // HALF, g % HALF * FCH
                        if c == 0:
                            pool.wait_ge(mixed_stored[u], h * 16 + 16)
                        nc.gpsimd.tensor_tensor(mixed[u][:, ::-1, c:c + FCH].rearrange("p m c -> p c m"), two[g % 2][:, :, :],
                                                part[:, 2, :, :], ALU.add).then_inc(mixed_done, 1)


def delta(nc, sems, io, keep):
    st = Stage(nc, sems)
    with st.ctx:
        wo = st.sb("wo", [P, KT, D])
        wo_raw = st.sb("wo_raw", [P, KT, D])
        norm_w = st.sb("norm_w", [P, 1])
        power = st.sb("power", [P, NS])
        head_eps = st.sb("head_eps", [P, NS])
        ln_eps = st.sb("ln_eps", [P, BATCH])
        qk = [st.sb(f"qk{i}", [P, 2 * KT, TOK]) for i in range(2)]
        ktok = [st.sb(f"kt{i}", [P, BATCH, D]) for i in range(2)]
        vtok = [st.sb(f"vt{i}", [P, HEADS, BATCH, DK]) for i in range(2)]
        xres = [st.sb(f"xres{i}", [P, BATCH, D]) for i in range(2)]
        mix = [st.sb(f"mix{i}", [P, BATCH, D]) for i in range(2)]
        ddiag = [st.sb(f"ddiag{i}", [P, NS, P]) for i in range(2)]
        tdiag = [st.sb(f"tdiag{i}", [P, NS, P]) for i in range(2)]
        lt = st.sb("lt", [P, NS, P])
        nmat = st.sb("nmat", [P, NS, P])
        r1 = st.sb("r1", [P, NS, P])
        r2 = st.sb("r2", [P, NS, P])
        tt = [st.sb(f"tt{i}", [P, NS, P]) for i in range(2)]
        att = [st.sb(f"att{i}", [P, NS, P]) for i in range(2)]
        v2 = [st.sb(f"v2{i}", [P, NS, DK]) for i in range(2)]
        x0 = st.sb("x0", [P, BH, 2, DK])
        us = st.sb("us", [P, BH, 2, DK])
        S = st.sb("S", [P, BH, 2, DK])
        o = st.sb("o", [P, BH, 2, DK])
        osq = st.sb("osq", [P, BH, 2, DK])
        ss = st.sb("ss", [P, NS])
        oT = st.sb("oT", [P, KT, TOK])
        y = [st.sb(f"y{i}", [P, BATCH, D]) for i in range(2)]
        stats = st.sb("stats", [P, BATCH, 6])
        mv = st.sb("mv", [P, BATCH, 2])
        rstd = st.sb("rstd", [P, BATCH])
        R = [st.ps(f"R{i}", [P, 4, P]) for i in range(4)]
        X = [st.ps(f"X{i}", [P, BH // 2, 2, DK]) for i in range(2)]
        Y = [st.ps(f"Y{i}", [P, BH // 2, 2, DK]) for i in range(2)]
        SI = Y[0][:, :, :, :].rearrange("p s r d -> p (s r) d")
        const, scales = keep["const"], keep["scales"]
        ident = const[:, C_ID:C_ID + P]
        REGION = {kind: (slice(0, P - n * CH), slice(n * CH, P)) for n, kind in enumerate("ABC", 1)}
        att_mask = const[:, C_ATT:C_ATT + P]

        def rounds(pre, tail):
            n, q, a, b, c = ([(kind, g, "act" if kind in "NAB" else "dve") for g in range(4)] for kind in "NQABC")
            t, w = ([(kind, g, "act" if kind == "T" else "dve") for g in range(2)] for kind in "TW")
            return (n if pre else []) + (t if tail else []) + (w if tail else []) + (q + a + b + c if pre else [])

        PRE, FULL, LAST = rounds(True, False), rounds(True, True), rounds(False, True)

        def used(seq, engine, n=None):
            return sum(e == engine for _, _, e in seq[:n])

        power_set, par_in, wo_done, s_zero, d_zero, edges_done = (
            st.sem(f"p3_{n}") for n in ("power_set", "par_in", "wo_done", "s_zero", "d_zero", "edges_done"))
        qk_in, kt_in, vt_in, x_in, mix_in, d_in = (st.pair(f"p3_{n}_in") for n in ("qk", "kt", "vt", "x", "mix", "d"))
        round_ready, dve_out, act_out = st.sem("p3_round_ready"), st.sem("p3_dve_out"), st.sem("p3_act_out")
        x_ready, x_done, y_ready, u_done = (st.sem(f"p3_{n}") for n in ("x_ready", "x_done", "y_ready", "u_done"))
        o_ready, s_ready, s_done, o_done = (st.sem(f"p3_{n}") for n in ("o_ready", "s_ready", "s_done", "o_done"))
        v2_done, direct_done, prep_done = st.sem("p3_v2_done"), st.sem("p3_direct_done"), st.sem("p3_prep_done")
        mixed, sq_done, ss_done, rs_done, on_done, st_done, pool_link = (
            st.sem(f"p3_{n}") for n in ("mixed", "sq_done", "ss_done", "rs_done", "on_done", "st_done", "pool_link"))
        var_done, rstd_done, x1_done = (st.sem(f"p3_{n}") for n in ("var_done", "rstd_done", "x1_done"))
        x1_stored = st.pair("p3_x1_stored")
        lt_in, second_in, lt_moved, t_zero, r_zero, terms_in = (
            st.sem(f"p3_{n}") for n in ("lt_in", "second_in", "lt_moved", "t_zero", "r_zero", "terms_in"))
        NPRE = len(PRE)
        MID = STEPS - 2

        def base(t, seq_count):
            pre, full = seq_count(PRE), seq_count(FULL)
            return (t - 1) * full + 2 * pre if isinstance(t, int) else t * full + (2 * pre - full)

        def dve_base(t):
            return base(t, lambda s: used(s, "dve"))

        def act_base(t):
            return base(t, lambda s: used(s, "act"))

        with nc.Block() as block:
            @block.sync
            def _(sp):
                def load(t, p):
                    sp.wait_ge(d_zero, 1 + p)
                    sp.wait_ge(t_zero, 1 + p)
                    for q in range(NQ):
                        part = slice(q * CH, q * CH + CH)
                        sp.dma_start(ddiag[p][part, :, part], io["d_s"][bass.ds(t * NS, NS), q].rearrange("s i j -> i s j")).then_inc(d_in[p], 16)
                        sp.dma_start(tdiag[p][part, :, part], io["t_s"][bass.ds(t * NS, NS), q].rearrange("s i j -> i s j")).then_inc(d_in[p], 16)
                    sp.dma_start(qk[p][:, :, :], row(io["qk_s"], t)).then_inc(qk_in[p], 16)
                    sp.dma_start(vtok[p][:, :, :, :].rearrange("p h b d -> p h (b d)"),
                                 io["v_s"][:, :, bass.ds(t + 1, 1), :, :].rearrange("h p o b d -> p h (o b d)")).then_inc(vt_in[p], 16)
                    sp.dma_start(ktok[p][:, :, :], row(io["k_s"], t)).then_inc(kt_in[p], 16)

                def load_mix(t, p):
                    for e in range(2):
                        sp.dma_start(mix[p][e * WIN:e * WIN + WIN, :, :].rearrange("m b (u d) -> m (b u) d", d=DK // 2),
                                     io["mix_s"][e, bass.ds(t, 1), :, :, :, :].rearrange("o b u m d -> m (o b u) d")
                                     ).then_inc(mix_in[p], 16)

                def load_x(t, p):
                    sp.dma_start(xres[p][:, :, :], io["x"][:, bass.ds(t * P, P), :].rearrange("b p d -> p b d")).then_inc(x_in[p], 16)

                def load_kk(t, dst, sem):
                    sp.dma_start(dst[:, :, :], io["kk_s"][:, bass.ds(t * NS, NS), :]).then_inc(sem, 16)

                def next_loads(t, p):
                    sp.wait_ge(s_ready, t + 1)
                    load_kk(t + 2, lt, lt_in)
                    load(t + 2, p)
                    sp.wait_ge(mixed, t + 1)
                    load_mix(t + 2, p)

                def store(t, p):
                    sp.wait_ge(x1_done, t + 1)
                    sp.dma_start(row(io["x1_s"], t), y[p][:, :, :]).then_inc(x1_stored[p], 16)

                load_kk(0, lt, lt_in)
                for t in range(2):
                    load(t, t)
                    load_mix(t, t)
                    load_x(t, t)
                    if t == 0:
                        sp.dma_start(wo_raw[:, :, :], io["w_o"]).then_inc(par_in, 16)
                        sp.dma_start(norm_w[:, :], io["norm_w"]).then_inc(par_in, 16)
                        load_kk(1, att[1], second_in)
                next_loads(0, 0)
                with sp.Fori(0, MID // 2 - 1) as i:
                    for j in range(2):
                        t = i * 2 + 1 + j
                        next_loads(t, 1 - j)
                        store(t - 1, j)
                        load_x(t + 1, j)
                t = MID - 1
                next_loads(t, 1)
                for t in range(MID - 1, MID + 1):
                    store(t - 1, (t - 1) % 2)
                    load_x(t + 1, (t + 1) % 2)
                for t in range(STEPS - 2, STEPS):
                    store(t, t % 2)
                for p in range(2):
                    sp.wait_ge(x1_stored[p], 8 * STEPS + 16)

            @block.tensor
            def _(pe):
                def bank_free(seq, r, dve0, act0):
                    if r >= 4:
                        before, engine = seq[:r - 3], seq[r - 4][2]
                        pe.wait_ge(dve_out if engine == "dve" else act_out, (dve0 if engine == "dve" else act0) + used(before, engine))
                    elif not isinstance(dve0, int) or dve0:
                        pe.wait_ge(dve_out, dve0 - 3 + r)

                def empties(seq, kind, g):
                    r = next(i for i, x in enumerate(seq) if x[:2] == (kind, g))
                    return used(seq, seq[r][2], r + 1)

                def run(kinds, seq, t, p, n, tp, dve0, act0):
                    for r, (kind, g, _) in enumerate(seq):
                        if kind not in kinds:
                            continue
                        bank = R[r % 4]
                        if g == 0:
                            if kind == "Q":
                                pe.wait_ge(qk_in[p], n * 16 + 16)
                            if kind == "N":
                                if isinstance(t, int) and t < 2:
                                    pe.wait_ge(lt_moved if t else lt_in, 1 if t else 16)
                                else:
                                    pe.wait_ge(lt_in, t * 16)
                                pe.wait_ge(d_in[p], n * (32 * NQ) + 32 * NQ)
                            if kind == "T":
                                pe.wait_ge(on_done, tp + 1)
                        before = {"A": "N", "B": "A", "C": "B", "W": "T"}.get(kind)
                        if before:
                            for h in [g] if kind != "W" else ([1] if g == 0 else []):
                                engine = seq[next(i for i, x in enumerate(seq) if x[:2] == (before, h))][2]
                                pe.wait_ge(dve_out if engine == "dve" else act_out,
                                           (dve0 if engine == "dve" else act0) + empties(seq, before, h))
                        bank_free(seq, r, dve0, act0)
                        par, half = g // 2, g % 2
                        if kind in "NQABC":
                            rows_out, cols_out = REGION.get(kind, (slice(0, P), slice(0, P - CH)))
                            for j in range(4):
                                s = half * 4 + j
                                b, hh = s // KT, s % KT
                                c = par * BH + s
                                if kind == "Q":
                                    rows = slice(64 * par, 64 * par + DK)
                                    left = qk[p][rows, KT + hh, b * P:b * P + P]
                                    right = qk[p][rows, hh, b * P:b * P + P]
                                    out = bank[:, j, :]
                                else:
                                    left = (lt if kind == "N" else nmat)[:, c, rows_out]
                                    right = {"N": ddiag[p], "A": tdiag[p], "B": r1, "C": r2}[kind][:, c, cols_out]
                                    out = bank[rows_out, j, cols_out]
                                last = nc.tensor.matmul(out, left, right, start=True, stop=True)
                        elif kind == "T":
                            for b in range(BATCH):
                                last = nc.tensor.transpose(bank[:, b, :], o[:, b * KT + g, :, :].rearrange("p r d -> p (r d)"), ident)
                        else:
                            for j in range(2):
                                b = 2 * g + j
                                for hh in range(KT):
                                    last = nc.tensor.matmul(bank[:, 2 * j:2 * j + 2, :], oT[:, hh, b * P:b * P + P], wo[:, hh, :],
                                                            start=(hh == 0), stop=(hh == KT - 1))
                        last.then_inc(round_ready, 1)

                def from_state(t, p):
                    pe.wait_ge(s_done, t * 2 + 2)
                    pe.wait_ge(o_done, t * 2 + 2)
                    for s in range(BH):
                        b, hh = s // KT, s % KT
                        last = nc.tensor.matmul(X[s // 4][:, s % 4, :, :], qk[p][:, KT + hh, b * P:b * P + P],
                                                S[:, s, :, :], start=True, stop=True)
                        if s % 4 == 3:
                            last.then_inc(x_ready, 1)

                def solve(t, p):
                    for i in range(2):
                        pe.wait_ge(x_done, t * 2 + i + 1)
                        for s in range(4 * i, 4 * i + 4):
                            for par in range(2):
                                last = nc.tensor.matmul(Y[i][:, s % 4, par, :], tt[p][:, par * BH + s, :], x0[:, s, par, :],
                                                        start=True, stop=True)
                        last.then_inc(y_ready, 1)

                def outputs(t, p, n):
                    pe.wait_ge(u_done, t * 2 + 2)
                    for s in range(BH):
                        b, hh = s // KT, s % KT
                        nc.tensor.matmul(X[s // 4][:, s % 4, :, :], qk[p][:, hh, b * P:b * P + P], S[:, s, :, :],
                                         start=True, stop=False)
                        for par in range(2):
                            last = nc.tensor.matmul(X[s // 4][:, s % 4, par, :], att[p][:, par * BH + s, :], us[:, s, par, :],
                                                    start=False, stop=(par == 1))
                        if s % 4 == 3:
                            last.then_inc(o_ready, 1)
                    pe.wait_ge(kt_in[p], n * 16 + 16)
                    for s in range(BH):
                        b, hh = s // KT, s % KT
                        for par in range(2):
                            c = hh * P + par * DK
                            last = nc.tensor.matmul(SI[64 * par:64 * par + DK, s, :], ktok[p][:, b, c:c + DK],
                                                    us[:, s, par, :], start=True, stop=True)
                    last.then_inc(s_ready, 1)

                pe.wait_ge(s_zero, 1)

                def step(t, p, n, nn, seq, dve0, act0, last_c):
                    rest = (seq, t + 1, 1 - p, nn, t - 1, dve0, act0)
                    from_state(t, p)
                    run("N", *rest)
                    run("T", *rest)
                    pe.wait_ge(edges_done, t + 1)
                    pe.wait_ge(dve_out, last_c)
                    solve(t, p)
                    run("W", *rest)
                    outputs(t, p, n)
                    run("QABC", *rest)

                run("NQABC", PRE, 0, 0, 0, 0, 0, 0)
                d, a = used(PRE, "dve"), used(PRE, "act")
                step(0, 0, 0, 0, PRE, d, a, d)
                pe.wait_ge(wo_done, 1)
                with pe.Fori(0, MID // 2) as i:
                    for j in range(2):
                        t = i * 2 + 1 + j
                        step(t, 1 - j, i + j, i + 1, FULL, dve_base(t), act_base(t), dve_base(t))
                t = STEPS - 1
                step(t, 1, t // 2, 0, LAST, dve_base(t), act_base(t), dve_base(t))
                d, a = dve_base(t) + used(LAST, "dve"), act_base(t) + used(LAST, "act")
                pe.wait_ge(dve_out, d)
                pe.wait_ge(act_out, a)
                pe.wait_ge(on_done, STEPS)
                for g in range(2):
                    for b in range(BATCH):
                        last = nc.tensor.transpose(R[g][:, b, :], o[:, b * KT + g, :, :].rearrange("p r d -> p (r d)"), ident)
                    last.then_inc(round_ready, 1)
                pe.wait_ge(act_out, a + 2)
                for g in range(2):
                    for j in range(2):
                        b = 2 * g + j
                        for hh in range(KT):
                            last = nc.tensor.matmul(R[2 + g][:, 2 * j:2 * j + 2, :], oT[:, hh, b * P:b * P + P], wo[:, hh, :],
                                                    start=(hh == 0), stop=(hh == KT - 1))
                    last.then_inc(round_ready, 1)

            def arrived(eng, seq, kind, g, round0):
                r = next(i for i, x in enumerate(seq) if x[:2] == (kind, g))
                eng.wait_ge(round_ready, round0 + r + 1)
                return R[r % 4]

            def round_base(t):
                return base(t, len)

            @block.scalar
            def _(act):
                def copy_rounds(kind, seq, round0):
                    for g in range(2 if kind == "T" else 4):
                        bank = arrived(act, seq, kind, g, round0)
                        c = slice(g * 4, g * 4 + 4)
                        rows, cols = REGION.get(kind, (slice(0, P), slice(0, P - CH if kind == "N" else P)))
                        if kind == "T":
                            dst = oT[:, g, :].rearrange("p (b n) -> p b n", b=BATCH)
                        else:
                            dst = {"N": nmat, "A": r1, "B": r2}[kind][rows, c, cols]
                        nc.scalar.activation(dst, bank[rows, :, cols], ACT.Copy).then_inc(act_out, 1)

                def edges(t, p):
                    for end in (slice(0, CH), slice(P - CH, P)):
                        last = nc.scalar.activation(tt[p][end, :, end], tdiag[p][end, :, end], ACT.Copy)
                    last.then_inc(edges_done, 1)

                def step(t, p, seq, round0, pre, tail):
                    if pre:
                        copy_rounds("N", seq, round0)
                    if tail:
                        copy_rounds("T", seq, round0)
                    for i in range(2):
                        act.wait_ge(y_ready, t * 2 + i + 1)
                        nc.scalar.activation(us[:, 4 * i:4 * i + 4, :, :], Y[i][:, :, :, :], ACT.Copy).then_inc(u_done, 1)
                    if pre:
                        edges(t + 1, p)
                    act.wait_ge(mixed, t + 1)
                    nc.scalar.activation(osq[:, :, :, :], o[:, :, :, :], ACT.Square).then_inc(sq_done, 1)
                    if pre:
                        copy_rounds("A", seq, round0)
                        copy_rounds("B", seq, round0)

                copy_rounds("N", PRE, 0)
                act.wait_ge(d_zero, 4)
                act.wait_ge(r_zero, 2)
                copy_rounds("A", PRE, 0)
                copy_rounds("B", PRE, 0)
                edges(0, 0)
                step(0, 1, PRE, NPRE, True, False)
                with act.Fori(0, MID // 2) as i:
                    for j in range(2):
                        t = i * 2 + 1 + j
                        step(t, j, FULL, round_base(t), True, True)
                t = STEPS - 1
                step(t, 0, LAST, round_base(t), False, True)
                copy_rounds("T", LAST, round_base(t) + len(LAST))

            @block.vector
            def _(dve):
                for p in range(2):
                    nc.vector.memset(tdiag[p][:, :, :], 0.0).then_inc(t_zero, 1)
                nc.vector.memset(S[:, :, :, :], 0.0).then_inc(s_zero, 1)
                dve.sem_inc(s_done, 2)
                dve.sem_inc(o_done, 2)
                for p in range(2):
                    dve.sem_inc(x1_stored[p], 16)

                def add_term(kind, seq, act0, t, p):
                    rows, cols = REGION[kind]
                    for half in range(2):
                        c = slice(8 * half, 8 * half + 8)
                        if kind == "B":
                            dve.wait_ge(terms_in, t * 4 + half + 1)
                        n = next(i for i, x in enumerate(seq) if x[:2] == (kind, 2 * half + 1))
                        dve.wait_ge(act_out, act0 + used(seq, "act", n + 1))
                        if kind == "A":
                            last = nc.vector.tensor_tensor(tt[p][rows, c, cols], tdiag[p][rows, c, cols], r1[rows, c, cols], ALU.subtract)
                        else:
                            last = nc.vector.tensor_tensor(tt[p][rows, c, cols], tt[p][rows, c, cols], r2[rows, c, cols], ALU.add)
                        last.then_inc(terms_in, 1)

                def evacuate(kind, seq, round0, t, p):
                    for g in range(4):
                        bank = arrived(dve, seq, kind, g, round0)
                        c = slice(g * 4, g * 4 + 4)
                        if kind == "Q":
                            last = nc.vector.tensor_tensor(att[p][:, c, :], bank[:, :, :], bcast_mid(att_mask, 4), ALU.mult)
                        else:
                            rows, cols = REGION[kind]
                            if g == 0:
                                dve.wait_ge(terms_in, t * 4 + 4)
                            last = nc.vector.tensor_tensor(tt[p][rows, c, cols], tt[p][rows, c, cols], bank[rows, :, cols],
                                                           ALU.subtract)
                        last.then_inc(dve_out, 1)

                def right_side(t, p):
                    dve.wait_ge(prep_done, t + 1)
                    for i in range(2):
                        dve.wait_ge(x_ready, t * 2 + i + 1)
                        nc.vector.tensor_tensor(x0[:, 4 * i:4 * i + 4, :, :].rearrange("p s r d -> p (s r) d"), v2[p][:, 8 * i:8 * i + 8, :],
                                                X[i][:, :, :, :].rearrange("p s r d -> p (s r) d"), ALU.subtract).then_inc(x_done, 1)

                def outputs(t, p):
                    for i in range(2):
                        dve.wait_ge(o_ready, t * 2 + i + 1)
                        c3 = scales[:, 1, bass.ds(t, 1), 8 * i:8 * i + 8].rearrange("p o s -> p (o s)")
                        nc.vector.tensor_tensor(o[:, 4 * i:4 * i + 4, :, :].rearrange("p s r d -> p (s r) d"),
                                                X[i][:, :, :, :].rearrange("p s r d -> p (s r) d"), bcast(c3, DK), ALU.mult).then_inc(o_done, 1)
                    dve.wait_ge(s_ready, t + 1)
                    for par in range(2):
                        rows = slice(64 * par, 64 * par + DK)
                        nc.vector.tensor_tensor(S[rows, :, par, :], S[rows, :, par, :], SI[rows, :, :], ALU.add).then_inc(s_done, 1)
                    dve.wait_ge(o_done, t * 2 + 4)
                    of = o[:, :, :, :].rearrange("p s r d -> p (s r d)")
                    nc.vector.tensor_tensor(of, of, mix[p][:, :, :].rearrange("p b d -> p (b d)"), ALU.add).then_inc(mixed, 1)

                def head_sums(t):
                    dve.wait_ge(sq_done, t + 1)
                    nc.vector.tensor_reduce(ss[:, :], osq[:, :, :, :].rearrange("p s r d -> p (s r) d"), AX.X,
                                            ALU.add).then_inc(ss_done, 1)

                def head_norm(t):
                    dve.wait_ge(rs_done, t + 1)
                    of = o[:, :, :, :].rearrange("p s r d -> p (s r) d")
                    nc.vector.scalar_tensor_tensor(out=of, in0=of, scalar=float(DK) ** 0.5, in1=bcast(ss[:, :], DK),
                                                   op0=ALU.mult, op1=ALU.mult).then_inc(on_done, 1)

                def residual(t, p, n, seq, round0):
                    dve.wait_ge(x_in[p], n * 16 + 16)
                    dve.wait_ge(x1_stored[p], n * 16 + 16)
                    for g in range(2):
                        bank = arrived(dve, seq, "W", g, round0)
                        nc.vector.tensor_tensor(y[p][:, 2 * g:2 * g + 2, :], bank[:, :, :].rearrange("p (b k) d -> p b (k d)", b=2),
                                                xres[p][:, 2 * g:2 * g + 2, :], ALU.add).then_inc(dve_out, 1)

                def spread(t, p, out0):
                    dve.wait_ge(dve_out, out0)
                    for b in range(BATCH):
                        last = nc.vector.bn_stats(stats[:, b, :], y[p][:, b, :])
                    last.then_inc(st_done, 1)

                def spread_sum(t):
                    dve.wait_ge(par_in, 32)
                    dve.wait_ge(st_done, t + 1)
                    for b in range(BATCH):
                        last = nc.vector.bn_aggr(mv[:, b, :], stats[:, b, :])
                    last.then_inc(var_done, 1)

                def layer_norm(t, p):
                    dve.wait_ge(rstd_done, t + 1)
                    for b in range(BATCH):
                        last = nc.vector.tensor_scalar(y[p][:, b, :], y[p][:, b, :], mv[:, b, 0:1], rstd[:, b:b + 1],
                                                       ALU.subtract, ALU.mult)
                    last.then_inc(x1_done, 1)

                def step(t, p, ntail, seq, round0, dve0, act0, pre, tail):
                    right_side(t, p)
                    if tail:
                        residual(t - 1, 1 - p, ntail, seq, round0)
                    outputs(t, p)
                    if pre:
                        evacuate("Q", seq, round0, t + 1, 1 - p)
                    head_sums(t)
                    if tail:
                        spread(t - 1, 1 - p, dve0 + used(seq, "dve", 1 + next(i for i, x in enumerate(seq) if x[:2] == ("W", 1))))
                    if pre:
                        add_term("A", seq, act0, t + 1, 1 - p)
                    if tail:
                        spread_sum(t - 1)
                    if pre:
                        add_term("B", seq, act0, t + 1, 1 - p)
                    if pre:
                        evacuate("C", seq, round0, t + 1, 1 - p)
                    head_norm(t)
                    if tail:
                        layer_norm(t - 1, 1 - p)

                for buf in (r1, r2):
                    nc.vector.memset(buf[:, :, :], 0.0).then_inc(r_zero, 1)
                for kind in "QABC":
                    if kind in "AB":
                        if kind == "A":
                            dve.wait_ge(d_zero, 4)
                        add_term(kind, PRE, 0, 0, 0)
                    else:
                        evacuate(kind, PRE, 0, 0, 0)
                    if kind == "C":
                        dve.wait_ge(par_in, 32)
                        nc.vector.tensor_scalar(wo[:, :, :], wo_raw[:, :, :], norm_w[:, 0:1], None, ALU.mult).then_inc(wo_done, 1)
                    if kind == "A":
                        dve.wait_ge(act_out, 4)
                        dve.wait_ge(second_in, 16)
                        nc.vector.tensor_copy(lt[:, :, :], att[1][:, :, :]).then_inc(lt_moved, 1)
                step(0, 0, 0, PRE, NPRE, used(PRE, "dve"), used(PRE, "act"), True, False)
                with dve.Fori(0, MID // 2) as i:
                    for j in range(2):
                        t = i * 2 + 1 + j
                        step(t, 1 - j, i, FULL, round_base(t), dve_base(t), act_base(t), True, True)
                t = STEPS - 1
                step(t, 1, (t - 1) // 2, LAST, round_base(t), dve_base(t), act_base(t), False, True)
                residual(t, 1, t // 2, LAST, round_base(t) + len(LAST))
                spread(t, 1, dve_base(t) + 2 * used(LAST, "dve"))
                spread_sum(t)
                layer_norm(t, 1)

            @block.gpsimd
            def _(pool):
                for buf in (ddiag[0], ddiag[1], tt[0], tt[1]):
                    nc.gpsimd.memset(buf[:, :, :], 0.0).then_inc(d_zero, 1)
                nc.gpsimd.memset(head_eps[:, :], DK * LN_EPS)
                nc.gpsimd.memset(ln_eps[:, :], LN_EPS)
                nc.gpsimd.memset(power[:, :], -0.5).then_inc(power_set, 1)
                pool.wait_ge(power_set, 1)

                def prep(t, p, n):
                    pool.wait_ge(vt_in[p], n * 16 + 16)
                    sk = scales[:, 0, bass.ds(t, 1), :].rearrange("p o s -> p (o s)")
                    v = vtok[p][:, :, :, :].rearrange("p h b d -> p b h d")
                    nc.gpsimd.tensor_tensor(v2[p][:, :, :].rearrange("p (b h) d -> p b h d", h=HEADS), v,
                                            bcast(sk.rearrange("p (b h) -> p b h", h=HEADS), DK), ALU.mult).then_inc(v2_done, 1)
                    p4 = keep["pw"][:, :, 4, bass.ds(t * BATCH, BATCH)].rearrange("p h b -> p b h")
                    pool.wait_ge(v2_done, t + 1)
                    nc.gpsimd.tensor_tensor(v, v, bcast(p4, DK), ALU.mult).then_inc(direct_done, 1)
                    terms = mix[p][:, :, :].rearrange("p b (h d) -> p b h d", h=HEADS)
                    pool.wait_ge(mix_in[p], n * 32 + 32)
                    pool.wait_ge(direct_done, t + 1)
                    nc.gpsimd.tensor_tensor(terms, terms, v, ALU.add).then_inc(prep_done, 1)

                def norm(t, links):
                    pool.wait_ge(ss_done, t + 1)
                    nc.gpsimd.tensor_tensor(ss[:, :], ss[:, :], head_eps[:, :], ALU.add).then_inc(pool_link, 1)
                    pool.wait_ge(pool_link, links)
                    nc.gpsimd.tensor_tensor(ss[:, :], ss[:, :], power[:, :], ALU.pow).then_inc(rs_done, 1)

                def tail(t, links):
                    pool.wait_ge(var_done, t + 1)
                    nc.gpsimd.tensor_tensor(rstd[:, :], mv[:, :, 1:2].rearrange("p b o -> p (b o)"), ln_eps[:, :],
                                            ALU.add).then_inc(pool_link, 1)
                    pool.wait_ge(pool_link, links)
                    nc.gpsimd.tensor_tensor(rstd[:, :], rstd[:, :], power[:, 0:BATCH], ALU.pow).then_inc(rstd_done, 1)

                prep(0, 0, 0)
                prep(1, 1, 0)
                norm(0, 1)
                with pool.Fori(0, MID // 2) as i:
                    for j in range(2):
                        t = i * 2 + 1 + j
                        pool.wait_ge(x_done, t * 2)
                        prep(t + 1, j, i + 1)
                        norm(t, t * 2)
                        tail(t - 1, t * 2 + 1)
                t = STEPS - 1
                norm(t, t * 2)
                tail(t - 1, t * 2 + 1)
                tail(t, t * 2 + 2)


def round_weights(nc, sems, io, wr, flag, total):
    st = Stage(nc, sems)
    with st.ctx:
        CW = 2048
        NCH = W_END // CW
        NRAWS = 4
        raw = [st.sb(f"wraw{i}", [P, CW]) for i in range(NRAWS)]
        diff = st.sb("wdiff", [P, CW])
        worst = st.sb("worst", [P, NCH])
        most = st.sb("most", [P, 1])
        ones = st.sb("ones", [P, 1])
        raw_in = [st.sem(f"p4_raw_in{i}") for i in range(NRAWS)]
        rounded, diff_done, most_done, total_ready, flag_done, flag_stored = (
            st.sem(f"p4_{n}") for n in ("rounded", "diff_done", "most_done", "total_ready", "flag_done", "flag_stored"))

        with nc.Block() as block:
            @block.sync
            def _(sp):
                for c in range(NCH):
                    if c >= NRAWS:
                        sp.wait_ge(diff_done, c - NRAWS + 1)
                    sp.dma_start(raw[c % NRAWS][:, :], io["ffn_w"][:, c * CW:c * CW + CW]).then_inc(raw_in[c % NRAWS], 16)
                sp.wait_ge(flag_done, 1)
                sp.dma_start(io["flag_s"], flag[:, :]).then_inc(flag_stored, 16)
                sp.wait_ge(flag_stored, 16)

            @block.vector
            def _(dve):
                nc.vector.memset(ones[:, :], 1.0)
                for c in range(NCH):
                    dve.wait_ge(rounded, c + 1)
                    if c:
                        dve.wait_ge(diff_done, c)
                    nc.vector.scalar_tensor_tensor(
                        out=diff[:, :], in0=raw[c % NRAWS][:, :], scalar=1.0, in1=wr[:, c * CW:c * CW + CW].bitcast(f32),
                        op0=ALU.mult, op1=ALU.not_equal, accum_out=worst[:, c:c + 1]).then_inc(diff_done, 1)
                dve.wait_ge(diff_done, NCH)
                nc.vector.tensor_reduce(most[:, :], worst[:, :], AX.X, ALU.add).then_inc(most_done, 1)

            @block.tensor
            def _(pe):
                pe.wait_ge(most_done, 1)
                nc.tensor.matmul(total, most[:, :], ones[:, :], start=True, stop=True).then_inc(total_ready, 1)

            @block.scalar
            def _(act):
                for c in range(NCH):
                    act.wait_ge(raw_in[c % NRAWS], 16 * (c // NRAWS) + 16)
                    nc.scalar.activation(wr[:, c * CW:c * CW + CW], raw[c % NRAWS][:, :], ACT.Copy).then_inc(rounded, 1)
                act.wait_ge(total_ready, 1)
                nc.scalar.activation(flag[:, :], total, ACT.Copy).then_inc(flag_done, 1)


def ffn(nc, sems, io, keep):
    outer = Stage(nc, sems)
    with outer.ctx:
        flag = outer.sb("flag", [1, 1])
        scol = outer.sb("scol", [P, 4 * HT])
        srow = outer.sb("srow", [P, D])
        power = outer.sb("power5", [P, BATCH])
        ln_eps = outer.sb("ln_eps5", [P, BATCH])
        x1 = [outer.sb(f"x1{i}", [P, BATCH, D]) for i in range(2)]
        z = [outer.sb(f"z{i}", [P, BATCH, D]) for i in range(2)]
        gate = [outer.sb(f"gate{i}", [P, TOK]) for i in range(2)]
        stats = outer.sb("stats5", [P, BATCH, 6])
        mv = outer.sb("mv5", [P, BATCH, 2])
        rstd = outer.sb("rstd5", [P, BATCH])
        B = [outer.ps(f"B{i}", [P, TOK]) for i in range(4)]
        O = outer.ps("O", [P, BATCH, D])
        T = outer.ps("T", [P, KT, TOK])
        ident = keep["const"][:, C_ID:C_ID + P]
        fast = Stage(nc, sems)
        with fast.ctx:
            wr = fast.sb("wr", [P, W_END], f32r)
            round_weights(nc, sems, io, wr, flag, B[0][0:1, 0:1])
            xh, xl = fast.sb("xh", [P, KT, TOK], f32r), fast.sb("xl", [P, KT, TOK], f32r)
            sets = [[fast.sb(f"act{i}{n}", [P, HT, TOK], f32r) for n in "hl"] for i in range(2)]
            yb = [fast.sb(f"yb{i}", [P, TOK]) for i in range(3)]
        slow = Stage(nc, sems)
        with slow.ctx:
            wblk = [slow.sb(f"wblk{i}", [P, HT, P]) for i in range(2)]
            xf = slow.sb("xf", [P, KT, TOK])
            full = [slow.sb(f"full{i}", [P, HT, TOK]) for i in range(2)]

        par_in, power_set = outer.sem("p5_par_in"), outer.sem("p5_power_set")
        x_in, out_stored, w_in = outer.pair("p5_x_in"), outer.pair("p5_out_stored"), outer.pair("p5_w_in")
        (tr_ready, xh_done, x_split, bank_ready, gate_done, f_ready, hi_done, lo_done, o_ready, o_free, z_done,
         st_done, var_done, rs_link, rstd_done, out_done, blk_used) = (outer.sem(f"p5_{n}") for n in (
             "tr_ready", "xh_done", "x_split", "bank_ready", "gate_done", "f_ready", "hi_done", "lo_done", "o_ready",
             "o_free", "z_done", "st_done", "var_done", "rs_link", "rstd_done", "out_done", "blk_used"))
        BLOCKS = 3 * HT
        F0 = 4
        FILLS = 4 * HT
        WBLOCKS = 3 * HT + KT

        def either(eng, emit):
            inexact = eng.value_load(io["flag_s"].bitcast(i32), min_val=0, max_val=2 ** 31 - 1)
            with eng.If(inexact != 0):
                emit(True)
            with eng.Else():
                emit(False)

        with nc.Block() as block:
            @block.sync
            def _(sp):
                sp.dma_start(scol[:, :], io["scol"]).then_inc(par_in, 16)
                src = io["srow"]
                sp.dma_start(srow[:, :], bass.AP(tensor=src.tensor, offset=0, ap=[[0, P], [1, D]])).then_inc(par_in, 16)

                def load(t, p):
                    sp.dma_start(x1[p][:, :, :], row(io["x1_s"], t)).then_inc(x_in[p], 16)

                def store(t, p):
                    sp.wait_ge(out_done, t + 1)
                    sp.dma_start(io["out"][:, bass.ds(t * P, P), :].rearrange("b p d -> p b d"), z[p][:, :, :]).then_inc(out_stored[p], 16)

                def stream(t):
                    w = io["ffn_w"]
                    for n in range(WBLOCKS):
                        sp.wait_ge(blk_used, t * WBLOCKS + n + 1)
                        if n < HT:
                            for j, base in enumerate((W1, W2)):
                                sp.dma_start(wblk[n % 2][:, j * KT:j * KT + KT, :],
                                             w[:, base:base + KT * HID].rearrange("p (k m) -> p k m", k=KT)[:, :, n * P:n * P + P]
                                             ).then_inc(w_in[n % 2], 16)
                        else:
                            base, width, m = ((H1, HID, n - HT) if n < 2 * HT else (H2, HID, n - 2 * HT) if n < 3 * HT
                                              else (W3, D, n - 3 * HT))
                            sp.dma_start(wblk[n % 2][:, :, :], w[:, base:base + HT * width].rearrange("p (k m) -> p k m", k=HT)[:, :, m * P:m * P + P]
                                         ).then_inc(w_in[n % 2], 16)

                def emit(general):
                    if general:
                        stream(0)
                    with sp.Fori(0, STEPS // 2 - 1) as i:
                        for p in range(2):
                            if general:
                                stream(i * 2 + p + 1)
                            store(i * 2 + p, p)
                            load(i * 2 + p + 2, p)
                    if general:
                        stream(STEPS - 1)
                    for p in range(2):
                        store(STEPS - 2 + p, p)

                load(0, 0)
                load(1, 1)
                either(sp, emit)
                for p in range(2):
                    sp.wait_ge(out_stored[p], 8 * STEPS + 16)

            @block.tensor
            def _(pe):
                def turn(p, n):
                    pe.wait_ge(x_in[p], n * 16 + 16)
                    for k in range(KT):
                        for b in range(BATCH):
                            last = nc.tensor.transpose(T[:, k, b * P:b * P + P], x1[p][:, b, k * P:k * P + P], ident)
                    last.then_inc(tr_ready, 1)

                def layers(t, general):
                    def weights_in(n):
                        per = HT + HT + KT // 2
                        before = n // 2 * 2 if n < HT else HT + (n - HT) // 2
                        pe.wait_ge(w_in[n % 2], t * (16 * per) + 16 * (before + (2 if n < HT else 1)))

                    def block_rhs(layer, k):
                        if layer == 0:
                            return [xf[:, k, :]] if general else [xh[:, k, :], xl[:, k, :]]
                        s = (layer - 1) % 2
                        return [full[s][:, k, :]] if general else [sets[s][0][:, k, :], sets[s][1][:, k, :]]

                    pe.wait_ge(x_split, t + 1)
                    for layer in range(3):
                        kts = HT if layer else KT
                        for m in range(HT):
                            n = layer * HT + m
                            if general:
                                weights_in(n)
                            for j in range(1 if layer else 2):
                                slot = 2 * m + j if layer == 0 else (layer + 1) * HT + m
                                if layer == 0:
                                    pe.wait_ge(f_ready, F0 + t * BLOCKS + (m - 1 if m >= 2 else 2 * m - 2))
                                elif layer == 1 and m == 0:
                                    pe.wait_ge(f_ready, F0 + t * BLOCKS + HT - 1)
                                elif m >= 4 or layer == 2:
                                    pe.wait_ge(f_ready, F0 + t * BLOCKS + n - 3)
                                base, width = ((W1, W2)[j], HID) if layer == 0 else ((H1, H2)[layer - 1], HID)
                                for k in range(kts):
                                    if layer and m == 0:
                                        pe.wait_ge(f_ready if general else lo_done, (F0 if general else 0) + t * BLOCKS + (layer - 1) * HT + k + 1)
                                    c = base + k * width + m * P
                                    w = wblk[n % 2][:, j * KT + k, :] if general else wr[:, c:c + P]
                                    parts = block_rhs(layer, k)
                                    for i, part in enumerate(parts):
                                        last = nc.tensor.matmul(B[slot % 4][:, :], w, part, start=(k == 0 and i == 0),
                                                                stop=(k == kts - 1 and i == len(parts) - 1))
                                last.then_inc(bank_ready, 1)
                            if general:
                                pe.drain().then_inc(blk_used, 1)

                def last_layer(t, general):
                    pe.wait_ge(o_free, t + 1)
                    if general:
                        pe.wait_ge(f_ready, F0 + t * BLOCKS + BLOCKS)
                        per = HT + HT + KT // 2
                        for half in range(KT):
                            n = 3 * HT + half
                            pe.wait_ge(w_in[n % 2], t * (16 * per) + 16 * (HT + (n - HT) // 2 + 1))
                            for b in range(BATCH):
                                for k in range(HT):
                                    last = nc.tensor.matmul(O[:, b, half * P:half * P + P], full[0][:, k, b * P:b * P + P],
                                                            wblk[n % 2][:, k, :], start=(k == 0), stop=(k == HT - 1))
                            pe.drain().then_inc(blk_used, 1)
                    else:
                        for first in range(2):
                            for k in range(HT):
                                if first == 0:
                                    pe.wait_ge(lo_done, t * BLOCKS + 2 * HT + k + 1)
                                for i in range(2):
                                    for b in (first, first + 2):
                                        last = nc.tensor.matmul(O[:, b, :], sets[0][i][:, k, b * P:b * P + P],
                                                                wr[:, W3 + k * D:W3 + k * D + D], start=(k == 0 and i == 0),
                                                                stop=(k == HT - 1 and i == 1))
                    last.then_inc(o_ready, 1) if not general else pe.drain().then_inc(o_ready, 1)

                def emit(general):
                    with pe.Fori(0, STEPS // 2 - 1) as i:
                        for p in range(2):
                            layers(i * 2 + p, general)
                            turn(1 - p, i + p)
                            last_layer(i * 2 + p, general)
                    layers(STEPS - 2, general)
                    turn(1, STEPS // 2 - 1)
                    last_layer(STEPS - 2, general)
                    layers(STEPS - 1, general)
                    last_layer(STEPS - 1, general)

                turn(0, 0)
                either(pe, emit)

            @block.scalar
            def _(act):
                act.wait_ge(par_in, 32)

                def split(t, general):
                    act.wait_ge(tr_ready, t + 1)
                    nc.scalar.activation((xf if general else xh)[:, :, :], T[:, :, :], ACT.Copy).then_inc(x_split if general else xh_done, 1)

                def high(t, m):
                    act.wait_ge(f_ready, F0 + t * BLOCKS + m + 1)
                    nc.scalar.activation(sets[0][0][:, m, :], yb[m % 3][:, :], ACT.Copy).then_inc(hi_done, 1)

                def layers(t, general):
                    for m in range(HT):
                        act.wait_ge(bank_ready, t * FILLS + 2 * m + 1)
                        act.wait_ge(f_ready, F0 + t * BLOCKS + (m - 1 if m >= 2 else 2 * m - 2))
                        nc.scalar.activation(gate[m % 2][:, :], B[2 * m % 4][:, :], ACT.Silu, scale=scol[:, m:m + 1]).then_inc(gate_done, 1)
                        if not general and m:
                            high(t, m - 1)
                    if not general:
                        high(t, HT - 1)
                    for layer in (1, 2):
                        for m in range(HT):
                            slot = (layer + 1) * HT + m
                            n = layer * HT + m
                            act.wait_ge(bank_ready, t * FILLS + slot + 1)
                            if not general:
                                act.wait_ge(lo_done, t * BLOCKS + n - 2)
                            dst = full[layer % 2][:, m, :] if general else yb[n % 3][:, :]
                            last = nc.scalar.activation(dst, B[slot % 4][:, :], ACT.Gelu, scale=scol[:, slot:slot + 1])
                            if not general:
                                last = nc.scalar.activation(sets[layer % 2][0][:, m, :], B[slot % 4][:, :], ACT.Gelu,
                                                            scale=scol[:, slot:slot + 1])
                            last.then_inc(f_ready, 1)

                def emit(general):
                    split(0, general)
                    with act.Fori(0, STEPS - 1) as t:
                        layers(t, general)
                        split(t + 1, general)
                    layers(STEPS - 1, general)

                either(act, emit)

            @block.vector
            def _(dve):
                dve.wait_ge(par_in, 32)
                dve.sem_inc(f_ready, F0)
                dve.sem_inc(o_free, 1)
                dve.sem_inc(blk_used, 2)
                for p in range(2):
                    dve.sem_inc(out_stored[p], 16)

                def split(t):
                    dve.wait_ge(xh_done, t + 1)
                    nc.vector.tensor_tensor(xl[:, :, :], T[:, :, :], xh[:, :, :].bitcast(f32), ALU.subtract).then_inc(x_split, 1)

                def low(t, n, s, m):
                    if n < HT:
                        dve.wait_ge(hi_done, t * HT + n + 1)
                    else:
                        dve.wait_ge(f_ready, F0 + t * BLOCKS + n + 1)
                    nc.vector.tensor_tensor(sets[s][1][:, m, :], yb[n % 3][:, :], sets[s][0][:, m, :].bitcast(f32),
                                            ALU.subtract).then_inc(lo_done, 1)

                def layers(t, general, after_first):
                    for m in range(HT):
                        dve.wait_ge(gate_done, t * HT + m + 1)
                        dve.wait_ge(bank_ready, t * FILLS + 2 * m + 2)
                        if not general and m >= 3:
                            dve.wait_ge(lo_done, t * BLOCKS + m - 2)
                        dst = full[0][:, m, :] if general else yb[m % 3][:, :]
                        nc.vector.scalar_tensor_tensor(out=dst, in0=B[(2 * m + 1) % 4][:, :], scalar=scol[:, HT + m:HT + m + 1],
                                                       in1=gate[m % 2][:, :], op0=ALU.mult, op1=ALU.mult).then_inc(f_ready, 1)
                        if not general and m:
                            low(t, m - 1, 0, m - 1)
                    if not general:
                        low(t, HT - 1, 0, HT - 1)
                    for layer in (1, 2):
                        for m in range(HT):
                            if not general:
                                low(t, layer * HT + m, layer % 2, m)
                            if layer == 1 and m < len(after_first):
                                after_first[m]()
                    if not general:
                        dve.wait_ge(lo_done, t * BLOCKS + BLOCKS)

                def tail(t, p, n):
                    def scale():
                        dve.wait_ge(o_ready, t + 1)
                        dve.wait_ge(out_stored[p], n * 16 + 16)
                        nc.vector.tensor_tensor(z[p][:, :, :], O[:, :, :], bcast_mid(srow[:, :], BATCH), ALU.mult).then_inc(o_free, 1)

                    def residual():
                        dve.wait_ge(o_free, t + 2)
                        nc.vector.tensor_tensor(z[p][:, :, :], z[p][:, :, :], x1[p][:, :, :], ALU.add).then_inc(z_done, 1)

                    def spread():
                        dve.wait_ge(z_done, t + 1)
                        for b in range(BATCH):
                            last = nc.vector.bn_stats(stats[:, b, :], z[p][:, b, :])
                        last.then_inc(st_done, 1)

                    def spread_sum():
                        dve.wait_ge(par_in, 32)
                        dve.wait_ge(st_done, t + 1)
                        for b in range(BATCH):
                            last = nc.vector.bn_aggr(mv[:, b, :], stats[:, b, :])
                        last.then_inc(var_done, 1)

                    def layer_norm():
                        dve.wait_ge(rstd_done, t + 1)
                        for b in range(BATCH):
                            last = nc.vector.tensor_scalar(z[p][:, b, :], z[p][:, b, :], mv[:, b, 0:1], rstd[:, b:b + 1],
                                                           ALU.subtract, ALU.mult)
                        last.then_inc(out_done, 1)

                    return [scale, residual, spread, spread_sum, layer_norm]

                def emit(general):
                    if not general:
                        split(0)
                    layers(0, general, [])
                    if not general:
                        split(1)
                    with dve.Fori(0, STEPS // 2 - 1) as i:
                        for p in range(2):
                            t = i * 2 + p + 1
                            layers(t, general, tail(t - 1, p, i))
                            if not general:
                                split(t + 1)
                    layers(STEPS - 1, general, tail(STEPS - 2, 0, STEPS // 2 - 1))
                    for piece in tail(STEPS - 1, 1, STEPS // 2 - 1):
                        piece()

                either(dve, emit)

            @block.gpsimd
            def _(pool):
                nc.gpsimd.memset(ln_eps[:, :], LN_EPS)
                nc.gpsimd.memset(power[:, :], -0.5).then_inc(power_set, 1)
                pool.wait_ge(power_set, 1)

                def tail(t):
                    pool.wait_ge(var_done, t + 1)
                    nc.gpsimd.tensor_tensor(rstd[:, :], mv[:, :, 1:2].rearrange("p b o -> p (b o)"), ln_eps[:, :],
                                            ALU.add).then_inc(rs_link, 1)
                    pool.wait_ge(rs_link, t + 1)
                    nc.gpsimd.tensor_tensor(rstd[:, :], rstd[:, :], power[:, :], ALU.pow).then_inc(rstd_done, 1)

                def emit(general):
                    with pool.Fori(0, STEPS) as t:
                        tail(t)

                either(pool, emit)


def build(nc, io):
    sems = ExitStack()
    with sems:
        whole = Stage(nc, sems)
        with whole.ctx:
            keep = {
                "const": whole.sb("const", [P, C_END]),
                "pw": whole.sb("pw", [P, HEADS, 5, STEPS * BATCH]),
                "scales": whole.sb("scales", [P, 2, STEPS, NS]),
            }
            early = Stage(nc, sems)
            with early.ctx:
                keep["raw"] = early.sb("raw", [P, STEPS * BATCH, NRAW])
                keep["prm"] = early.sb("prm", [P, NGATE + 2 * HEADS])
                keep["kk"] = early.sb("kk", [P, STEPS, 2, BH])
                keep["tri"] = early.sb("tri", [P, SLOTS, CH, CH])
                keep["tri_in"] = early.sem("tri_in")
                project(nc, sems, io, keep)
                weights_fir(nc, sems, io, keep)
            delta(nc, sems, io, keep)
            ffn(nc, sems, io, keep)


def host_layout(np, a):
    g = {k.replace("L0_attn_", "").replace("L0_ffn_", ""): np.asarray(v, dtype=np.float32) for k, v in a.items()}
    x = g["hidden_states"]
    cols = np.pad(x.transpose(0, 2, 1), ((0, 0), (0, 0), (HALO, 0)))
    xt = np.stack([cols[:, :, t * P:t * P + XW] for t in range(STEPS)])
    xt = xt.reshape(STEPS, BATCH, KT, P, XW).transpose(0, 3, 2, 1, 4)

    def kmajor(w):
        return w.T.reshape(w.shape[1] // P, P, w.shape[0]).transpose(1, 0, 2)

    def columns(w):
        return w.reshape(-1, P).T

    w_qkv = np.concatenate([kmajor(g[n]) for n in ("Wq", "Wk", "Wv")], axis=2)
    w_gate = np.concatenate([kmajor(g["gate_w"].reshape(NGATE, D)), kmajor(g["Wb"])], axis=2)
    taps = np.concatenate([g[n].reshape(KT, P, CONV) for n in ("conv_q", "conv_k", "conv_v")]).transpose(1, 0, 2)
    firp = np.zeros((D, NF, FIRPAD), np.float32)
    for f, (n, k) in enumerate(zip(("fir_s", "fir_m", "fir_l"), FIRS)):
        firp[:, f, 2 * WIN - k:2 * WIN] = g[n].reshape(D, k)
    prm = np.concatenate([g["gate_b"].reshape(-1), g["log_temp"].reshape(-1), g["eps_param"].reshape(-1)])[None]
    ffn_w = np.concatenate([kmajor(g[n]).reshape(P, -1) for n in ("w1_w", "w2_w", "h1_w", "h2_w", "w3_w")], axis=1)
    scol = np.concatenate([columns(g[n]) for n in ("w1_s", "w2_s", "h1_s", "h2_s")], axis=1)
    i, j = np.arange(P)[:, None], np.arange(P)[None, :]
    const = np.zeros((P, C_END), np.float32)
    const[:, C_ID:C_ID + P] = i == j
    const[:, C_OFF:C_OFF + P] = j // CH > i // CH
    const[:, C_ATT:C_ATT + P] = j >= i
    const[:, C_ONE:C_ONE + CH] = np.arange(CH)[None, :] == i % CH
    const[:, C_SEL:C_SEL + 2] = i // DK == np.arange(2)[None, :]
    return {"x": x, "xt": xt, "w_qkv": w_qkv, "w_gate": w_gate, "taps": taps, "firp": firp, "prm": prm, "ffn_w": ffn_w,
            "scol": scol, "srow": g["w3_s"][None], "const": const, "w_o": kmajor(g["Wo"]),
            "norm_w": np.concatenate([g["norm_w"]] * 2)[:, None]}


SCRATCH = {
    "qk_s": (STEPS, P, 2 * KT, TOK),
    "k_s": (STEPS, P, BATCH, D),
    "v_s": (HEADS, P, STEPS + 1, BATCH, DK),
    "kk_s": (P, GRP, P),
    "a_s": (P, GRP, CH),
    "d_s": (GRP, NQ, CH, CH),
    "t_s": (GRP, NQ, CH, CH),
    "mix_s": (2, STEPS, BATCH, 2 * HEADS, WIN, DK // 2),
    "x1_s": (STEPS, P, BATCH, D),
    "flag_s": (1, 1),
}


def kernel(**inputs):
    import numpy as np
    import concourse.bacc as bacc
    from concourse.bass_utils import run_bass_kernel_spmd

    nc = bacc.Bacc("TRN2", target_bir_lowering=False, num_devices=1)
    arrays = {f"in_{k}": np.ascontiguousarray(v) for k, v in host_layout(np, inputs).items()}
    io = {k[3:]: nc.dram_tensor(k, v.shape, f32, kind="ExternalInput").ap() for k, v in arrays.items()}
    for k, shape in SCRATCH.items():
        io[k] = nc.dram_tensor(k, shape, f32).ap()
    io["out"] = nc.dram_tensor("out", (BATCH, SEQ, D), f32, kind="ExternalOutput").ap()
    build(nc, io)
    r = run_bass_kernel_spmd(nc, [arrays], core_ids=[0])
    return r.results[0]["out"]
```
